# Optimizing a Trainium2 kernel written in Bass

```python
import numpy as np
import jax
import jax.numpy as jnp

def _softmax(x, axis=-1):
    return jax.nn.softmax(x, axis=axis)

def _gelu(x):
    return jax.nn.gelu(x, approximate=True)

def _silu(x):
    return jax.nn.silu(x)

def _sigmoid(x):
    return jax.nn.sigmoid(x)

def _layernorm(x, axis=-1, eps=1e-05):
    m = jnp.mean(x, axis=axis, keepdims=True)
    v = jnp.var(x, axis=axis, keepdims=True)
    return (x - m) / jnp.sqrt(v + eps)

def _scatter_add(tgt, idx, src, axis=0):
    return tgt.at[idx].add(src)

def _segment_sum(src, seg, n):
    return jax.ops.segment_sum(src, seg, n)
kernel_name = 'mk_gnn_resnorm_d4_gnn_r8_f2c5f4'

def setup_inputs(seed: int=0):
    np.random.seed(seed)
    _w = jnp.asarray

    def _rec_inputs():
        import jax
        import jax.numpy as jnp
        _gk = jax.random.key(seed)
        x = -0.000202 + 1 * jax.random.normal(jax.random.fold_in(_gk, 1), (12500, 64), jnp.float32)
        src = jax.random.randint(jax.random.fold_in(_gk, 2), (200000,), 0, 12500, jnp.int32)
        dst = jax.random.randint(jax.random.fold_in(_gk, 3), (200000,), 0, 12500, jnp.int32)
        _o = jnp.argsort(dst, stable=True)
        src = src[_o]
        dst = dst[_o]
        edge_attr_64 = -5.16925e-05 + 1.00005 * jax.random.normal(jax.random.fold_in(_gk, 11), (200000, 64), jnp.float32)
        edge_type_8 = jax.random.randint(jax.random.fold_in(_gk, 13), (200000,), 0, 8, jnp.int32)
        edge_weight = jax.random.uniform(jax.random.fold_in(_gk, 14), (200000,), jnp.float32, 0.0, 0.999999)
        return (x, src, dst, edge_attr_64, edge_type_8, edge_weight)
    x, src, dst, edge_attr_64, edge_type_8, edge_weight = _rec_inputs()

    def _L0_gnn_setup():
        import jax, jax.numpy as jnp
        import numpy as np
        N = 12500
        E = 200000
        D_IN = 64
        D_OUT = 64
        key = jax.random.key(seed)
        k1, k2, k3, k4, k5 = jax.random.split(key, 5)
        x = jax.random.normal(k1, (N, D_IN), dtype=jnp.float32)
        edge_index = jax.random.randint(k2, (2, E), 0, N, dtype=jnp.int32)
        edge_weight = jax.random.uniform(k3, (E,), dtype=jnp.float32)
        gain = float(np.sqrt(2.0))
        limit = gain * float(np.sqrt(6.0 / (D_IN + D_OUT)))
        W_self = jax.random.uniform(k4, (D_OUT, D_IN), minval=-limit, maxval=limit, dtype=jnp.float32)
        W_neigh = jax.random.uniform(k5, (D_OUT, D_IN), minval=-limit, maxval=limit, dtype=jnp.float32)
        bias = jnp.zeros((D_OUT,), dtype=jnp.float32)
        return {'x': x, 'edge_index': edge_index, 'edge_weight': edge_weight, 'W_self': W_self, 'W_neigh': W_neigh, 'bias': bias}
    _L0_gnn_all = _L0_gnn_setup()
    _L0_gnn_in = {k: v for k, v in _L0_gnn_all.items() if k in ('W_self', 'W_neigh', 'bias')}
    del _L0_gnn_all

    def _L1_gnn_setup():
        import jax, jax.numpy as jnp
        import numpy as np
        N_NODES = 12500
        N_EDGES = 200000
        D = 64
        key = jax.random.key(seed)
        ks = jax.random.split(key, 7)
        x = jax.random.normal(ks[0], (N_NODES, D), dtype=jnp.float32)
        edge_index = jax.random.randint(ks[1], (2, N_EDGES), 0, N_NODES, dtype=jnp.int64)
        edge_attr = jax.random.normal(ks[2], (N_EDGES, D), dtype=jnp.float32)
        s = 1.0 / np.sqrt(D)
        W1 = jax.random.normal(ks[3], (D, D), dtype=jnp.float32) * s
        b1 = jnp.zeros((D,), dtype=jnp.float32)
        W2 = jax.random.normal(ks[4], (D, D), dtype=jnp.float32) * s
        b2 = jnp.zeros((D,), dtype=jnp.float32)
        return {'x': x, 'edge_index': edge_index, 'edge_attr': edge_attr, 'W1': W1, 'b1': b1, 'W2': W2, 'b2': b2}
    _L1_gnn_all = _L1_gnn_setup()
    _L1_gnn_in = {k: v for k, v in _L1_gnn_all.items() if k in ('W1', 'b1', 'W2', 'b2')}
    del _L1_gnn_all

    def _L2_gnn_setup():
        import jax, jax.numpy as jnp
        import numpy as np
        N_NODES = 12500
        N_EDGES = 200000
        IN_F = 64
        OUT_F = 64
        BN_EPS = 1e-05
        LRELU_SLOPE = 0.01
        key = jax.random.key(seed)
        k1, k2, k3, k4 = jax.random.split(key, 4)
        node_features = jax.random.normal(k1, (N_NODES, IN_F), dtype=jnp.float32)
        edge_index = jax.random.randint(k2, (2, N_EDGES), 0, N_NODES, dtype=jnp.int64)
        W = jax.random.normal(k3, (OUT_F, 2 * IN_F), dtype=jnp.float32) * 0.08
        b = jax.random.normal(k4, (OUT_F,), dtype=jnp.float32) * 0.01
        gamma = jnp.ones((OUT_F,), dtype=jnp.float32)
        beta = jnp.zeros((OUT_F,), dtype=jnp.float32)
        return {'node_features': node_features, 'edge_index': edge_index, 'W': W, 'b': b, 'gamma': gamma, 'beta': beta}
    _L2_gnn_all = _L2_gnn_setup()
    _L2_gnn_in = {k: v for k, v in _L2_gnn_all.items() if k in ('W', 'b', 'gamma', 'beta')}
    del _L2_gnn_all

    def _L3_gnn_setup():
        import jax, jax.numpy as jnp
        import numpy as np
        NEG_SLOPE = 0.2

        def _gat_relation(x, src, dst, mask, N, Wr, a_src, a_dst, br):
            h = x @ Wr
            s = h @ a_src
            d = h @ a_dst
            e = jax.nn.leaky_relu(s[src] + d[dst], negative_slope=NEG_SLOPE)
            e = jnp.where(mask, e, -jnp.inf)
            m = jax.ops.segment_max(e, dst, num_segments=N)
            w = jnp.where(mask, jnp.exp(e - m[dst]), 0.0)
            denom = jax.ops.segment_sum(w, dst, num_segments=N)
            alpha = w / denom[dst]
            msg = alpha[:, None] * h[src]
            return jax.ops.segment_sum(msg, dst, num_segments=N) + br
        key = jax.random.key(seed)
        ks = jax.random.split(key, 9)
        N, E, D, F, R = (12500, 200000, 64, 64, 8)
        x = jax.random.normal(ks[0], (N, D), dtype=jnp.float32)
        edge_index = jax.random.randint(ks[1], (2, E), 0, N, dtype=jnp.int32)
        edge_type = jax.random.randint(ks[2], (E,), 0, R, dtype=jnp.int32)
        W_self = jax.random.normal(ks[3], (D, F), dtype=jnp.float32) * 0.1
        b_self = jax.random.normal(ks[4], (F,), dtype=jnp.float32) * 0.1
        W = jax.random.normal(ks[5], (R, D, F), dtype=jnp.float32) * 0.1
        att_src = jax.random.normal(ks[6], (R, F), dtype=jnp.float32) * 0.1
        att_dst = jax.random.normal(ks[7], (R, F), dtype=jnp.float32) * 0.1
        bias = jax.random.normal(ks[8], (R, F), dtype=jnp.float32) * 0.1
        return {'x': x, 'edge_index': edge_index, 'edge_type': edge_type, 'W_self': W_self, 'b_self': b_self, 'W': W, 'att_src': att_src, 'att_dst': att_dst, 'bias': bias}
    _L3_gnn_all = _L3_gnn_setup()
    _L3_gnn_in = {k: v for k, v in _L3_gnn_all.items() if k in ('W_self', 'b_self', 'W', 'att_src', 'att_dst', 'bias')}
    del _L3_gnn_all
    return {'x': x, 'src': src, 'dst': dst, 'edge_attr_64': edge_attr_64, 'edge_type_8': edge_type_8, 'edge_weight': edge_weight, 'L0_gnn_W_self': _L0_gnn_in['W_self'], 'L0_gnn_W_neigh': _L0_gnn_in['W_neigh'], 'L0_gnn_bias': _L0_gnn_in['bias'], 'L1_gnn_W1': _L1_gnn_in['W1'], 'L1_gnn_b1': _L1_gnn_in['b1'], 'L1_gnn_W2': _L1_gnn_in['W2'], 'L1_gnn_b2': _L1_gnn_in['b2'], 'L2_gnn_W': _L2_gnn_in['W'], 'L2_gnn_b': _L2_gnn_in['b'], 'L2_gnn_gamma': _L2_gnn_in['gamma'], 'L2_gnn_beta': _L2_gnn_in['beta'], 'L3_gnn_W_self': _L3_gnn_in['W_self'], 'L3_gnn_b_self': _L3_gnn_in['b_self'], 'L3_gnn_W': _L3_gnn_in['W'], 'L3_gnn_att_src': _L3_gnn_in['att_src'], 'L3_gnn_att_dst': _L3_gnn_in['att_dst'], 'L3_gnn_bias': _L3_gnn_in['bias']}

def reference(x, src, dst, edge_attr_64, edge_type_8, edge_weight, L0_gnn_W_self, L0_gnn_W_neigh, L0_gnn_bias, L1_gnn_W1, L1_gnn_b1, L1_gnn_W2, L1_gnn_b2, L2_gnn_W, L2_gnn_b, L2_gnn_gamma, L2_gnn_beta, L3_gnn_W_self, L3_gnn_b_self, L3_gnn_W, L3_gnn_att_src, L3_gnn_att_dst, L3_gnn_bias):
    import jax
    import jax.numpy as jnp

    def _L0_gnn_ref(x, edge_index, edge_weight, W_self, W_neigh, bias):
        import jax, jax.numpy as jnp
        import numpy as np
        N = 12500
        E = 200000
        D_IN = 64
        D_OUT = 64
        src, dst = (edge_index[0], edge_index[1])
        n = x.shape[0]
        msg = x[src] * edge_weight[:, None]
        agg = jax.ops.segment_sum(msg, dst, num_segments=n)
        w_sum = jax.ops.segment_sum(edge_weight, dst, num_segments=n)
        w_sum = jnp.maximum(w_sum, 1e-08)
        neigh = agg / w_sum[:, None]
        out = x @ W_self.T + neigh @ W_neigh.T + bias
        norm = jnp.linalg.norm(out, axis=-1, keepdims=True)
        return out / jnp.maximum(norm, 1e-12)

    def _L1_gnn_ref(x, edge_index, edge_attr, W1, b1, W2, b2):
        import jax, jax.numpy as jnp
        import numpy as np
        N_NODES = 12500
        N_EDGES = 200000
        D = 64
        src = edge_index[0]
        dst = edge_index[1]
        msg = jax.nn.relu(x[src] + edge_attr)
        agg = jax.ops.segment_sum(msg, dst, num_segments=x.shape[0])
        h = x + agg
        h = jax.nn.relu(h @ W1 + b1)
        return h @ W2 + b2

    def _L2_gnn_ref(node_features, edge_index, W, b, gamma, beta):
        import jax, jax.numpy as jnp
        import numpy as np
        N_NODES = 12500
        N_EDGES = 200000
        IN_F = 64
        OUT_F = 64
        BN_EPS = 1e-05
        LRELU_SLOPE = 0.01
        src, dst = (edge_index[0], edge_index[1])
        x_i = node_features[dst]
        x_j = node_features[src]
        msg_in = jnp.concatenate([x_i, x_j - x_i], axis=-1)
        msg = msg_in @ W.T + b
        h = jax.ops.segment_sum(msg, dst, num_segments=node_features.shape[0])
        mean = jnp.mean(h, axis=0)
        var = jnp.mean(jnp.square(h - mean), axis=0)
        h_bn = gamma * (h - mean) * jax.lax.rsqrt(var + BN_EPS) + beta
        return jnp.where(h_bn >= 0, h_bn, LRELU_SLOPE * h_bn)

    def _L3_gnn_ref(x, edge_index, edge_type, W_self, b_self, W, att_src, att_dst, bias):
        import jax, jax.numpy as jnp
        import numpy as np
        NEG_SLOPE = 0.2

        def _gat_relation(x, src, dst, mask, N, Wr, a_src, a_dst, br):
            h = x @ Wr
            s = h @ a_src
            d = h @ a_dst
            e = jax.nn.leaky_relu(s[src] + d[dst], negative_slope=NEG_SLOPE)
            e = jnp.where(mask, e, -jnp.inf)
            m = jax.ops.segment_max(e, dst, num_segments=N)
            w = jnp.where(mask, jnp.exp(e - m[dst]), 0.0)
            denom = jax.ops.segment_sum(w, dst, num_segments=N)
            alpha = w / denom[dst]
            msg = alpha[:, None] * h[src]
            return jax.ops.segment_sum(msg, dst, num_segments=N) + br
        N = x.shape[0]
        R = W.shape[0]
        loops = jnp.arange(N, dtype=edge_index.dtype)
        src = jnp.concatenate([edge_index[0], loops])
        dst = jnp.concatenate([edge_index[1], loops])
        ones_loops = jnp.ones((N,), dtype=bool)
        out = x @ W_self + b_self
        for r in range(R):
            mask = jnp.concatenate([edge_type == r, ones_loops])
            out = out + _gat_relation(x, src, dst, mask, N, W[r], att_src[r], att_dst[r], bias[r])
        return out
    edge_index = jnp.stack([src, dst])
    x = _layernorm(x + _L0_gnn_ref(x, edge_index, edge_weight, L0_gnn_W_self, L0_gnn_W_neigh, L0_gnn_bias), axis=-1)
    x = _layernorm(x + _L1_gnn_ref(x, edge_index, edge_attr_64, L1_gnn_W1, L1_gnn_b1, L1_gnn_W2, L1_gnn_b2), axis=-1)
    x = _layernorm(x + _L2_gnn_ref(x, edge_index, L2_gnn_W, L2_gnn_b, L2_gnn_gamma, L2_gnn_beta), axis=-1)
    x = _layernorm(x + _L3_gnn_ref(x, edge_index, edge_type_8, L3_gnn_W_self, L3_gnn_b_self, L3_gnn_W, L3_gnn_att_src, L3_gnn_att_dst, L3_gnn_bias), axis=-1)
    return x

_drawn_inputs = setup_inputs


def setup_inputs(seed=0):
    import zlib

    import numpy as np

    out = dict(_drawn_inputs(seed))
    spreads = {'L0_gnn_bias': (0.0, 0.691),
     'L1_gnn_b1': (0.0, 0.514),
     'L1_gnn_b2': (0.0, 0.379),
     'L2_gnn_gamma': (1.0, 0.2),
     'L2_gnn_beta': (0.0, 0.1)}
    factors = {'edge_weight': 31.324, 'L2_gnn_b': 8.0, 'L0_gnn_W_neigh': 3.001}
    for name, (base, spread) in spreads.items():
        noise = np.random.default_rng([zlib.crc32(name.encode()), seed]).standard_normal(out[name].shape)
        drawn = base * np.exp(spread * noise) if base else spread * noise
        out[name] = jnp.asarray(drawn.astype(out[name].dtype))
    for name, factor in factors.items():
        out[name] = (out[name] * factor).astype(out[name].dtype)
    return out
```

```python
import concourse.bass as bass
from concourse import mybir
from contextlib import ExitStack

N, E, D, R = 12500, 200000, 64, 8
P, S = 125, 8
GE = P * S
G = E // GE
Q = 4
IT = G // Q
W = 128
NW = -(-N // W)
NP = NW * W
FW = 32
BT = 7
NB = NW // BT
BC = BT * W
HB = BC // 2
TAIL = N - (NB - 1) * BC
TAIL_TILES, TAIL_ROWS = TAIL // W, TAIL % W
HROW = 72
T = E // P
SG = 100
BIG = 1e37
EPS_LN = 1e-5

WEIGHTS = [("ws65", (65, 64)), ("wn", (64, 64)), ("w1", (64, 64)), ("b1", (64, 1)), ("w2b", (65, 64)),
           ("wi", (64, 64)), ("wj", (64, 64)), ("b2", (1, 64)), ("gamma", (64, 1)), ("beta", (64, 1)),
           ("wself", (64, 64)), ("bself", (1, 64)), ("wcat", (64, 512)), ("wrt", (64, 512)),
           ("att", (64, 16)), ("rbias", (1, 512))]


def program(nc, x, src_p, dst_p, type_p, weight_p, dst_f, type_f, edge_attr, weights, out, upto):
    f32, i32, i16 = mybir.dt.float32, mybir.dt.int32, mybir.dt.int16
    ALU, ACT, AX = mybir.AluOpType, mybir.ActivationFunctionType, mybir.AxisListType
    dram = lambda n, s, d=f32: nc.dram_tensor(n, s, d, kind="Internal").ap()
    x1_d, x2_d, x3_d = dram("x1_d", (NP, D)), dram("x2_d", (NP, D)), dram("x3_d", (NP, D))
    rel_d = dram("rel_d", (NP * R, HROW))
    he_d = dram("he_d", (G, P, S * HROW))
    key_d = dram("key_d", (P, G, S), i32)
    dst16_d = dram("dst16_d", (E,), i16)
    trip_d = dram("trip_d", (E * 3,))
    alpha_d = dram("alpha_d", (E,))
    run_out_d, run_in_d = dram("run_out_d", (2, P, 2 * R + 2)), dram("run_in_d", (2, P, 2 * R))

    with ExitStack() as ctx:
        sb = lambda n, s, d=f32: ctx.enter_context(nc.sbuf_tensor(n, s, d))
        ps = lambda n, s: ctx.enter_context(nc.psum_tensor(n, s, f32))
        sem = lambda n: ctx.enter_context(nc.semaphore(n))

        ident, iota = sb("ident", [128, 128]), sb("iota", [128, W])
        fine_col, node_col = sb("fine_col", [128, NP // FW]), sb("node_col", [128, NW])
        rel_col = sb("rel_col", [128, R])
        wt = {n: sb("w_" + n, list(s)) for n, s in WEIGHTS}
        wn66, wj66 = sb("wn66", [D + 2, D + 2]), sb("wj66", [D + 2, D])
        wd65, wself65 = sb("wd65", [65, D]), sb("wself65", [65, D])
        sdw, brow = sb("sdw", [D, 2 * R]), sb("brow", [1, D])
        eps_col = sb("eps_col", [128, 1])
        idx = sb("idx", [P, Q, S], i32)
        gat = sb("gat", [P, Q, S, HROW])
        ea = sb("ea", [P, Q, S, D])
        msg = sb("msg", [P, 2, S, HROW])
        oh = sb("oh", [P, 2, S, W])
        dstf, edge_w, typef = sb("dstf", [P, G, S]), sb("edge_w", [P, G, S]), sb("typef", [P, G, S])
        trip, trip_s = sb("trip", [P, G, S, 3]), sb("trip_s", [P, T, 3])
        drow, oht = sb("drow", [128, 2, GE], i16), sb("oht", [128, GE])
        toh, sel, sel2 = sb("toh", [P, S, R]), sb("sel", [P, S, 2, R]), sb("sel2", [P, S, 2])
        ends, runs, run_in = sb("ends", [P, 2]), sb("runs", [P, 2 * R + 2]), sb("run_in", [P, 2 * R])
        sum_t = sb("sum_t", [128, NP + W - FW])
        deg = sb("deg", [128, NW])
        dtab = sb("dtab", [128, NW, 2 * R])
        win = sb("win", [1, 2, G], i32)
        link_row = sb("link_row", [1, 4, P + 1])
        ends_g, ends_i = sb("ends_g", [SG, 2, 2]), sb("ends_i", [SG, 4, 2], i32)
        wcols, wrows, wones = sb("wcols", [SG, 4, 2]), sb("wrows", [1, 6, G]), sb("wones", [1, G])
        wint = sb("wint", [1, 3, G], i32)
        xs, xd = sb("xs", [128, 2, BT, D]), sb("xd", [128, 2, BT, D + 1])
        stage, xt = sb("stage", [128, 2, BC]), sb("xt", [65, 2, BC])
        ya, yb, yo = sb("ya", [128, BT, D]), sb("yb", [128, BT, D]), sb("yo", [128, 2, BT, D])
        r1, r2 = sb("r1", [128, BT]), sb("r2", [128, BT])
        sd, self_w, hs = sb("sd", [128, BT, 2 * R]), sb("self_w", [128, BT, R]), sb("hs", [128, R, D])
        bn, bnm = sb("bn", [D, 25, 6]), sb("bnm", [D, 6])
        trip_flat = trip[:, :, :, :].rearrange("p g s c -> p (g s c)")
        scan_flat = trip_s[:, :, :].rearrange("p t c -> p (t c)")
        src_i, type_i, dst_i = [trip_flat.bitcast(i32)[:, k * T:(k + 1) * T] for k in range(3)]
        dstn_i = scan_flat.bitcast(i32)[:, 0:T]
        dst16 = scan_flat[:, 2 * T:2 * T + T // 2].bitcast(i16)
        stat_i = oh[0:SG, :, :, :].rearrange("p a s w -> p (a s w)")[:, 0:2 * GE].bitcast(i32)
        stat_i = stat_i.rearrange("p (a e) -> p a e", a=2)
        hst = sum_t[:, 0:2 * BT * R * HROW].rearrange("p (u t r c) -> p u t r c", u=2, t=BT, r=R)
        rtype, brk_f, brk_b, lead, trail, val, fwd = [sum_t[0:P, k * T:(k + 1) * T] for k in range(7)]
        bwd, best, off = [trip_flat[:, k * T:(k + 1) * T] for k in range(3)]
        scan_dst_i, scan_type_i = fwd.bitcast(i32), rtype.bitcast(i32)
        run_row = gat[0:1, :, :, :].rearrange("a q s c -> a (q s c)")[:, 0:P * (2 * R + 2)]\
            .rearrange("a (p c) -> a p c", p=P)
        carry_row = ea[0:1, :, :, :].rearrange("a q s d -> a (q s d)")[:, 0:P * 2 * R].rearrange("a (p c) -> a p c", p=P)
        init_row = oh[0:1, :, :, :].rearrange("a u s w -> a (u s w)")[:, 0:P * 2 * R].rearrange("a (p c) -> a p c", p=P)
        score, gap, self_score, self_gap = trip_s[:, :, 0], trip_s[:, :, 1], trip_s[:, :, 2], off
        oht_tile = oht[:, :].rearrange("n (p s) -> n p s", s=S)
        p_sum, p_tr = ps("p_sum", [128, 2, 512]), ps("p_tr", [128, 2, 512])
        p_a, p_b = ps("p_a", [128, 2, 512]), ps("p_b", [128, 2, 512])
        p_tr_flat = p_tr[:, :, :].rearrange("p a c -> p (a c)")

        s_load = [sem(f"s_load{k}") for k in range(6)]
        s_wload, s_const, s_vconst = sem("s_wload"), sem("s_const"), sem("s_vconst")
        s_cols, s_rows, s_win = sem("s_cols"), sem("s_rows"), sem("s_win")
        s_prep, s_patch, s_sdw = sem("s_prep"), sem("s_patch"), sem("s_sdw")
        s_key, s_keyst, s_zero = sem("s_key"), sem("s_keyst"), sem("s_zero")
        s_idx = [sem(f"s_idx{q}") for q in range(Q)]
        s_gat = [sem(f"s_gat{q}") for q in range(Q)]
        s_free = [sem(f"s_free{q}") for q in range(Q)]
        s_ea = [sem(f"s_ea{q}") for q in range(Q)]
        s_hest = [sem(f"s_hest{q}") for q in range(Q)]
        s_held = [sem(f"s_held{q}") for q in range(Q)]
        s_pre, s_msg = sem("s_pre"), sem("s_msg")
        s_oh = [[sem(f"s_oh{n}_{h}") for h in range(2)] for n in range(5)]
        s_agg = [sem(f"s_agg{n}") for n in range(5)]
        s_sum = [sem(f"s_sum{n}") for n in range(5)]
        s_acc, s_scan_copy = sem("s_acc"), sem("s_scan_copy")
        s_drow = [sem(f"s_drow{u}") for u in range(2)]
        s_drused, s_trip, s_tripd = sem("s_drused"), sem("s_trip"), sem("s_tripd")
        s_rld = [sem(f"s_rld{k}") for k in range(2)]
        s_scan, s_run, s_rund = sem("s_scan"), sem("s_run"), sem("s_rund")
        s_ein, s_eout, s_alpha, s_alphad, s_alphal = [sem(n) for n in
                                                      ("s_ein", "s_eout", "s_alpha", "s_alphad", "s_alphal")]
        NS = 6
        s_tail = sem("s_tail")
        s_xs = [sem(f"s_xs{u}") for u in range(2)]
        s_xfree = [sem(f"s_xfree{n}") for n in range(NS)]
        s_tr = {n: sem(f"s_tr{n}") for n in (0, 1, 2, 4, 5)}
        s_stage = {n: sem(f"s_stage{n}") for n in (0, 1, 2, 4, 5)}
        s_mid = {n: sem(f"s_mid{n}") for n in (1, 2, 3, 5)}
        s_act = {n: sem(f"s_act{n}") for n in (1, 2, 3, 4)}
        s_mm = [sem(f"s_mm{n}") for n in range(NS)]
        s_sqrt_in, s_sqrt = [{n: sem(f"s_{k}{n}") for n in (0, 1, 3, 5)} for k in ("sqrt_in", "sqrt")]
        s_y = {n: sem(f"s_y{n}") for n in (0, 1, 3, 4, 5)}
        s_yst = [sem(f"s_yst{u}") for u in range(2)]
        s_yfree = {n: sem(f"s_yfree{n}") for n in (0, 1, 3, 4, 5)}
        s_table = sem("s_table")
        s_bn, s_bnr, s_bnc = sem("s_bn"), sem("s_bnr"), sem("s_bnc")
        s_h = [[sem(f"s_h{n}_{k}") for k in range(2)] for n in range(2)]
        s_hc = [[sem(f"s_hc{n}_{k}") for k in range(2)] for n in range(2)]
        s_vch, s_ach = sem("s_vch"), sem("s_ach")
        s_turn = sem("s_turn")
        block = ctx.enter_context(nc.Block())

        class Chain:

            def __init__(self, eng, s):
                self.eng, self.s, self.n = eng, s, 0

            def start(self):
                self.eng.sem_clear(self.s)
                self.n = 0

            def add(self, ins):
                ins.then_inc(self.s, 1)
                self.n += 1

            def wait(self):
                self.eng.wait_ge(self.s, self.n)

            def __call__(self, ins):
                self.add(ins)
                self.wait()

        def wait_reg(eng, s, v):
            eng.wait_ge(s, v)
            eng.sem_inc(s_turn, 1)

        def group_windows(eng, table, g):
            v = eng.value_load(win[0:1, table, bass.ds(g, 1)], min_val=0, max_val=(NW * G << 16) - 1)
            return eng.snap((v >> 7) & 511), eng.snap((v & 127) + 1), eng.snap(v >> 16)

        def within(v, most):
            return nc.s_assert_within(v, 0, most, skip_runtime_bounds_check_because=(
                "a group's last window holds its largest dst, which is below N"))

        def rows(table, b):
            return table[bass.ds(b * BC, BC), :].rearrange("(t p) d -> p t d", p=W)

        def of_group(buf, g):
            return buf[:, bass.ds(g, 1), :].rearrange("p a s -> p (a s)")

        def nodes(b, width=BC, at=0):
            return bass.ds(b * BC + at, width)

        X = [x, x1_d, x2_d, x2_d, x3_d, x3_d]
        Y = {0: x1_d, 1: x2_d, 3: x3_d, 5: out}
        NI = NB // 2
        stored = {0: 0, 1: 1, 3: 2, 4: 3, 5: 4}

        @block.sync
        def _(sp):
            flat = "p g s -> p (g s)"
            sp.dma_start(stat_i, dst_f.rearrange("(a g e) -> g a e", a=2, g=SG)).then_inc(s_load[0], 16)
            sp.dma_start(dst_i, dst_p.rearrange(flat)).then_inc(s_load[1], 16)
            sp.dma_start(edge_w[:, :, :].rearrange(flat), weight_p.rearrange(flat)).then_inc(s_load[2], 16)
            for q in range(Q):
                sp.dma_start(idx[:, q, :], src_p[:, q, :]).then_inc(s_idx[q], 16)
            sp.dma_start(src_i, src_p.rearrange(flat)).then_inc(s_load[3], 16)
            sp.dma_start(type_i, type_p.rearrange(flat)).then_inc(s_load[4], 16)
            sp.dma_start(dstn_i, dst_f.rearrange("(p t) -> p t", p=P)).then_inc(s_load[5], 16)
            for name, _ in WEIGHTS:
                sp.dma_start(wt[name][:, :], weights[name]).then_inc(s_wload, 16)
            sp.wait_ge(s_prep, 1)
            sp.dma_start(wn66[0:D, 0:D], weights["wn"]).then_inc(s_patch, 16)
            sp.dma_start(wself65[D:D + 1, :], brow[0:1, :]).then_inc(s_patch, 16)
            sp.dma_start(wself65[0:D, :], weights["wself"]).then_inc(s_patch, 16)
            sp.dma_start(wd65[D:D + 1, :], weights["b2"]).then_inc(s_patch, 16)
            sp.wait_ge(s_key, 1)
            sp.dma_start(key_d.rearrange(flat), src_i).then_inc(s_keyst, 16)
            sp.dma_start(dst16_d.rearrange("(p t) -> p t", p=P), dst16).then_inc(s_keyst, 16)

            def refill(n, q, it, source):
                wait_reg(sp, s_free[q], it + (2 + IT * n))
                sp.dma_start(idx[:, q, :], source[:, bass.ds(it * Q + (Q + q), 1), :]
                             .rearrange("p a s -> p (a s)")).then_inc(s_idx[q], 16)

            def first_indices(n, source):
                for q in range(Q):
                    sp.wait_ge(s_free[q], IT * n + 1)
                    sp.dma_start(idx[:, q, :], source[:, q, :]).then_inc(s_idx[q], 16)

            def dense_io(n):
                r0 = (NB - 1) * BC

                def load(u, b):
                    sp.dma_start(xs[:, u, :, :], rows(X[n], b)).then_inc(s_xs[u], 16)

                def load_last():
                    if X[n] is not x:
                        return load(1, NB - 1)
                    sp.dma_start(xs[0:TAIL_ROWS, 1, TAIL_TILES, :], x[r0 + TAIL_TILES * W:N, :])\
                        .then_inc(s_tail, 16)
                    sp.wait_ge(s_tail, 16)
                    sp.dma_start(xs[:, 1, 0:TAIL_TILES, :], x[r0:r0 + TAIL_TILES * W, :]
                                 .rearrange("(t p) d -> p t d", p=W)).then_inc(s_xs[1], 16)

                def store(u, it, b):
                    if n in Y:
                        sp.dma_start(rows(Y[n], b), yo[:, u, :, :]).then_inc(s_yst[u], 16)
                    elif n == 4:
                        sp.dma_start(rel_d[bass.ds(b * BC * R, BC * R), :]
                                     .rearrange("(t p r) c -> p t (r c)", p=W, r=R),
                                     hst[:, u, :, :, :].rearrange("p t r c -> p t (r c)")).then_inc(s_yst[u], 16)

                def store_last():
                    if Y.get(n) is not out:
                        return store(1, NI - 1, NB - 1)
                    sp.dma_start(out[r0:r0 + TAIL_TILES * W, :].rearrange("(t p) d -> p t d", p=W),
                                 yo[:, 1, 0:TAIL_TILES, :]).then_inc(s_yst[1], 16)
                    sp.dma_start(out[r0 + TAIL_TILES * W:N, :], yo[0:TAIL_ROWS, 1, TAIL_TILES, :])\
                        .then_inc(s_tail, 16)

                def turn(it, final):
                    for u in range(2):
                        b = it * 2 + u
                        if n != 2:
                            wait_reg(sp, s_y[n], b + 1)
                            if n == 4:
                                wait_reg(sp, s_act[n], b + 1)
                            store(u, it, b)
                        wait_reg(sp, s_xfree[n], b + 3)
                        if final and u == 1:
                            load_last()
                        else:
                            load(u, b + 2)
                        if n != 2:
                            wait_reg(sp, s_yst[u], it * 16 + 16 * (1 + NI * stored[n]))
                            sp.sem_inc(s_yfree[n], 1)

                if n:
                    sp.wait_ge(s_xfree[n - 1], NB + 2)
                for u in range(2):
                    load(u, u)
                with sp.Fori(0, NI - 2) as it:
                    turn(it, False)
                turn(NI - 2, True)
                if n == 2:
                    return
                for b in (NB - 2, NB - 1):
                    sp.wait_ge(s_y[n], b + 1)
                    if n == 4:
                        sp.wait_ge(s_act[n], b + 1)
                    if b == NB - 2:
                        store(0, NI - 1, b)
                    else:
                        store_last()
                for u in range(2):
                    sp.wait_ge(s_yst[u], 16 * NI * (1 + stored[n]))
                if n == 5:
                    sp.wait_ge(s_tail, 32)
                sp.sem_inc(s_table, 1)

            with sp.Fori(0, IT - 1) as it:
                for q in range(Q):
                    refill(0, q, it, src_p)
            sp.wait_ge(s_keyst, 32)
            dense_io(0)
            if upto == 0:
                return
            first_indices(1, src_p)
            ea_d = edge_attr.rearrange("(g p s) d -> g p (s d)", p=P, s=S)
            ea_slot = [ea[:, q, :, :].rearrange("p s d -> p (s d)") for q in range(Q)]
            for q in range(Q):
                sp.dma_start(ea_slot[q], ea_d[q, :, :]).then_inc(s_ea[q], 16)
            with sp.Fori(0, IT - 1) as it:
                for q in range(Q):
                    refill(1, q, it, src_p)
                    sp.dma_start(ea_slot[q], ea_d[bass.ds(it * Q + (Q + q), 1), :, :]
                                 .rearrange("a p e -> (a p) e")).then_inc(s_ea[q], 16)
            dense_io(1)
            if upto == 1:
                return
            first_indices(2, src_p)
            with sp.Fori(0, IT - 1) as it:
                for q in range(Q):
                    refill(2, q, it, src_p)
            dense_io(2)
            dense_io(3)
            if upto == 2:
                return
            dense_io(4)
            first_indices(3, key_d)

            def dst_row(u, g):
                sp.dma_start(drow[:, u, :], dst16_d[bass.ds(g * GE, GE)].unsqueeze(0).to_broadcast([128, GE]))\
                    .then_inc(s_drow[u], 16)

            for u in range(2):
                dst_row(u, u)
            sp.dma_start(scan_dst_i, dst_f.rearrange("(p t) -> p t", p=P)).then_inc(s_rld[0], 16)
            sp.dma_start(scan_type_i, type_f.rearrange("(p t) -> p t", p=P)).then_inc(s_rld[1], 16)

            def pass3(it, final):
                for q in range(Q):
                    if not (final and q >= Q - 2):
                        wait_reg(sp, s_drused, it * Q + (q + 1))
                        dst_row(q % 2, it * Q + (q + 2))
                    if not final:
                        refill(3, q, it, key_d)

            with sp.Fori(0, IT - 1) as it:
                pass3(it, False)
            pass3(IT - 1, True)
            sp.wait_ge(s_trip, 2)
            sp.dma_start(trip_d.rearrange("(g p e) -> p g e", g=G, p=P),
                         trip[:, :, :, :].rearrange("p g s c -> p g (s c)")).then_inc(s_tripd, 16)
            sp.wait_ge(s_tripd, 16)
            sp.dma_start(scan_flat, trip_d.rearrange("(p e) -> p e", p=P)).then_inc(s_scan, 16)
            for k in range(2):
                sp.wait_ge(s_run, 2 * k + 1)
                sp.dma_start(run_out_d[k, :, :], runs[:, :]).then_inc(s_rund, 16)
                sp.wait_ge(s_rund, 64 * k + 16)
                sp.dma_start(run_row.rearrange("a p c -> a (p c)"),
                             run_out_d[k:k + 1, :, :].rearrange("a p c -> a (p c)")).then_inc(s_rund, 16)
                sp.wait_ge(s_run, 2 * k + 2)
                sp.dma_start(run_in_d[k:k + 1, :, :].rearrange("a p c -> a (p c)"),
                             init_row.rearrange("a p c -> a (p c)")).then_inc(s_rund, 16)
                sp.wait_ge(s_rund, 64 * k + 48)
                sp.dma_start(run_in[:, :], run_in_d[k, :, :]).then_inc(s_rund, 16)
            sp.wait_ge(s_alpha, 1)
            sp.dma_start(alpha_d.rearrange("(p t) -> p t", p=P), val).then_inc(s_alphad, 16)
            sp.wait_ge(s_alphad, 16)
            sp.dma_start(edge_w[:, :, :], alpha_d.rearrange("(g p s) -> p g s", g=G, p=P)).then_inc(s_alphal, 16)
            he_slot = [gat[:, q, :, :].rearrange("p s c -> p (s c)") for q in range(Q)]
            for q in range(Q):
                sp.dma_start(he_slot[q], he_d[q, :, :]).then_inc(s_held[q], 16)
            with sp.Fori(0, IT - 1) as it:
                for q in range(Q):
                    wait_reg(sp, s_free[q], it + (2 + 4 * IT))
                    sp.dma_start(he_slot[q], he_d[bass.ds(it * Q + (Q + q), 1), :, :]
                                 .rearrange("a p e -> (a p) e")).then_inc(s_held[q], 16)
            dense_io(5)

        @block.gpsimd
        def _(pool):
            nc.gpsimd.memset(ident[:, :], 0.0).then_inc(s_const, 1)
            pool.wait_ge(s_const, 1)
            exact = dict(allow_small_or_imprecise_dtypes=True)
            nc.gpsimd.affine_select(out=ident[:, :], in_=ident[:, :], compare_op=ALU.not_equal, fill=1.0, base=0,
                                    pattern=[[-1, 128]], channel_multiplier=1).then_inc(s_const, 1)
            nc.gpsimd.iota(iota[:, :], pattern=[[1, W]], base=0, channel_multiplier=0, **exact).then_inc(s_const, 1)
            nc.gpsimd.iota(fine_col[:, :], pattern=[[FW, NP // FW]], base=0, channel_multiplier=0, **exact)\
                .then_inc(s_const, 1)
            nc.gpsimd.iota(node_col[:, :], pattern=[[W, NW]], base=0, channel_multiplier=1, **exact)\
                .then_inc(s_const, 1)
            nc.gpsimd.iota(rel_col[:, :], pattern=[[1, R]], base=0, channel_multiplier=0, **exact).then_inc(s_const, 1)

            def gather_pass(n, table, width):
                with pool.Fori(0, IT) as it:
                    for q in range(Q):
                        wait_reg(pool, s_idx[q], it * 16 + 16 * (1 + IT * n))
                        wait_reg(pool, s_free[q], it + (1 + IT * n))
                        for s in range(S):
                            nc.gpsimd.indirect_dma_start(
                                out=gat[:, q, s, 0:width], out_offset=None, in_=table,
                                in_offset=bass.IndirectOffsetOnAxis(ap=idx[:, q, s:s + 1], axis=0),
                            ).then_inc(s_gat[q], 16)

            gather_pass(0, x, D)
            for n, table in ((1, x1_d), (2, x2_d)):
                if upto >= n:
                    pool.wait_ge(s_table, n)
                    gather_pass(n, table, D)
            if upto == 3:
                pool.wait_ge(s_table, 4)
                pool.wait_ge(s_keyst, 32)
                gather_pass(3, rel_d, HROW)

        @block.scalar
        def _(act):
            ch = Chain(act, s_ach)

            def square_root(n, b, k, per):
                wait_reg(act, s_sqrt_in[n], b * per + (k + 1))
                if k == per - 1:
                    nc.scalar.activation(r2[:, :], r2[:, :], ACT.Sqrt, bias=eps_col[:, 0:1], scale=1.0 / D)\
                        .then_inc(s_sqrt[n], 1)
                else:
                    nc.scalar.activation(r1[:, :], r1[:, :], ACT.Sqrt).then_inc(s_sqrt[n], 1)

            act.wait_ge(s_vconst, 2)
            act.wait_ge(s_sum[0], 1)
            with act.Fori(0, NI) as it:
                for u in range(2):
                    b = act.snap(it * 2 + u)
                    wait_reg(act, s_mm[0], b + 1)
                    nc.scalar.activation(stage[0:66, u, :], sum_t[0:66, nodes(b)], ACT.Copy)
                    wait_reg(act, s_tr[0], b + 1)
                    nc.scalar.activation(xt[0:D, u, :], p_tr_flat[0:D, 0:BC], ACT.Copy).then_inc(s_stage[0], 1)
                    square_root(0, b, 0, 2)
                    square_root(0, b, 1, 2)
            if upto == 0:
                return
            with act.Fori(0, IT) as it:
                for q in range(Q):
                    wait_reg(act, s_pre, it * Q + (q + 1))
                    nc.scalar.activation(msg[:, q % 2, :, 0:D], ea[:, q, :, :], ACT.Relu).then_inc(s_msg, 1)
                    wait_reg(act, s_msg, it * Q + (G + q + 1))
                    act.sem_inc(s_free[q], 1)
            with act.Fori(0, NI) as it:
                for u in range(2):
                    b = act.snap(it * 2 + u)
                    wait_reg(act, s_mid[1], b + 1)
                    for h, bank in ((0, p_a), (1, p_b)):
                        ins = nc.scalar.activation(xt[0:D, u, h * HB:(h + 1) * HB], bank[0:D, u, 0:HB], ACT.Relu,
                                                   bias=wt["b1"][:, 0:1])
                    ins.then_inc(s_act[1], 1)
                    square_root(1, b, 0, 1)
            if upto == 1:
                return
            with act.Fori(0, NI) as it:
                for u in range(2):
                    b = act.snap(it * 2 + u)
                    wait_reg(act, s_mm[2], b + 1)
                    wait_reg(act, s_tr[2], b + 3)
                    nc.scalar.activation(stage[0:D + 1, u, :], p_tr_flat[0:D + 1, 0:BC], ACT.Copy)\
                        .then_inc(s_stage[2], 1)
            act.wait_ge(s_bn, 1)
            nc.scalar.activation(bnm[:, 2:3], bnm[:, 1:2], ACT.Sqrt, bias=eps_col[0:D, 0:1]).then_inc(s_bnr, 1)
            act.wait_ge(s_bnc, 1)
            with act.Fori(0, NI) as it:
                for u in range(2):
                    b = act.snap(it * 2 + u)
                    wait_reg(act, s_mid[3], b + 1)
                    nc.scalar.activation(stage[0:D, u, :], sum_t[0:D, nodes(b)], ACT.Identity,
                                         bias=bnm[:, 4:5], scale=bnm[:, 3:4]).then_inc(s_act[3], 1)
                    square_root(3, b, 0, 1)
            if upto == 2:
                return
            act.wait_ge(s_zero, 1)
            with act.Fori(0, NI) as it:
                for u in range(2):
                    b = act.snap(it * 2 + u)
                    wait_reg(act, s_mm[4], b + 1)
                    wait_reg(act, s_tr[4], b + 1)
                    nc.scalar.activation(xt[0:D, u, :], p_tr_flat[0:D, 0:BC], ACT.Copy).then_inc(s_stage[4], 1)
                    wait_reg(act, s_yfree[4], b + 1)
                    for t in range(u, BT, 2):
                        m = (BT * u + t) // 2
                        wait_reg(act, s_h[0][0], it * BT + (m + 1))
                        nc.scalar.activation(hst[:, u, t, :, 0:D],
                                             p_a[:, 0, :].rearrange("p (r d) -> p r d", r=R), ACT.Copy)\
                            .then_inc(s_hc[0][0], 1)
                    wait_reg(act, s_hc[0][0], it * BT + (m + 2))
                    act.sem_inc(s_act[4], 1)
            act.wait_ge(s_zero, 2)

            def free_slot(q, it):
                wait_reg(act, s_scan_copy, it * Q + (q + 1))
                wait_reg(act, s_hest[q], it * 16 + 16)
                act.sem_inc(s_free[q], 1)

            with act.Fori(0, IT) as it:
                for q in range(Q):
                    wait_reg(act, s_gat[q], it * 128 + 128 * (1 + 3 * IT))
                    act.dma_start(he_d[bass.ds(it * Q + q, 1), :, :].rearrange("a p e -> (a p) e"),
                                  gat[:, q, :, :].rearrange("p s c -> p (s c)")).then_inc(s_hest[q], 16)
                    nc.scalar.activation(trip[:, bass.ds(it * Q + q, 1), :, 0].rearrange("p a s -> p (a s)"),
                                         gat[:, q, :, D], ACT.Copy).then_inc(s_scan_copy, 1)
                    if q:
                        free_slot(q - 1, it)
                free_slot(Q - 1, it)
            act.wait_ge(s_scan_copy, G)
            act.sem_inc(s_trip, 1)
            for k, (dst, srcv) in enumerate(((score, gap), (self_score, self_gap))):
                act.wait_ge(s_ein, k + 1)
                nc.scalar.activation(dst, srcv, ACT.Exp).then_inc(s_eout, 1)
            act.wait_ge(s_sum[4], 1)
            with act.Fori(0, NI) as it:
                for u in range(2):
                    b = act.snap(it * 2 + u)
                    wait_reg(act, s_mm[5], b + 1)
                    nc.scalar.activation(stage[0:HROW, u, :], sum_t[0:HROW, nodes(b)], ACT.Copy)
                    wait_reg(act, s_tr[5], b + 1)
                    nc.scalar.activation(xt[0:D, u, :], p_tr_flat[0:D, 0:BC], ACT.Copy).then_inc(s_stage[5], 1)
                    square_root(5, b, 0, 1)

        @block.tensor
        def _(pe):
            pe.wait_ge(s_const, 2)
            pe.wait_ge(s_cols, 1)
            for c in range(4):
                for a in range(2):
                    at = (c % 2) * G + a * SG
                    ins = nc.tensor.matmul(p_a[0:1, c // 2, at:at + SG], wcols[:, c, a:a + 1], ident[0:SG, 0:SG],
                                           start=True, stop=True)
            ins.then_inc(s_rows, 1)
            pe.wait_ge(s_wload, 16 * len(WEIGHTS))
            for r in range(R):
                ins = nc.tensor.matmul(p_b[0:D, 0, 2 * r:2 * r + 2], wt["wrt"][:, r * D:(r + 1) * D],
                                       wt["att"][:, 2 * r:2 * r + 2], start=True, stop=True)
            ins.then_inc(s_sdw, 1)
            pe.wait_ge(s_win, 1)
            pe.wait_ge(s_patch, 64)

            def sum_pass(n, width, ready, lhs):
                with pe.Fori(0, IT) as it:
                    for q in range(Q):
                        _, cnt, cum = group_windows(pe, 0, it * Q + q)
                        ready(it, q)
                        with pe.Fori(0, cnt) as k:
                            for s in range(S):
                                if s % (S // 2) == 0:
                                    pe.wait_ge(s_oh[n][s // (S // 2)], cum + k + 1)
                                ins = nc.tensor.matmul(p_sum[0:width, 0, 0:W], lhs(q, s), oh[:, 0, s, :],
                                                       start=(s == 0), stop=(s == S - 1))
                            ins.then_inc(s_agg[n], 1)

            def transposes(n, width, src):
                for t in range(BT):
                    ins = nc.tensor.transpose(p_tr[0:width, t // 4, (t % 4) * W:(t % 4 + 1) * W], src(t), ident[:, :])
                ins.then_inc(s_tr[n], 1)

            def tile(buf, u, t, k):
                return buf[0:k, u, t * W:(t + 1) * W]

            sum_pass(0, D + 2, lambda it, q: wait_reg(pe, s_msg, it * Q + (q + 1)), lambda q, s: msg[:, q % 2, s, 0:D + 2])
            with pe.Fori(0, NI) as it:
                for u in range(2):
                    b = pe.snap(it * 2 + u)
                    wait_reg(pe, s_xs[u], it * 16 + 16 * (1 + NI * 0))
                    wait_reg(pe, s_stage[0], b + 1)
                    transposes(0, D, lambda t: xs[:, u, t, :])
                    wait_reg(pe, s_stage[0], b + 2)
                    wait_reg(pe, s_xfree[0], b + 1)
                    for t in range(BT):
                        nc.tensor.matmul(p_a[:, u, t * D:(t + 1) * D], tile(xt, u, t, D + 1), wt["ws65"][:, :],
                                         start=True, stop=True)
                        ins = nc.tensor.matmul(p_b[:, u, t * 66:(t + 1) * 66], tile(stage, u, t, 66), wn66[:, :],
                                               start=True, stop=True)
                    ins.then_inc(s_mm[0], 1)
            if upto == 0:
                return
            sum_pass(1, D, lambda it, q: wait_reg(pe, s_msg, it * Q + (G + q + 1)), lambda q, s: msg[:, q % 2, s, 0:D])
            with pe.Fori(0, NI) as it:
                for u in range(2):
                    b = pe.snap(it * 2 + u)
                    wait_reg(pe, s_xs[u], it * 16 + 16 * (1 + NI * 1))
                    wait_reg(pe, s_stage[1], b + 1)
                    transposes(1, D, lambda t: xs[:, u, t, :])
                    wait_reg(pe, s_stage[1], b + 2)
                    wait_reg(pe, s_xfree[1], b + 1)
                    for h, bank in ((0, p_a), (1, p_b)):
                        ins = nc.tensor.matmul(bank[0:D, u, 0:HB], wt["w1"][:, :],
                                               stage[0:D, u, h * HB:(h + 1) * HB], start=True, stop=True)
                    ins.then_inc(s_mid[1], 1)
                    wait_reg(pe, s_act[1], b + 1)
                    for t in range(BT):
                        ins = nc.tensor.matmul(p_a[:, u, t * D:(t + 1) * D], tile(xt, u, t, D + 1),
                                               wt["w2b"][:, :], start=True, stop=True)
                    ins.then_inc(s_mm[1], 1)
            if upto == 1:
                return
            sum_pass(2, D, lambda it, q: wait_reg(pe, s_gat[q], it * 128 + 128 * (1 + 2 * IT)),
                     lambda q, s: gat[:, q, s, 0:D])
            pe.wait_ge(s_sum[2], 1)
            with pe.Fori(0, NI) as it:
                for u in range(2):
                    b = pe.snap(it * 2 + u)
                    wait_reg(pe, s_act[2], b + 1)
                    wait_reg(pe, s_stage[2], b + 1)
                    transposes(2, D + 1, lambda t: xd[:, u, t, :])
                    wait_reg(pe, s_stage[2], b + 2)
                    wait_reg(pe, s_mid[2], b + 1)
                    for h, bank in ((0, p_a), (1, p_b)):
                        nc.tensor.matmul(bank[0:D, u, 0:HB], wd65[:, :], stage[0:D + 1, u, h * HB:(h + 1) * HB],
                                         start=True, stop=False)
                        ins = nc.tensor.matmul(bank[0:D, u, 0:HB], wj66[:, :], sum_t[0:D + 2, nodes(b, HB, h * HB)],
                                               start=False, stop=True)
                    ins.then_inc(s_mm[2], 1)
            with pe.Fori(0, NI) as it:
                for u in range(2):
                    b = pe.snap(it * 2 + u)
                    wait_reg(pe, s_mid[3], b + 3)
                    wait_reg(pe, s_xfree[3], b + 1)
                    for t in range(BT):
                        ins = nc.tensor.transpose(p_b[:, u, t * D:(t + 1) * D], tile(xt, u, t, D), ident[0:D, 0:D])
                    ins.then_inc(s_mm[3], 1)
            if upto == 2:
                return
            with pe.Fori(0, NI) as it:
                for u in range(2):
                    b = pe.snap(it * 2 + u)
                    wait_reg(pe, s_xs[u], it * 16 + 16 * (1 + NI * 4))
                    wait_reg(pe, s_stage[4], b + 1)
                    transposes(4, D, lambda t: xs[:, u, t, :])
                    wait_reg(pe, s_stage[4], b + 2)
                    wait_reg(pe, s_xfree[4], b + 1)
                    for t in range(BT):
                        nc.tensor.matmul(p_sum[:, u, t * 16:(t + 1) * 16], tile(xt, u, t, D), sdw[:, :],
                                         start=True, stop=True)
                    for t in range(BT):
                        k, m = (BT * u + t) % 2, (BT * u + t) // 2
                        wait_reg(pe, s_hc[0][k], it * BT + (m + 1))
                        ins = nc.tensor.matmul(p_a[:, k, :], tile(xt, u, t, D), wt["wcat"][:, :],
                                               start=True, stop=True)
                        ins.then_inc(s_h[0][k], 1)
                    wait_reg(pe, s_h[0][k], it * BT + (m + 1))
                    pe.sem_inc(s_mm[4], 1)
            with pe.Fori(0, IT) as it:
                for q in range(Q):
                    first, cnt, cum = group_windows(pe, 1, it * Q + q)
                    with pe.Fori(0, cnt) as k:
                        wait_reg(pe, s_oh[3][0], cum + k + 1)
                        w = within(first + k, NW - 1)
                        table = dtab[:, bass.ds(w, 1), :].rearrange("p a c -> p (a c)")
                        for s in range(S):
                            ins = nc.tensor.matmul(p_sum[0:P, 0, s * 2 * R:(s + 1) * 2 * R], oht_tile[:, :, s], table,
                                                   start=True, stop=True)
                        ins.then_inc(s_agg[3], 1)
            sum_pass(4, HROW, lambda it, q: wait_reg(pe, s_msg, it * Q + (2 * G + q + 1)),
                     lambda q, s: msg[:, q % 2, s, :])
            with pe.Fori(0, NI) as it:
                for u in range(2):
                    b = pe.snap(it * 2 + u)
                    wait_reg(pe, s_xs[u], it * 16 + 16 * (1 + NI * 5))
                    wait_reg(pe, s_stage[5], b + 1)
                    transposes(5, D, lambda t: xs[:, u, t, :])
                    wait_reg(pe, s_stage[5], b + 2)
                    wait_reg(pe, s_xfree[5], b + 1)
                    for t in range(BT):
                        nc.tensor.matmul(p_a[:, u, t * D:(t + 1) * D], tile(xt, u, t, D + 1), wself65[:, :],
                                         start=True, stop=True)
                        ins = nc.tensor.matmul(p_b[:, u, t * HROW:(t + 1) * HROW], tile(stage, u, t, HROW),
                                               ident[0:HROW, 0:HROW], start=True, stop=True)
                    ins.then_inc(s_mid[5], 1)
                    for t in range(BT):
                        k, m = (BT * u + t) % 2, (BT * u + t) // 2
                        wait_reg(pe, s_hc[1][k], it * BT + (m + 1))
                        ins = nc.tensor.matmul(p_sum[:, k, :], tile(xt, u, t, D), wt["wcat"][:, :],
                                               start=True, stop=True)
                        ins.then_inc(s_h[1][k], 1)
                    wait_reg(pe, s_h[1][k], it * BT + (m + 1))
                    pe.sem_inc(s_mm[5], 1)

        @block.vector
        def _(dve):
            ch = Chain(dve, s_vch)
            vec = nc.vector

            def bc(ap, *shape):
                return ap.to_broadcast(list(shape))

            for q in range(Q):
                dve.sem_inc(s_free[q], 1)
            for group, credit in ((s_xfree, 2), (s_mm, 2), (s_stage.values(), 1), (s_yfree.values(), 2)):
                for s in group:
                    dve.sem_inc(s, credit)
            for s in (s_tr[2], s_mid[2], s_mid[3]):
                dve.sem_inc(s, 2)
            for n in range(2):
                for k in range(2):
                    dve.sem_inc(s_hc[n][k], 1)
            vec.memset(eps_col[:, :], EPS_LN)
            vec.memset(wones[:, :], 1.0)
            vec.memset(xt[D:D + 1, :, :], 1.0)
            vec.memset(msg[:, :, :, D + 1], 1.0).then_inc(s_vconst, 1)
            vec.memset(xs[:, :, :, :], 0.0).then_inc(s_vconst, 1)

            ch.start()
            dve.wait_ge(s_load[0], 16)
            ch.add(vec.tensor_reduce(out=ends_g[:, 0, :], in_=stat_i, op=ALU.min, axis=AX.X))
            ch(vec.tensor_reduce(out=ends_g[:, 1, :], in_=stat_i, op=ALU.max, axis=AX.X))
            ch(vec.tensor_copy(ends_i[:, 0:2, :], ends_g[:, :, :]))
            for table, shift in ((0, 5), (1, 7)):
                lo, steps = ends_i[:, 2, :], ends_i[:, 3, :]
                ch(vec.tensor_single_scalar(lo, ends_i[:, 0, :], shift, op=ALU.arith_shift_right))
                ch(vec.tensor_copy(wcols[:, 2 * table, :], lo))
                ch(vec.scalar_tensor_tensor(out=steps, in0=wcols[:, 2 * table, :], scalar=-float(1 << shift),
                                            in1=ends_g[:, 1, :], op0=ALU.mult, op1=ALU.add))
                ch(vec.tensor_single_scalar(steps, steps, 7, op=ALU.arith_shift_right))
                ch(vec.tensor_copy(wcols[:, 2 * table + 1, :], steps))
            dve.sem_inc(s_cols, 1)
            dve.wait_ge(s_load[1], 16)
            vec.tensor_copy(dstf[:, :, :].rearrange("p g s -> p (g s)"), dst_i)
            dve.wait_ge(s_rows, 1)
            ch(vec.tensor_copy(wrows[:, 0:2, :], p_a[0:1, 0, 0:2 * G].rearrange("a (c g) -> a c g", c=2)))
            ch(vec.tensor_copy(wrows[:, 2:4, :], p_a[0:1, 1, 0:2 * G].rearrange("a (c g) -> a c g", c=2)))
            for table in range(2):
                first, more, before, upto_g = (wrows[:, 2 * table, :], wrows[:, 2 * table + 1, :],
                                               wrows[:, 4, :], wrows[:, 5, :])
                ch(vec.tensor_scalar_add(upto_g, more, 1.0))
                ch(vec.tensor_tensor_scan(before, wones[:, :], upto_g, 0.0, ALU.mult, ALU.add))
                ch(vec.tensor_tensor(before, before, upto_g, ALU.subtract))
                for c, rowv in enumerate((first, more, before)):
                    ch.add(vec.tensor_copy(wint[:, c, :], rowv))
                ch.wait()
                ch(vec.tensor_single_scalar(wint[:, 0, :], wint[:, 0, :], 7, op=ALU.logical_shift_left))
                ch(vec.tensor_single_scalar(wint[:, 2, :], wint[:, 2, :], 16, op=ALU.logical_shift_left))
                ch(vec.tensor_tensor(wint[:, 0, :], wint[:, 0, :], wint[:, 1, :], ALU.bitwise_or))
                ch(vec.tensor_tensor(win[:, table, :], wint[:, 0, :], wint[:, 2, :], ALU.bitwise_or))
            dve.sem_inc(s_win, 1)

            dve.wait_ge(s_const, 6)
            dve.wait_ge(s_wload, 16 * len(WEIGHTS))
            ch.add(vec.tensor_copy(wn66[:, :], ident[0:D + 2, 0:D + 2]))
            ch(vec.memset(wj66[:, :], 0.0))
            ch.add(vec.tensor_copy(wj66[0:D, :], wt["wj"][:, :]))
            ch.add(vec.tensor_tensor(wd65[0:D, :], wt["wi"][:, :], wt["wj"][:, :], ALU.subtract))
            ch(vec.tensor_reduce(out=brow[0:1, :], in_=wt["rbias"][0:1, :].rearrange("a (r d) -> a d r", r=R),
                                 op=ALU.add, axis=AX.X))
            ch(vec.tensor_tensor(brow[0:1, :], brow[0:1, :], wt["bself"][0:1, :], ALU.add))
            dve.sem_inc(s_prep, 1)
            dve.wait_ge(s_sdw, 1)
            ch(vec.tensor_copy(sdw[:, :].rearrange("d (c r) -> d c r", c=2),
                               p_b[0:D, 0, 0:2 * R].rearrange("d (r c) -> d c r", c=2)))
            dve.wait_ge(s_load[3], 16)
            dve.wait_ge(s_load[4], 16)
            dve.wait_ge(s_load[5], 16)
            ch.add(vec.tensor_copy(typef[:, :, :].rearrange("p g s -> p (g s)"), type_i))
            ch.add(vec.scalar_tensor_tensor(out=src_i, in0=src_i, scalar=float(R), in1=type_i, op0=ALU.mult, op1=ALU.add))
            ch(vec.tensor_copy(dst16, dstn_i))
            dve.sem_inc(s_key, 1)

            def by_tile(ap, width):
                return bc(ap.unsqueeze(2), P, S, width)

            def sum_windows(n, width, g, first, cnt, cum):
                with dve.Fori(0, cnt) as k:
                    at = dve.snap(within(first + k * (W // FW), (N - 1) // FW))
                    half = S // 2
                    for h in range(2):
                        dst = dstf[:, bass.ds(g, 1), h * half:(h + 1) * half].rearrange("p a s -> p (a s)")
                        vec.scalar_tensor_tensor(
                            out=oh[:, 0, h * half:(h + 1) * half, :], in0=bc(dst.unsqueeze(2), P, half, W),
                            scalar=fine_col[0:P, bass.ds(at, 1)], in1=bc(iota[0:P, :].unsqueeze(1), P, half, W),
                            op0=ALU.subtract, op1=ALU.is_equal).then_inc(s_oh[n][h], 1)
                    wait_reg(dve, s_agg[n], cum + k + 1)
                    part = sum_t[0:width, bass.ds(at * FW, W)]
                    vec.tensor_tensor(part, part, p_sum[0:width, 0, 0:W], ALU.add).then_inc(s_acc, 1)

            def sum_pass(n, width, prepare, done=None):
                ch.start()
                ch(vec.memset(sum_t[0:max(width, D + 2), :], 0.0))
                with dve.Fori(0, IT) as it:
                    for q in range(Q):
                        g = it * Q + q
                        first, cnt, cum = group_windows(dve, 0, g)
                        prepare(it, q, g)
                        sum_windows(n, width, g, first, cnt, cum)
                        if done:
                            done(q)
                vec.memset(r1[:, :], 0.0).then_inc(s_sum[n], 1)

            def weighted(n):
                landed, per, base = (s_gat, 16 * S, 0) if n == 0 else (s_held, 16, 0)
                count = 0 if n == 0 else 2 * G

                def prepare(it, q, g):
                    wait_reg(dve, landed[q], it * per + per)
                    w = of_group(edge_w, g)
                    if n == 0:
                        vec.tensor_copy(msg[:, q % 2, :, D], w)
                    else:
                        ch.start()
                        ch(vec.tensor_tensor(toh[:, :, :], by_tile(of_group(typef, g), R),
                                             bc(rel_col[0:P, :].unsqueeze(1), P, S, R), ALU.is_equal))
                        vec.tensor_tensor(msg[:, q % 2, :, D:HROW], toh[:, :, :], by_tile(w, R), ALU.mult)
                    vec.tensor_tensor(msg[:, q % 2, :, 0:D], gat[:, q, :, 0:D], by_tile(w, D), ALU.mult)\
                        .then_inc(s_msg, 1)
                    wait_reg(dve, s_msg, it * Q + (count + q + 1))
                    dve.sem_inc(s_free[q], 1)
                return prepare

            def layer_norm(n, b, u):
                ch(vec.tensor_reduce(out=r2[:, :], in_=ya[:, :, :], op=ALU.add, axis=AX.X))
                ch(vec.tensor_scalar(r2[:, :], r2[:, :], 1.0 / D, None, ALU.mult))
                ch(vec.tensor_tensor(ya[:, :, :], ya[:, :, :], bc(r2[:, :].unsqueeze(2), 128, BT, D), ALU.subtract))
                ch(vec.tensor_tensor(yb[:, :, :], ya[:, :, :], ya[:, :, :], ALU.mult))
                ch(vec.tensor_reduce(out=r2[:, :], in_=yb[:, :, :], op=ALU.add, axis=AX.X))
                dve.sem_inc(s_sqrt_in[n], 1)
                wait_reg(dve, s_sqrt[n], b * (2 if n == 0 else 1) + (2 if n == 0 else 1))
                ch(vec.reciprocal(r2[:, :], r2[:, :]))
                wait_reg(dve, s_yfree[n], b + 1)
                vec.tensor_tensor(yo[:, u, :, :], ya[:, :, :], bc(r2[:, :].unsqueeze(2), 128, BT, D), ALU.mult)\
                    .then_inc(s_y[n], 1)

            def bank(p, u, width):
                return p[:, u, 0:BT * width].rearrange("p (t d) -> p t d", t=BT)

            dve.wait_ge(s_load[2], 16)
            sum_pass(0, D + 2, weighted(0))
            with dve.Fori(0, NI) as it:
                for u in range(2):
                    b = dve.snap(it * 2 + u)
                    ch.start()
                    wait_reg(dve, s_mm[0], b + 3)
                    own, nb = bank(p_a, u, D), bank(p_b, u, D + 2)
                    ch.add(vec.tensor_copy(deg[:, bass.ds(b * BT, BT)], nb[:, :, D + 1]))
                    ch(vec.tensor_scalar_max(r1[:, :], nb[:, :, D], 1e-8))
                    ch(vec.reciprocal(r1[:, :], r1[:, :]))
                    ch(vec.tensor_tensor(ya[:, :, :], nb[:, :, 0:D], bc(r1[:, :].unsqueeze(2), 128, BT, D), ALU.mult))
                    ch(vec.tensor_tensor(ya[:, :, :], ya[:, :, :], own, ALU.add))
                    ch(vec.tensor_tensor(yb[:, :, :], ya[:, :, :], ya[:, :, :], ALU.mult))
                    ch(vec.tensor_reduce(out=r1[:, :], in_=yb[:, :, :], op=ALU.add, axis=AX.X))
                    dve.sem_inc(s_sqrt_in[0], 1)
                    wait_reg(dve, s_sqrt[0], b * 2 + 1)
                    ch(vec.tensor_scalar_max(r1[:, :], r1[:, :], 1e-12))
                    ch(vec.reciprocal(r1[:, :], r1[:, :]))
                    ch(vec.tensor_tensor(ya[:, :, :], ya[:, :, :], bc(r1[:, :].unsqueeze(2), 128, BT, D), ALU.mult))
                    wait_reg(dve, s_xs[u], it * 16 + 16 * (1 + NI * 0))
                    ch(vec.tensor_tensor(ya[:, :, :], ya[:, :, :], xs[:, u, :, :], ALU.add))
                    dve.sem_inc(s_xfree[0], 1)
                    layer_norm(0, b, u)
            if upto == 0:
                return

            def prepare1(it, q, g):
                wait_reg(dve, s_gat[q], it * 128 + 128 * (1 + IT))
                wait_reg(dve, s_ea[q], it * 16 + 16)
                vec.tensor_tensor(ea[:, q, :, :], ea[:, q, :, :], gat[:, q, :, 0:D], ALU.add).then_inc(s_pre, 1)

            sum_pass(1, D, prepare1)
            with dve.Fori(0, NI) as it:
                for u in range(2):
                    b = dve.snap(it * 2 + u)
                    ch.start()
                    wait_reg(dve, s_tr[1], b + 1)
                    vec.tensor_tensor(stage[0:D, u, :], p_tr_flat[0:D, 0:BC], sum_t[0:D, nodes(b)], ALU.add)\
                        .then_inc(s_stage[1], 1)
                    wait_reg(dve, s_mm[1], b + 3)
                    wait_reg(dve, s_xs[u], it * 16 + 16 * (1 + NI * 1))
                    ch(vec.tensor_tensor(ya[:, :, :], bank(p_a, u, D), xs[:, u, :, :], ALU.add))
                    dve.sem_inc(s_xfree[1], 1)
                    layer_norm(1, b, u)
            if upto == 1:
                return

            def prepare2(it, q, g):
                pass

            sum_pass(2, D, prepare2, lambda q: dve.sem_inc(s_free[q], 1))

            def scale_rows(it, u, b):
                wait_reg(dve, s_xs[u], it * 16 + 16 * (1 + NI * 2))
                wait_reg(dve, s_tr[2], b + 1)
                dv = deg[:, bass.ds(b * BT, BT)]
                vec.tensor_copy(xd[:, u, :, D], dv)
                vec.tensor_tensor(xd[:, u, :, 0:D], xs[:, u, :, :], bc(dv.unsqueeze(2), 128, BT, D), ALU.mult)\
                    .then_inc(s_act[2], 1)
                wait_reg(dve, s_act[2], b + 1)
                dve.sem_inc(s_xfree[2], 1)

            with dve.Fori(0, NI) as it:
                for u in range(2):
                    b = dve.snap(it * 2 + u)
                    scale_rows(it, u, b)
                    wait_reg(dve, s_mm[2], b + 3)
                    vec.tensor_copy(sum_t[0:D, nodes(b, HB)], p_a[0:D, u, 0:HB])
                    vec.tensor_copy(sum_t[0:D, nodes(b, HB, HB)], p_b[0:D, u, 0:HB]).then_inc(s_mid[2], 1)
            dve.wait_ge(s_mid[2], NB + 2)
            ch.start()
            for c in range(25):
                ch.add(vec.bn_stats(out=bn[:, c, :], in_=sum_t[0:D, c * (N // 25):(c + 1) * (N // 25)]))
            ch.wait()
            ch(vec.bn_aggr(out=bnm[:, 0:2], in_=bn[:, :, :].rearrange("d c k -> d (c k)")))
            dve.sem_inc(s_bn, 1)
            dve.wait_ge(s_bnr, 1)
            ch(vec.reciprocal(bnm[:, 3:4], bnm[:, 2:3]))
            ch(vec.tensor_tensor(bnm[:, 3:4], bnm[:, 3:4], wt["gamma"][:, :], ALU.mult))
            ch(vec.tensor_tensor(bnm[:, 4:5], bnm[:, 0:1], bnm[:, 3:4], ALU.mult))
            ch(vec.tensor_tensor(bnm[:, 4:5], wt["beta"][:, :], bnm[:, 4:5], ALU.subtract))
            dve.sem_inc(s_bnc, 1)
            with dve.Fori(0, NI) as it:
                for u in range(2):
                    b = dve.snap(it * 2 + u)
                    ch.start()
                    wait_reg(dve, s_act[3], b + 1)
                    vec.scalar_tensor_tensor(out=xt[0:D, u, :], in0=stage[0:D, u, :], scalar=0.01,
                                             in1=stage[0:D, u, :], op0=ALU.mult, op1=ALU.max).then_inc(s_mid[3], 1)
                    wait_reg(dve, s_mm[3], b + 3)
                    wait_reg(dve, s_xs[u], it * 16 + 16 * (1 + NI * 3))
                    ch(vec.tensor_tensor(ya[:, :, :], bank(p_b, u, D), xs[:, u, :, :], ALU.add))
                    dve.sem_inc(s_xfree[3], 1)
                    layer_norm(3, b, u)
            if upto == 2:
                return

            ch.start()
            dve.wait_ge(s_y[3], NB)
            for u in range(2):
                ch(vec.memset(hst[:, u, :, :, D + 1:HROW], 0.0))
            dve.sem_inc(s_zero, 1)
            with dve.Fori(0, NI) as it:
                for u in range(2):
                    b = dve.snap(it * 2 + u)
                    ch.start()
                    wait_reg(dve, s_yfree[4], b + 1)
                    for t in range(1 - u, BT, 2):
                        m = (BT * u + t) // 2
                        wait_reg(dve, s_h[0][1], it * BT + (m + 1))
                        vec.tensor_copy(hst[:, u, t, :, 0:D], p_a[:, 1, :].rearrange("p (r d) -> p r d", r=R))\
                            .then_inc(s_hc[0][1], 1)
                    wait_reg(dve, s_mm[4], b + 3)
                    ch(vec.tensor_copy(sd[:, :, :], bank(p_sum, u, 2 * R)))
                    dve.sem_inc(s_xfree[4], 1)
                    table = dtab[:, bass.ds(b * BT, BT), :]
                    ch.add(vec.tensor_copy(hst[:, u, :, :, D], sd[:, :, 0:R]))
                    ch.add(vec.tensor_copy(table[:, :, 0:R], sd[:, :, R:2 * R]))
                    ch(vec.tensor_tensor(sd[:, :, 0:R], sd[:, :, 0:R], sd[:, :, R:2 * R], ALU.add))
                    ch(vec.scalar_tensor_tensor(out=table[:, :, R:2 * R], in0=sd[:, :, 0:R], scalar=0.2,
                                                in1=sd[:, :, 0:R], op0=ALU.mult, op1=ALU.max))
                    wait_reg(dve, s_hc[0][1], it * BT + (m + 2))
                    dve.sem_inc(s_y[4], 1)

            ch.start()
            ch(vec.memset(trip_flat, 0.0))
            dve.sem_inc(s_zero, 1)
            dve.wait_ge(s_table, 4)
            dve.wait_ge(s_rld[0], 16)
            dve.wait_ge(s_rld[1], 16)
            ch.add(vec.tensor_copy(val, scan_dst_i))
            ch(vec.tensor_copy(rtype, scan_type_i))
            ch.add(vec.tensor_copy(ends[:, 0:1], val[:, 0:1]))
            ch.add(vec.tensor_copy(ends[:, 1:2], val[:, T - 1:T]))
            ch.add(vec.tensor_tensor(brk_f[:, 1:T], val[:, 1:T], val[:, 0:T - 1], ALU.is_equal))
            ch.add(vec.memset(brk_f[:, 0:1], 1.0))
            ch.add(vec.tensor_tensor(brk_b[:, 0:T - 1], val[:, 1:T], val[:, 0:T - 1], ALU.is_equal))
            ch(vec.memset(brk_b[:, T - 1:T], 1.0))
            ch.add(vec.tensor_scalar(lead, val, ends[:, 0:1], None, ALU.is_equal))
            ch(vec.tensor_scalar(trail, val, ends[:, 1:2], None, ALU.is_equal))
            masks = (brk_f, brk_b, lead, trail)
            for m_ in masks:
                ch.add(vec.tensor_scalar(m_, m_, 1.0, BIG, ALU.subtract, ALU.mult))
            ch.add(vec.tensor_copy(runs[:, 2 * R:2 * R + 2], ends[:, :]))
            ch.wait()

            with dve.Fori(0, IT) as it:
                for q in range(Q):
                    g = it * Q + q
                    first, cnt, cum = group_windows(dve, 1, g)
                    ch.start()
                    ch(vec.tensor_tensor(toh[:, :, :], by_tile(of_group(typef, g), R),
                                         bc(rel_col[0:P, :].unsqueeze(1), P, S, R), ALU.is_equal))
                    wait_reg(dve, s_drow[q % 2], it * 32 + 16 * (1 + q // 2))
                    with dve.Fori(0, cnt) as k:
                        w = dve.snap(within(first + k, NW - 1))
                        ch2 = Chain(dve, s_vch)
                        ch2.start()
                        vec.tensor_scalar(oht[:, :], drow[:, q % 2, :], node_col[:, bass.ds(w, 1)], None,
                                          ALU.is_equal).then_inc(s_oh[3][0], 1)
                        wait_reg(dve, s_agg[3], cum + k + 1)
                        ch2(vec.tensor_tensor(
                            sel[:, :, :, :], p_sum[0:P, 0, 0:S * 2 * R].rearrange("p (s c r) -> p s c r", s=S, c=2),
                            bc(toh[:, :, :].unsqueeze(2), P, S, 2, R), ALU.mult))
                        ch2(vec.tensor_reduce(out=sel2[:, :, :], in_=sel[:, :, :, :], op=ALU.add, axis=AX.X))
                        part = trip[:, bass.ds(g, 1), :, 1:3].rearrange("p a s c -> p (a s) c")
                        ch2(vec.tensor_tensor(part, part, sel2[:, :, :], ALU.add))
                    dve.sem_inc(s_drused, 1)
            dve.sem_inc(s_trip, 1)

            ch.start()
            dve.wait_ge(s_scan, 16)
            ch(vec.tensor_tensor(score, score, gap, ALU.add))
            ch(vec.scalar_tensor_tensor(out=score, in0=score, scalar=0.2, in1=score, op0=ALU.mult, op1=ALU.max))
            ch(vec.tensor_copy(best, self_score))

            def exchange(k, maximum):
                neutral = -BIG if maximum else 0.0
                dve.wait_ge(s_rund, 64 * k + 32)
                firsts, lasts = run_row[:, :, 2 * R], run_row[:, :, 2 * R + 1]
                joined, through = link_row[:, 0, :], link_row[:, 1, :]
                ch(vec.memset(link_row[:, :, :], 0.0))
                ch.add(vec.tensor_tensor(joined[:, 1:P], firsts[:, 1:P], lasts[:, 0:P - 1], ALU.is_equal))
                ch(vec.tensor_tensor(through[:, 0:P], firsts, lasts, ALU.is_equal))
                pf, pb = link_row[:, 2, 0:P], link_row[:, 3, 0:P]
                ch.add(vec.tensor_tensor(pf, joined[:, 0:P], through[:, 0:P], ALU.mult))
                ch(vec.tensor_tensor(pb, joined[:, 1:P + 1], through[:, 0:P], ALU.mult))
                if maximum:
                    ch(vec.tensor_scalar(link_row[:, 0, :], link_row[:, 0, :], 1.0, BIG, ALU.subtract, ALU.mult))
                    ch(vec.tensor_scalar(link_row[:, 2:4, :], link_row[:, 2:4, :], 1.0, BIG, ALU.subtract, ALU.mult))
                op0, op1 = (ALU.add, ALU.max) if maximum else (ALU.mult, ALU.add)
                for r in range(R):
                    ch.add(vec.tensor_tensor_scan(carry_row[:, :, r], pf, run_row[:, :, r], neutral, op0, op1))
                    ch.add(vec.tensor_tensor_scan(carry_row[:, ::-1, R + r], pb[:, ::-1], run_row[:, ::-1, R + r],
                                                  neutral, op0, op1))
                ch.wait()
                link_op = ALU.add if maximum else ALU.mult
                ch.add(vec.memset(init_row[:, 0:1, 0:R], neutral))
                ch.add(vec.memset(init_row[:, P - 1:P, R:2 * R], neutral))
                ch.add(vec.tensor_tensor(init_row[:, 1:P, 0:R], carry_row[:, 0:P - 1, 0:R],
                                         bc(joined[:, 1:P].unsqueeze(2), 1, P - 1, R), link_op))
                ch(vec.tensor_tensor(init_row[:, 0:P - 1, R:2 * R], carry_row[:, 1:P, R:2 * R],
                                     bc(joined[:, 1:P].unsqueeze(2), 1, P - 1, R), link_op))
                dve.sem_inc(s_run, 1)
                dve.wait_ge(s_rund, 64 * k + 64)

            ends_of = ((trail, 0), (lead, R))
            with dve.Fori(0, R) as r:
                ch2 = Chain(dve, s_vch)
                ch2.start()
                ch2(vec.tensor_scalar(off, rtype, rel_col[0:P, bass.ds(r, 1)], -BIG, ALU.not_equal, ALU.mult))
                ch2(vec.tensor_tensor(val, score, off, ALU.add))
                for mask, at in ends_of:
                    ch2(vec.tensor_tensor(fwd, val, mask, ALU.add))
                    ch2(vec.tensor_reduce(out=runs[:, bass.ds(r + at, 1)], in_=fwd, op=ALU.max, axis=AX.X))
            ch.start()
            dve.sem_inc(s_run, 1)
            exchange(0, True)
            with dve.Fori(0, R) as r:
                ch2 = Chain(dve, s_vch)
                ch2.start()
                ch2(vec.tensor_scalar(off, rtype, rel_col[0:P, bass.ds(r, 1)], -BIG, ALU.not_equal, ALU.mult))
                ch2(vec.tensor_tensor(val, score, off, ALU.add))
                ch2.add(vec.tensor_tensor_scan(fwd, brk_f, val, run_in[:, bass.ds(r, 1)], ALU.add, ALU.max))
                ch2(vec.tensor_tensor_scan(bwd[:, ::-1], brk_b[:, ::-1], val[:, ::-1], run_in[:, bass.ds(r + R, 1)],
                                           ALU.add, ALU.max))
                ch2(vec.tensor_tensor(fwd, fwd, bwd, ALU.max))
                ch2(vec.tensor_tensor(fwd, fwd, off, ALU.add))
                ch2(vec.tensor_tensor(best, best, fwd, ALU.max))
            ch.start()
            ch(vec.tensor_tensor(gap, score, best, ALU.subtract))
            dve.sem_inc(s_ein, 1)
            ch.add(vec.tensor_tensor(self_gap, self_score, best, ALU.subtract))
            for m_ in masks:
                ch.add(vec.tensor_single_scalar(m_, m_, 0.0, op=ALU.is_equal))
            ch.wait()
            dve.sem_inc(s_ein, 1)
            dve.wait_ge(s_eout, 2)
            ch(vec.tensor_copy(best, self_score))
            with dve.Fori(0, R) as r:
                ch2 = Chain(dve, s_vch)
                ch2.start()
                ch2(vec.scalar_tensor_tensor(out=val, in0=rtype, scalar=rel_col[0:P, bass.ds(r, 1)], in1=score,
                                             op0=ALU.is_equal, op1=ALU.mult))
                for mask, at in ends_of:
                    ch2(vec.tensor_tensor(fwd, val, mask, ALU.mult))
                    ch2(vec.tensor_reduce(out=runs[:, bass.ds(r + at, 1)], in_=fwd, op=ALU.add, axis=AX.X))
            ch.start()
            dve.sem_inc(s_run, 1)
            exchange(1, False)
            with dve.Fori(0, R) as r:
                ch2 = Chain(dve, s_vch)
                ch2.start()
                ch2(vec.scalar_tensor_tensor(out=val, in0=rtype, scalar=rel_col[0:P, bass.ds(r, 1)], in1=score,
                                             op0=ALU.is_equal, op1=ALU.mult))
                ch2.add(vec.tensor_tensor_scan(fwd, brk_f, val, run_in[:, bass.ds(r, 1)], ALU.mult, ALU.add))
                ch2(vec.tensor_tensor_scan(bwd[:, ::-1], brk_b[:, ::-1], val[:, ::-1], run_in[:, bass.ds(r + R, 1)],
                                           ALU.mult, ALU.add))
                ch2(vec.tensor_tensor(fwd, fwd, bwd, ALU.add))
                ch2(vec.tensor_tensor(fwd, fwd, val, ALU.subtract))
                ch2(vec.scalar_tensor_tensor(out=fwd, in0=rtype, scalar=rel_col[0:P, bass.ds(r, 1)], in1=fwd,
                                             op0=ALU.is_equal, op1=ALU.mult))
                ch2(vec.tensor_tensor(best, best, fwd, ALU.add))
            ch.start()
            ch(vec.reciprocal(best, best))
            ch(vec.tensor_tensor(val, score, best, ALU.mult))
            dve.sem_inc(s_alpha, 1)
            dve.wait_ge(s_alphal, 16)

            sum_pass(4, HROW, weighted(4))
            with dve.Fori(0, NI) as it:
                for u in range(2):
                    b = dve.snap(it * 2 + u)
                    ch.start()
                    wait_reg(dve, s_mid[5], b + 1)
                    own, nb = bank(p_a, u, D), bank(p_b, u, HROW)
                    ch(vec.tensor_scalar(self_w[:, :, :], nb[:, :, D:HROW], -1.0, 1.0, ALU.mult, ALU.add))
                    for t in range(BT):
                        k, m = (BT * u + t) % 2, (BT * u + t) // 2
                        wait_reg(dve, s_h[1][k], it * BT + (m + 1))
                        ch(vec.tensor_tensor(hs[:, :, :], p_sum[:, k, :].rearrange("p (r d) -> p r d", r=R),
                                             bc(self_w[:, t, :].unsqueeze(2), 128, R, D), ALU.mult))
                        dve.sem_inc(s_hc[1][k], 1)
                        ch(vec.tensor_reduce(out=yb[:, t, :], in_=hs[:, :, :].rearrange("p r d -> p d r"),
                                             op=ALU.add, axis=AX.X))
                    ch(vec.tensor_tensor(ya[:, :, :], yb[:, :, :], own, ALU.add))
                    ch(vec.tensor_tensor(ya[:, :, :], ya[:, :, :], nb[:, :, 0:D], ALU.add))
                    wait_reg(dve, s_xs[u], it * 16 + 16 * (1 + NI * 5))
                    ch(vec.tensor_tensor(ya[:, :, :], ya[:, :, :], xs[:, u, :, :], ALU.add))
                    dve.sem_inc(s_xfree[5], 1)
                    layer_norm(5, b, u)


UPTO = 3


def kernel(**inputs):
    import numpy as np
    import concourse.bacc as bacc
    from concourse.bass_utils import run_bass_kernel_spmd

    nc = bacc.Bacc("TRN2", target_bir_lowering=False, num_devices=1)
    arrays = {}

    def given(name, a):
        a = np.ascontiguousarray(a)
        arrays[f"in_{name}"] = a
        return nc.dram_tensor(f"in_{name}", a.shape, mybir.dt.from_np(a.dtype), kind="ExternalInput").ap()

    i = {k: np.asarray(v) for k, v in inputs.items()}
    grouped = lambda a: a.reshape(G, P, S).transpose(1, 0, 2)
    w2 = i["L2_gnn_W"].T
    laid = {
        "ws65": np.concatenate([i["L0_gnn_W_self"].T, i["L0_gnn_bias"][None]]), "wn": i["L0_gnn_W_neigh"].T,
        "w1": i["L1_gnn_W1"], "b1": i["L1_gnn_b1"][:, None],
        "w2b": np.concatenate([i["L1_gnn_W2"], i["L1_gnn_b2"][None]]),
        "wi": w2[:D], "wj": w2[D:], "b2": i["L2_gnn_b"][None],
        "gamma": i["L2_gnn_gamma"][:, None], "beta": i["L2_gnn_beta"][:, None],
        "wself": i["L3_gnn_W_self"], "bself": i["L3_gnn_b_self"][None],
        "wcat": i["L3_gnn_W"].transpose(1, 0, 2).reshape(D, R * D),
        "wrt": i["L3_gnn_W"].transpose(2, 0, 1).reshape(D, R * D),
        "att": np.stack([i["L3_gnn_att_src"], i["L3_gnn_att_dst"]], -1).transpose(1, 0, 2).reshape(D, 2 * R),
        "rbias": i["L3_gnn_bias"].reshape(1, R * D),
    }
    args = [given("x", i["x"]), given("src_p", grouped(i["src"])), given("dst_p", grouped(i["dst"])),
            given("type_p", grouped(i["edge_type_8"])), given("weight_p", grouped(i["edge_weight"])),
            given("dst_f", i["dst"]), given("type_f", i["edge_type_8"]), given("edge_attr", i["edge_attr_64"]),
            {name: given(name, laid[name]) for name, _ in WEIGHTS}]
    out = nc.dram_tensor("out", (N, D), mybir.dt.float32, kind="ExternalOutput").ap()
    program(nc, *args, out, UPTO)
    return run_bass_kernel_spmd(nc, [arrays], core_ids=[0]).results[0]["out"]
```

```python
import concourse.bass as bass
from concourse import mybir
from contextlib import ExitStack

N, E, D, R = 12500, 200000, 64, 8
P, S = 125, 8
GE = P * S
G = E // GE
Q = 4
IT = G // Q
W = 128
NW = -(-N // W)
NP = NW * W
FW = 32
BT = 7
NB = NW // BT
BC = BT * W
HB = BC // 2
TAIL = N - (NB - 1) * BC
TAIL_TILES, TAIL_ROWS = TAIL // W, TAIL % W
HROW = 72
T = E // P
SG = 100
BIG = 1e37
EPS_LN = 1e-5

WEIGHTS = [("ws65", (65, 64)), ("wn", (64, 64)), ("w1", (64, 64)), ("b1", (64, 1)), ("w2b", (65, 64)),
           ("wi", (64, 64)), ("wj", (64, 64)), ("b2", (1, 64)), ("gamma", (64, 1)), ("beta", (64, 1)),
           ("wself", (64, 64)), ("bself", (1, 64)), ("wcat", (64, 512)), ("wrt", (64, 512)),
           ("att", (64, 16)), ("rbias", (1, 512))]


def program(nc, x, src_p, dst_p, type_p, weight_p, dst_f, type_f, edge_attr, weights, out):
    f32, i32, i16, bf16 = mybir.dt.float32, mybir.dt.int32, mybir.dt.int16, mybir.dt.bfloat16
    ALU, ACT, AX = mybir.AluOpType, mybir.ActivationFunctionType, mybir.AxisListType
    dram = lambda n, s, d=f32: nc.dram_tensor(n, s, d, kind="Internal").ap()
    x1_d, x2_d, x3_d = dram("x1_d", (NP, D)), dram("x2_d", (NP, D)), dram("x3_d", (NP, D))
    rel_d = dram("rel_d", (NP * R, HROW))
    he_d = dram("he_d", (G, P, S * HROW))
    key_d = dram("key_d", (P, G, S), i32)
    dst16_d = dram("dst16_d", (E,), i16)
    trip_d = dram("trip_d", (E * 3,))
    alpha_d = dram("alpha_d", (E,))
    run_out_d, run_in_d = dram("run_out_d", (2, P, 2 * R + 2)), dram("run_in_d", (2, P, 2 * R))

    with ExitStack() as ctx:
        sb = lambda n, s, d=f32: ctx.enter_context(nc.sbuf_tensor(n, s, d))
        ps = lambda n, s: ctx.enter_context(nc.psum_tensor(n, s, f32))
        sem = lambda n: ctx.enter_context(nc.semaphore(n))

        ident, iota = sb("ident", [128, 128]), sb("iota", [128, W])
        fine_col, node_col = sb("fine_col", [128, NP // FW]), sb("node_col", [128, NW])
        rel_col = sb("rel_col", [128, R])
        wt = {n: sb("w_" + n, list(s)) for n, s in WEIGHTS}
        wn66, wj66 = sb("wn66", [D + 2, D + 2]), sb("wj66", [D + 2, D])
        wd65, wself65 = sb("wd65", [65, D]), sb("wself65", [65, D])
        sdw, brow = sb("sdw", [D, 2 * R]), sb("brow", [1, D])
        eps_col = sb("eps_col", [128, 1])
        idx = sb("idx", [P, Q, S], i32)
        gat = sb("gat", [P, Q, S, HROW])
        ea = sb("ea", [P, Q, S, D])
        msg = sb("msg", [P, 2, S, HROW])
        oh = sb("oh", [P, 2, S, W])
        dstf, edge_w, typef = [sb(n, [P, G + 1, S]) for n in ("dstf", "edge_w", "typef")]
        trip, trip_s = sb("trip", [128, G, S, 3]), sb("trip_s", [128, T, 3])
        drow, oht = sb("drow", [128, 2, GE], i16), sb("oht", [128, S * W], bf16)
        toh, sel, sel2 = sb("toh", [P, 2, S, R]), sb("sel", [P, S, 2, 3 * R]), sb("sel2", [P, S, 2])
        ends, runs, run_in = sb("ends", [P, 2]), sb("runs", [P, 2 * R + 2]), sb("run_in", [P, 2 * R])
        sum_t = sb("sum_t", [128, NP + W - FW])
        deg = sb("deg", [128, NW])
        dtab = sb("dtab", [128, NW, 2 * R])
        win = sb("win", [1, 2, G + 1], i32)
        link_row = sb("link_row", [1, 4, P + 1])
        ends_g, ends_i = sb("ends_g", [SG, 2, 2]), sb("ends_i", [SG, 4, 2], i32)
        wcols, wrows, wones = sb("wcols", [SG, 4, 2]), sb("wrows", [1, 6, G]), sb("wones", [1, G])
        wint = sb("wint", [1, 3, G], i32)
        xs, xd = sb("xs", [128, 2, BT, D]), sb("xd", [128, 2, BT, D + 1])
        stage, xt = sb("stage", [128, 2, BC]), sb("xt", [65, 2, BC])
        ya, yb, yo = sb("ya", [128, BT, D]), sb("yb", [128, BT, D]), sb("yo", [128, 2, BT, D])
        r1, r2 = sb("r1", [128, BT]), sb("r2", [128, BT])
        sd, self_w = sb("sd", [128, BT, 2 * R]), sb("self_w", [128, BT, R])
        bn, bnm = sb("bn", [D, 25, 6]), sb("bnm", [D, 6])
        trip_flat = trip[0:P, :, :, :].rearrange("p g s c -> p (g s c)")
        scan_flat = trip_s[0:P, :, :].rearrange("p t c -> p (t c)")
        dtab3 = trip_s[:, :, :].rearrange("p t c -> p (t c)").bitcast(bf16)[:, 0:NW * 6 * R]\
            .rearrange("p (w c k r) -> p w c k r", w=NW, c=2, k=3)
        src_i, type_i, dst_i = [trip_flat.bitcast(i32)[:, k * T:(k + 1) * T] for k in range(3)]
        dstn_i = scan_flat.bitcast(i32)[:, 0:T]
        dst16 = scan_flat[:, 2 * T:2 * T + T // 2].bitcast(i16)
        stat_i = oh[0:SG, :, :, :].rearrange("p a s w -> p (a s w)")[:, 0:2 * GE].bitcast(i32)
        stat_i = stat_i.rearrange("p (a e) -> p a e", a=2)
        self_h = [flat[:, 0:BT * R * D].rearrange("p (t r d) -> p t r d", t=BT, r=R)
                  for flat in (trip[:, :, :, :].rearrange("p g s c -> p (g s c)"),
                               trip_s[:, :, :].rearrange("p t c -> p (t c)"))]
        hst = sum_t[:, 0:2 * BT * R * HROW].rearrange("p (u t r c) -> p u t r c", u=2, t=BT, r=R)
        rtype, brk_f, brk_b, lead, trail, val, fwd = [sum_t[0:P, k * T:(k + 1) * T] for k in range(7)]
        bwd, best, off = [trip_flat[:, k * T:(k + 1) * T] for k in range(3)]
        scan_dst_i, scan_type_i = fwd.bitcast(i32), rtype.bitcast(i32)
        run_row = gat[0:1, :, :, :].rearrange("a q s c -> a (q s c)")[:, 0:P * (2 * R + 2)]\
            .rearrange("a (p c) -> a p c", p=P)
        carry_row = ea[0:1, :, :, :].rearrange("a q s d -> a (q s d)")[:, 0:P * 2 * R].rearrange("a (p c) -> a p c", p=P)
        init_row = oh[0:1, :, :, :].rearrange("a u s w -> a (u s w)")[:, 0:P * 2 * R].rearrange("a (p c) -> a p c", p=P)
        score, gap, self_score, self_gap = trip_s[0:P, :, 0], trip_s[0:P, :, 1], trip_s[0:P, :, 2], off
        oht_tile = oht[:, :].rearrange("n (p s) -> n p s", s=S)
        p_sum, p_tr = ps("p_sum", [128, 2, 512]), ps("p_tr", [128, 2, 512])
        p_a, p_b = ps("p_a", [128, 2, 512]), ps("p_b", [128, 2, 512])
        p_tr_flat = p_tr[:, :, :].rearrange("p a c -> p (a c)")

        s_load = [sem(f"s_load{k}") for k in range(6)]
        s_wload, s_const, s_vconst = sem("s_wload"), sem("s_const"), sem("s_vconst")
        s_cols, s_rows, s_win = sem("s_cols"), sem("s_rows"), sem("s_win")
        s_prep, s_patch, s_sdw = sem("s_prep"), sem("s_patch"), sem("s_sdw")
        s_key, s_keyst, s_zero = sem("s_key"), sem("s_keyst"), sem("s_zero")
        s_idx = [sem(f"s_idx{q}") for q in range(Q)]
        s_gat = [sem(f"s_gat{q}") for q in range(Q)]
        s_free = [sem(f"s_free{q}") for q in range(Q)]
        s_ea = [sem(f"s_ea{q}") for q in range(Q)]
        s_hest = [sem(f"s_hest{q}") for q in range(Q)]
        s_held = [sem(f"s_held{q}") for q in range(Q)]
        s_pre, s_msg = sem("s_pre"), sem("s_msg")
        s_oh = [[sem(f"s_oh{n}_{h}") for h in range(2)] for n in range(5)]
        s_agg = [sem(f"s_agg{n}") for n in range(5)]
        s_sum = [sem(f"s_sum{n}") for n in range(5)]
        s_acc, s_scan_copy = sem("s_acc"), sem("s_scan_copy")
        s_drow = [sem(f"s_drow{u}") for u in range(2)]
        s_drused, s_trip, s_tripd = sem("s_drused"), sem("s_trip"), sem("s_tripd")
        s_rld = [sem(f"s_rld{k}") for k in range(2)]
        s_scan, s_run, s_rund = sem("s_scan"), sem("s_run"), sem("s_rund")
        s_ein, s_eout, s_alpha, s_alphad, s_alphal = [sem(n) for n in
                                                      ("s_ein", "s_eout", "s_alpha", "s_alphad", "s_alphal")]
        NS = 6
        s_tail = sem("s_tail")
        s_xs = [sem(f"s_xs{u}") for u in range(2)]
        s_xfree = [sem(f"s_xfree{n}") for n in range(NS)]
        s_tr = {n: sem(f"s_tr{n}") for n in (0, 1, 2, 4, 5)}
        s_stage = {n: sem(f"s_stage{n}") for n in (0, 1, 2, 4, 5)}
        s_mid = {n: sem(f"s_mid{n}") for n in (1, 2, 3, 5)}
        s_act = {n: sem(f"s_act{n}") for n in (1, 2, 3, 4)}
        s_mm = [sem(f"s_mm{n}") for n in range(NS)]
        s_sqrt_in, s_sqrt = [{n: sem(f"s_{k}{n}") for n in (0, 1, 3, 5)} for k in ("sqrt_in", "sqrt")]
        s_y = {n: sem(f"s_y{n}") for n in (0, 1, 3, 4, 5)}
        s_yst = [sem(f"s_yst{u}") for u in range(2)]
        s_yfree = {n: sem(f"s_yfree{n}") for n in (0, 1, 3, 4, 5)}
        s_table = sem("s_table")
        s_bn, s_bnr, s_bnc = sem("s_bn"), sem("s_bnr"), sem("s_bnc")
        s_h = [[sem(f"s_h{n}_{k}") for k in range(2)] for n in range(2)]
        s_hc = [[sem(f"s_hc{n}_{k}") for k in range(2)] for n in range(2)]
        s_more = sem("s_more")
        s_group = sem("s_group")
        s_self, s_selfsum = sem("s_self"), sem("s_selfsum")
        s_vch, s_pch = sem("s_vch"), sem("s_pch")
        s_turn = sem("s_turn")
        block = ctx.enter_context(nc.Block())

        class Chain:

            def __init__(self, eng, s):
                self.eng, self.s, self.n = eng, s, 0

            def start(self):
                self.eng.sem_clear(self.s)
                self.n = 0

            def add(self, ins):
                ins.then_inc(self.s, 1)
                self.n += 1

            def wait(self):
                self.eng.wait_ge(self.s, self.n)

            def __call__(self, ins):
                self.add(ins)
                self.wait()

        def wait_reg(eng, s, v):
            eng.wait_ge(s, v)
            eng.sem_inc(s_turn, 1)

        def group_windows(eng, table, g):
            v = eng.value_load(win[0:1, table, bass.ds(g, 1)], min_val=0, max_val=(NW * G << 16) - 1)
            return eng.snap((v >> 7) & 511), eng.snap((v & 127) + 1), eng.snap(v >> 16)

        def within(v, most):
            return nc.s_assert_within(v, 0, most, skip_runtime_bounds_check_because=(
                "a group's last window holds its largest dst, which is below N"))

        def two_step(eng, first, second):
            def snap(v):
                return v if isinstance(v, int) else eng.snap(v)

            first(0, 0, 0)
            with eng.Fori(0, NI - 1) as it:
                first(it, 1, snap(it * 2 + 1))
                second(it, 0, snap(it * 2))
                first(snap(it + 1), 0, snap(it * 2 + 2))
                second(it, 1, snap(it * 2 + 1))
            first(NI - 1, 1, NB - 1)
            for u in range(2):
                second(NI - 1, u, NB - 2 + u)

        def rows(table, b):
            return table[bass.ds(b * BC, BC), :].rearrange("(t p) d -> p t d", p=W)

        def of_group(buf, g):
            return buf[:, bass.ds(g, 1), :].rearrange("p a s -> p (a s)")

        def bc(ap, *shape):
            return ap.to_broadcast(list(shape))

        def by_tile(ap, width):
            return bc(ap.unsqueeze(2), P, S, width)

        def nodes(b, width=BC, at=0):
            return bass.ds(b * BC + at, width)

        X = [x, x1_d, x2_d, x2_d, x3_d, x3_d]
        Y = {0: x1_d, 1: x2_d, 3: x3_d, 5: out}
        NI = NB // 2
        stored = {0: 0, 1: 1, 3: 2, 4: 3, 5: 4}

        @block.sync
        def _(sp):
            flat = "p g s -> p (g s)"
            sp.dma_start(stat_i, dst_f.rearrange("(a g e) -> g a e", a=2, g=SG)).then_inc(s_load[0], 16)
            sp.dma_start(dst_i, dst_p.rearrange(flat)).then_inc(s_load[1], 16)
            sp.dma_start(edge_w[:, 0:G, :].rearrange(flat), weight_p.rearrange(flat)).then_inc(s_load[2], 16)
            for q in range(Q):
                sp.dma_start(idx[:, q, :], src_p[:, q, :]).then_inc(s_idx[q], 16)
            sp.dma_start(src_i, src_p.rearrange(flat)).then_inc(s_load[3], 16)
            sp.dma_start(type_i, type_p.rearrange(flat)).then_inc(s_load[4], 16)
            sp.dma_start(dstn_i, dst_f.rearrange("(p t) -> p t", p=P)).then_inc(s_load[5], 16)
            for name, _ in WEIGHTS:
                sp.dma_start(wt[name][:, :], weights[name]).then_inc(s_wload, 16)
            sp.wait_ge(s_prep, 1)
            sp.dma_start(wn66[0:D, 0:D], weights["wn"]).then_inc(s_patch, 16)
            sp.dma_start(wself65[D:D + 1, :], brow[0:1, :]).then_inc(s_patch, 16)
            sp.dma_start(wself65[0:D, :], weights["wself"]).then_inc(s_patch, 16)
            sp.dma_start(wd65[D:D + 1, :], weights["b2"]).then_inc(s_patch, 16)
            sp.wait_ge(s_key, 1)
            sp.dma_start(key_d.rearrange(flat), src_i).then_inc(s_keyst, 16)
            sp.dma_start(dst16_d.rearrange("(p t) -> p t", p=P), dst16).then_inc(s_keyst, 16)

            def refill(n, q, it, source):
                wait_reg(sp, s_free[q], it + (2 + IT * n))
                sp.dma_start(idx[:, q, :], source[:, bass.ds(it * Q + (Q + q), 1), :]
                             .rearrange("p a s -> p (a s)")).then_inc(s_idx[q], 16)

            def first_indices(n, source):
                for q in range(Q):
                    sp.wait_ge(s_free[q], IT * n + 1)
                    sp.dma_start(idx[:, q, :], source[:, q, :]).then_inc(s_idx[q], 16)

            def dense_io(n):
                r0 = (NB - 1) * BC

                def load(u, b):
                    sp.dma_start(xs[:, u, :, :], rows(X[n], b)).then_inc(s_xs[u], 16)

                def load_last():
                    if X[n] is not x:
                        return load(1, NB - 1)
                    sp.dma_start(xs[0:TAIL_ROWS, 1, TAIL_TILES, :], x[r0 + TAIL_TILES * W:N, :])\
                        .then_inc(s_tail, 16)
                    sp.wait_ge(s_tail, 16)
                    sp.dma_start(xs[:, 1, 0:TAIL_TILES, :], x[r0:r0 + TAIL_TILES * W, :]
                                 .rearrange("(t p) d -> p t d", p=W)).then_inc(s_xs[1], 16)

                def store(u, it, b):
                    if n in Y:
                        sp.dma_start(rows(Y[n], b), yo[:, u, :, :]).then_inc(s_yst[u], 16)
                    elif n == 4:
                        sp.dma_start(rel_d[bass.ds(b * BC * R, BC * R), :]
                                     .rearrange("(t p r) c -> p t (r c)", p=W, r=R),
                                     hst[:, u, :, :, :].rearrange("p t r c -> p t (r c)")).then_inc(s_yst[u], 16)

                def store_last():
                    if Y.get(n) is not out:
                        return store(1, NI - 1, NB - 1)
                    sp.dma_start(out[r0:r0 + TAIL_TILES * W, :].rearrange("(t p) d -> p t d", p=W),
                                 yo[:, 1, 0:TAIL_TILES, :]).then_inc(s_yst[1], 16)
                    sp.dma_start(out[r0 + TAIL_TILES * W:N, :], yo[0:TAIL_ROWS, 1, TAIL_TILES, :])\
                        .then_inc(s_tail, 16)

                def turn(it, final):
                    for u in range(2):
                        b = it * 2 + u
                        if n != 2:
                            wait_reg(sp, s_y[n], b + 1)
                            if n == 4:
                                wait_reg(sp, s_act[n], b + 1)
                            store(u, it, b)
                        wait_reg(sp, s_xfree[n], b + 3)
                        if final and u == 1:
                            load_last()
                        else:
                            load(u, b + 2)
                        if n != 2:
                            wait_reg(sp, s_yst[u], it * 16 + 16 * (1 + NI * stored[n]))
                            sp.sem_inc(s_yfree[n], 1)

                if n:
                    sp.wait_ge(s_xfree[n - 1], NB + 2)
                for u in range(2):
                    load(u, u)
                with sp.Fori(0, NI - 2) as it:
                    turn(it, False)
                turn(NI - 2, True)
                if n == 2:
                    return
                for b in (NB - 2, NB - 1):
                    sp.wait_ge(s_y[n], b + 1)
                    if n == 4:
                        sp.wait_ge(s_act[n], b + 1)
                    if b == NB - 2:
                        store(0, NI - 1, b)
                    else:
                        store_last()
                for u in range(2):
                    sp.wait_ge(s_yst[u], 16 * NI * (1 + stored[n]))
                if n == 5:
                    sp.wait_ge(s_tail, 32)
                sp.sem_inc(s_table, 1)

            with sp.Fori(0, IT - 1) as it:
                for q in range(Q):
                    refill(0, q, it, src_p)
            sp.wait_ge(s_keyst, 32)
            dense_io(0)
            first_indices(1, src_p)
            ea_d = edge_attr.rearrange("(g p s) d -> g p (s d)", p=P, s=S)
            ea_slot = [ea[:, q, :, :].rearrange("p s d -> p (s d)") for q in range(Q)]
            for q in range(Q):
                sp.dma_start(ea_slot[q], ea_d[q, :, :]).then_inc(s_ea[q], 16)
            with sp.Fori(0, IT - 1) as it:
                for q in range(Q):
                    refill(1, q, it, src_p)
                    sp.dma_start(ea_slot[q], ea_d[bass.ds(it * Q + (Q + q), 1), :, :]
                                 .rearrange("a p e -> (a p) e")).then_inc(s_ea[q], 16)
            dense_io(1)
            first_indices(2, src_p)
            with sp.Fori(0, IT - 1) as it:
                for q in range(Q):
                    refill(2, q, it, src_p)
            dense_io(2)
            dense_io(3)
            dense_io(4)
            first_indices(3, key_d)

            def dst_row(u, g):
                sp.dma_start(drow[:, u, :], dst16_d[bass.ds(g * GE, GE)].unsqueeze(0).to_broadcast([128, GE]))\
                    .then_inc(s_drow[u], 16)

            for u in range(2):
                dst_row(u, u)
            sp.dma_start(scan_dst_i, dst_f.rearrange("(p t) -> p t", p=P)).then_inc(s_rld[0], 16)
            sp.dma_start(scan_type_i, type_f.rearrange("(p t) -> p t", p=P)).then_inc(s_rld[1], 16)

            def pass3(it, final):
                for q in range(Q):
                    if not (final and q >= Q - 2):
                        wait_reg(sp, s_drused, it * Q + (q + 1))
                        dst_row(q % 2, it * Q + (q + 2))
                    if not final:
                        refill(3, q, it, key_d)

            with sp.Fori(0, IT - 1) as it:
                pass3(it, False)
            pass3(IT - 1, True)
            sp.wait_ge(s_trip, 2)
            sp.dma_start(trip_d.rearrange("(g p e) -> p g e", g=G, p=P),
                         trip[0:P, :, :, :].rearrange("p g s c -> p g (s c)")).then_inc(s_tripd, 16)
            sp.wait_ge(s_tripd, 16)
            sp.dma_start(scan_flat, trip_d.rearrange("(p e) -> p e", p=P)).then_inc(s_scan, 16)
            for k in range(2):
                sp.wait_ge(s_run, 2 * k + 1)
                sp.dma_start(run_out_d[k, :, :], runs[:, :]).then_inc(s_rund, 16)
                sp.wait_ge(s_rund, 64 * k + 16)
                sp.dma_start(run_row.rearrange("a p c -> a (p c)"),
                             run_out_d[k:k + 1, :, :].rearrange("a p c -> a (p c)")).then_inc(s_rund, 16)
                sp.wait_ge(s_run, 2 * k + 2)
                sp.dma_start(run_in_d[k:k + 1, :, :].rearrange("a p c -> a (p c)"),
                             init_row.rearrange("a p c -> a (p c)")).then_inc(s_rund, 16)
                sp.wait_ge(s_rund, 64 * k + 48)
                sp.dma_start(run_in[:, :], run_in_d[k, :, :]).then_inc(s_rund, 16)
            sp.wait_ge(s_alpha, 1)
            sp.dma_start(alpha_d.rearrange("(p t) -> p t", p=P), val).then_inc(s_alphad, 16)
            sp.wait_ge(s_alphad, 16)
            sp.dma_start(edge_w[:, 0:G, :], alpha_d.rearrange("(g p s) -> p g s", g=G, p=P)).then_inc(s_alphal, 16)
            he_slot = [gat[:, q, :, :].rearrange("p s c -> p (s c)") for q in range(Q)]
            for q in range(Q):
                sp.dma_start(he_slot[q], he_d[q, :, :]).then_inc(s_held[q], 16)
            with sp.Fori(0, IT - 1) as it:
                for q in range(Q):
                    wait_reg(sp, s_free[q], it + (2 + 4 * IT))
                    sp.dma_start(he_slot[q], he_d[bass.ds(it * Q + (Q + q), 1), :, :]
                                 .rearrange("a p e -> (a p) e")).then_inc(s_held[q], 16)
            dense_io(5)

        @block.gpsimd
        def _(pool):
            nc.gpsimd.memset(ident[:, :], 0.0).then_inc(s_const, 1)
            pool.wait_ge(s_const, 1)
            exact = dict(allow_small_or_imprecise_dtypes=True)
            nc.gpsimd.affine_select(out=ident[:, :], in_=ident[:, :], compare_op=ALU.not_equal, fill=1.0, base=0,
                                    pattern=[[-1, 128]], channel_multiplier=1).then_inc(s_const, 1)
            nc.gpsimd.iota(iota[:, :], pattern=[[1, W]], base=0, channel_multiplier=0, **exact).then_inc(s_const, 1)
            nc.gpsimd.iota(fine_col[:, :], pattern=[[FW, NP // FW]], base=0, channel_multiplier=0, **exact)\
                .then_inc(s_const, 1)
            nc.gpsimd.iota(node_col[:, :], pattern=[[W, NW]], base=0, channel_multiplier=1, **exact)\
                .then_inc(s_const, 1)
            nc.gpsimd.iota(rel_col[:, :], pattern=[[1, R]], base=0, channel_multiplier=0, **exact).then_inc(s_const, 1)

            def gather_pass(n, table, width):
                with pool.Fori(0, IT) as it:
                    for q in range(Q):
                        wait_reg(pool, s_idx[q], it * 16 + 16 * (1 + IT * n))
                        wait_reg(pool, s_free[q], it + (1 + IT * n))
                        for s in range(S):
                            nc.gpsimd.indirect_dma_start(
                                out=gat[:, q, s, 0:width], out_offset=None, in_=table,
                                in_offset=bass.IndirectOffsetOnAxis(ap=idx[:, q, s:s + 1], axis=0),
                            ).then_inc(s_gat[q], 16)

            gather_pass(0, x, D)
            for n, table in ((1, x1_d), (2, x2_d)):
                pool.wait_ge(s_table, n)
                gather_pass(n, table, D)
            pool.wait_ge(s_table, 4)
            pool.wait_ge(s_keyst, 32)
            gather_pass(3, rel_d, HROW)
            pool.wait_ge(s_alphal, 16)
            with pool.Fori(0, IT) as it:
                for q in range(Q):
                    g = it * Q + q
                    alpha = of_group(edge_w, g)
                    wait_reg(pool, s_group, it * Q + (q + 1))
                    wait_reg(pool, s_held[q], it * 16 + 16)
                    nc.gpsimd.tensor_tensor(msg[:, q % 2, :, 0:D], gat[:, q, :, 0:D], by_tile(alpha, D), ALU.mult)
                    wait_reg(pool, s_oh[4][0], it * Q + (q + 1))
                    nc.gpsimd.tensor_tensor(msg[:, q % 2, :, D:HROW], toh[:, q % 2, :, :], by_tile(alpha, R), ALU.mult)\
                        .then_inc(s_msg, 1)
                    wait_reg(pool, s_msg, it * Q + (2 * G + q + 1))
                    pool.sem_inc(s_free[q], 1)
            with pool.Fori(0, NI) as it:
                for u in range(2):
                    wait_reg(pool, s_self, it * 2 + (u + 1))
                    width = R * D // 2
                    v = self_h[u].rearrange("p t r d -> p t (r d)")
                    for step in range(3):
                        nc.gpsimd.tensor_tensor(v[:, :, 0:width], v[:, :, 0:width], v[:, :, width:2 * width], ALU.add)\
                            .then_inc(s_pch, 1)
                        wait_reg(pool, s_pch, it * 6 + (u * 3 + step + 1))
                        width //= 2
                    pool.sem_inc(s_selfsum, 1)

        @block.scalar
        def _(act):
            def square_root(n, b, k, per):
                wait_reg(act, s_sqrt_in[n], b * per + (k + 1))
                if k == per - 1:
                    nc.scalar.activation(r2[:, :], r2[:, :], ACT.Sqrt, bias=eps_col[:, 0:1], scale=1.0 / D)\
                        .then_inc(s_sqrt[n], 1)
                else:
                    nc.scalar.activation(r1[:, :], r1[:, :], ACT.Sqrt).then_inc(s_sqrt[n], 1)

            act.wait_ge(s_vconst, 2)
            act.wait_ge(s_sum[0], 1)
            def stage_in(n, width):
                def copies(it, u, b):
                    wait_reg(act, s_mm[n], b + 1)
                    nc.scalar.activation(stage[0:width, u, :], sum_t[0:width, nodes(b)], ACT.Copy)
                    wait_reg(act, s_tr[n], b + 1)
                    nc.scalar.activation(xt[0:D, u, :], p_tr_flat[0:D, 0:BC], ACT.Copy).then_inc(s_stage[n], 1)
                return copies

            def roots(n, per):
                def take(it, u, b):
                    for k in range(per):
                        square_root(n, b, k, per)
                return take

            two_step(act, stage_in(0, D + 2), roots(0, 2))
            with act.Fori(0, IT) as it:
                for q in range(Q):
                    wait_reg(act, s_pre, it * Q + (q + 1))
                    nc.scalar.activation(msg[:, q % 2, :, 0:D], ea[:, q, :, :], ACT.Relu).then_inc(s_msg, 1)
                    wait_reg(act, s_msg, it * Q + (G + q + 1))
                    act.sem_inc(s_free[q], 1)
            def hidden(it, u, b):
                wait_reg(act, s_mid[1], b + 1)
                for h, bank in ((0, p_a), (1, p_b)):
                    ins = nc.scalar.activation(xt[0:D, u, h * HB:(h + 1) * HB], bank[0:D, u, 0:HB], ACT.Relu,
                                               bias=wt["b1"][:, 0:1])
                ins.then_inc(s_act[1], 1)

            two_step(act, hidden, roots(1, 1))
            with act.Fori(0, NI) as it:
                for u in range(2):
                    b = act.snap(it * 2 + u)
                    wait_reg(act, s_mm[2], b + 1)
                    wait_reg(act, s_tr[2], b + 3)
                    nc.scalar.activation(stage[0:D + 1, u, :], p_tr_flat[0:D + 1, 0:BC], ACT.Copy)\
                        .then_inc(s_stage[2], 1)
            act.wait_ge(s_bn, 1)
            nc.scalar.activation(bnm[:, 2:3], bnm[:, 1:2], ACT.Sqrt, bias=eps_col[0:D, 0:1]).then_inc(s_bnr, 1)
            act.wait_ge(s_bnc, 1)
            def scale_shift(it, u, b):
                wait_reg(act, s_mid[3], b + 1)
                nc.scalar.activation(stage[0:D, u, :], sum_t[0:D, nodes(b)], ACT.Identity,
                                     bias=bnm[:, 4:5], scale=bnm[:, 3:4]).then_inc(s_act[3], 1)

            two_step(act, scale_shift, roots(3, 1))
            act.wait_ge(s_zero, 1)
            with act.Fori(0, NI) as it:
                for u in range(2):
                    b = act.snap(it * 2 + u)
                    wait_reg(act, s_mm[4], b + 1)
                    wait_reg(act, s_tr[4], b + 1)
                    nc.scalar.activation(xt[0:D, u, :], p_tr_flat[0:D, 0:BC], ACT.Copy).then_inc(s_stage[4], 1)
                    wait_reg(act, s_yfree[4], b + 1)
                    for t in range(u, BT, 2):
                        m = (BT * u + t) // 2
                        wait_reg(act, s_h[0][0], it * BT + (m + 1))
                        nc.scalar.activation(hst[:, u, t, :, 0:D],
                                             p_a[:, 0, :].rearrange("p (r d) -> p r d", r=R), ACT.Copy)\
                            .then_inc(s_hc[0][0], 1)
                    wait_reg(act, s_hc[0][0], it * BT + (m + 2))
                    act.sem_inc(s_act[4], 1)
            act.wait_ge(s_zero, 2)

            def free_slot(q, it):
                wait_reg(act, s_scan_copy, it * Q + (q + 1))
                wait_reg(act, s_hest[q], it * 16 + 16)
                act.sem_inc(s_free[q], 1)

            with act.Fori(0, IT) as it:
                for q in range(Q):
                    wait_reg(act, s_gat[q], it * 128 + 128 * (1 + 3 * IT))
                    act.dma_start(he_d[bass.ds(it * Q + q, 1), :, :].rearrange("a p e -> (a p) e"),
                                  gat[:, q, :, :].rearrange("p s c -> p (s c)")).then_inc(s_hest[q], 16)
                    nc.scalar.activation(trip[0:P, bass.ds(it * Q + q, 1), :, 0].rearrange("p a s -> p (a s)"),
                                         gat[:, q, :, D], ACT.Copy).then_inc(s_scan_copy, 1)
                    if q:
                        free_slot(q - 1, it)
                free_slot(Q - 1, it)
            act.wait_ge(s_scan_copy, G)
            act.sem_inc(s_trip, 1)
            for k, (dst, srcv) in enumerate(((score, gap), (self_score, self_gap))):
                act.wait_ge(s_ein, k + 1)
                nc.scalar.activation(dst, srcv, ACT.Exp).then_inc(s_eout, 1)
            act.wait_ge(s_sum[4], 1)
            two_step(act, stage_in(5, HROW), roots(5, 1))

        @block.tensor
        def _(pe):
            pe.wait_ge(s_const, 2)
            pe.wait_ge(s_cols, 1)
            for c in range(4):
                for a in range(2):
                    at = (c % 2) * G + a * SG
                    ins = nc.tensor.matmul(p_a[0:1, c // 2, at:at + SG], wcols[:, c, a:a + 1], ident[0:SG, 0:SG],
                                           start=True, stop=True)
            ins.then_inc(s_rows, 1)
            pe.wait_ge(s_wload, 16 * len(WEIGHTS))
            for r in range(R):
                ins = nc.tensor.matmul(p_b[0:D, 0, 2 * r:2 * r + 2], wt["wrt"][:, r * D:(r + 1) * D],
                                       wt["att"][:, 2 * r:2 * r + 2], start=True, stop=True)
            ins.then_inc(s_sdw, 1)
            pe.wait_ge(s_win, 1)
            pe.wait_ge(s_patch, 64)

            def sum_pass(n, width, ready, lhs):
                with pe.Fori(0, IT) as it:
                    for q in range(Q):
                        _, cnt, cum = group_windows(pe, 0, it * Q + q)
                        ready(it, q)
                        with pe.Fori(0, cnt) as k:
                            for s in range(S):
                                if s % (S // 2) == 0:
                                    pe.wait_ge(s_oh[n][s // (S // 2)], cum + k + 1)
                                ins = nc.tensor.matmul(p_sum[0:width, 0, 0:W], lhs(q, s), oh[:, 0, s, :],
                                                       start=(s == 0), stop=(s == S - 1))
                            ins.then_inc(s_agg[n], 1)

            def transposes(n, width, src):
                for t in range(BT):
                    ins = nc.tensor.transpose(p_tr[0:width, t // 4, (t % 4) * W:(t % 4 + 1) * W], src(t), ident[:, :])
                ins.then_inc(s_tr[n], 1)

            def tile(buf, u, t, k):
                return buf[0:k, u, t * W:(t + 1) * W]

            sum_pass(0, D + 2, lambda it, q: wait_reg(pe, s_msg, it * Q + (q + 1)), lambda q, s: msg[:, q % 2, s, 0:D + 2])
            with pe.Fori(0, NI) as it:
                for u in range(2):
                    b = pe.snap(it * 2 + u)
                    wait_reg(pe, s_xs[u], it * 16 + 16 * (1 + NI * 0))
                    wait_reg(pe, s_stage[0], b + 1)
                    transposes(0, D, lambda t: xs[:, u, t, :])
                    wait_reg(pe, s_stage[0], b + 2)
                    wait_reg(pe, s_xfree[0], b + 1)
                    for t in range(BT):
                        nc.tensor.matmul(p_a[:, u, t * D:(t + 1) * D], tile(xt, u, t, D + 1), wt["ws65"][:, :],
                                         start=True, stop=True)
                        ins = nc.tensor.matmul(p_b[:, u, t * 66:(t + 1) * 66], tile(stage, u, t, 66), wn66[:, :],
                                               start=True, stop=True)
                    ins.then_inc(s_mm[0], 1)
            sum_pass(1, D, lambda it, q: wait_reg(pe, s_msg, it * Q + (G + q + 1)), lambda q, s: msg[:, q % 2, s, 0:D])
            def layer1(it, u, b):
                wait_reg(pe, s_xs[u], it * 16 + 16 * (1 + NI * 1))
                wait_reg(pe, s_stage[1], b + 1)
                transposes(1, D, lambda t: xs[:, u, t, :])
                wait_reg(pe, s_stage[1], b + 2)
                wait_reg(pe, s_xfree[1], b + 1)
                for h, bank in ((0, p_a), (1, p_b)):
                    ins = nc.tensor.matmul(bank[0:D, u, 0:HB], wt["w1"][:, :],
                                           stage[0:D, u, h * HB:(h + 1) * HB], start=True, stop=True)
                ins.then_inc(s_mid[1], 1)

            def layer2(it, u, b):
                wait_reg(pe, s_act[1], b + 1)
                for t in range(BT):
                    ins = nc.tensor.matmul(p_a[:, u, t * D:(t + 1) * D], tile(xt, u, t, D + 1),
                                           wt["w2b"][:, :], start=True, stop=True)
                ins.then_inc(s_mm[1], 1)

            two_step(pe, layer1, layer2)
            sum_pass(2, D, lambda it, q: wait_reg(pe, s_gat[q], it * 128 + 128 * (1 + 2 * IT)),
                     lambda q, s: gat[:, q, s, 0:D])
            pe.wait_ge(s_sum[2], 1)
            with pe.Fori(0, NI) as it:
                for u in range(2):
                    b = pe.snap(it * 2 + u)
                    wait_reg(pe, s_act[2], b + 1)
                    wait_reg(pe, s_stage[2], b + 1)
                    transposes(2, D + 1, lambda t: xd[:, u, t, :])
                    wait_reg(pe, s_stage[2], b + 2)
                    wait_reg(pe, s_mid[2], b + 1)
                    for h, bank in ((0, p_a), (1, p_b)):
                        nc.tensor.matmul(bank[0:D, u, 0:HB], wd65[:, :], stage[0:D + 1, u, h * HB:(h + 1) * HB],
                                         start=True, stop=False)
                        ins = nc.tensor.matmul(bank[0:D, u, 0:HB], wj66[:, :], sum_t[0:D + 2, nodes(b, HB, h * HB)],
                                               start=False, stop=True)
                    ins.then_inc(s_mm[2], 1)
            with pe.Fori(0, NI) as it:
                for u in range(2):
                    b = pe.snap(it * 2 + u)
                    wait_reg(pe, s_mid[3], b + 3)
                    wait_reg(pe, s_xfree[3], b + 1)
                    for t in range(BT):
                        ins = nc.tensor.transpose(p_b[:, u, t * D:(t + 1) * D], tile(xt, u, t, D), ident[0:D, 0:D])
                    ins.then_inc(s_mm[3], 1)
            with pe.Fori(0, NI) as it:
                for u in range(2):
                    b = pe.snap(it * 2 + u)
                    wait_reg(pe, s_xs[u], it * 16 + 16 * (1 + NI * 4))
                    wait_reg(pe, s_stage[4], b + 1)
                    transposes(4, D, lambda t: xs[:, u, t, :])
                    wait_reg(pe, s_stage[4], b + 2)
                    wait_reg(pe, s_xfree[4], b + 1)
                    for t in range(BT):
                        nc.tensor.matmul(p_sum[:, u, t * 16:(t + 1) * 16], tile(xt, u, t, D), sdw[:, :],
                                         start=True, stop=True)
                    for t in range(BT):
                        k, m = (BT * u + t) % 2, (BT * u + t) // 2
                        wait_reg(pe, s_hc[0][k], it * BT + (m + 1))
                        ins = nc.tensor.matmul(p_a[:, k, :], tile(xt, u, t, D), wt["wcat"][:, :],
                                               start=True, stop=True)
                        ins.then_inc(s_h[0][k], 1)
                    wait_reg(pe, s_h[0][k], it * BT + (m + 1))
                    pe.sem_inc(s_mm[4], 1)
            with pe.Fori(0, IT) as it:
                for q in range(Q):
                    first, cnt, cum = group_windows(pe, 1, it * Q + q)
                    with pe.Fori(0, cnt) as k:
                        wait_reg(pe, s_oh[3][0], cum + k + 1)
                        w = within(first + k, NW - 1)
                        table = dtab3[:, bass.ds(w, 1), :, :, :].rearrange("p a c k r -> p (a c k r)")
                        for s in range(S):
                            ins = nc.tensor.matmul(p_sum[:, 0, s * 6 * R:(s + 1) * 6 * R], oht_tile[:, :, s], table,
                                                   start=True, stop=True)
                        ins.then_inc(s_agg[3], 1)
            with pe.Fori(0, IT) as it:
                for q in range(Q):
                    u = q % 2

                    def window(ready):
                        for s in range(S):
                            if s % (S // 2) == 0:
                                ready(s // (S // 2))
                            ins = nc.tensor.matmul(p_sum[0:HROW, u, 0:W], msg[:, u, s, :], oh[:, u, s, :],
                                                   start=(s == 0), stop=(s == S - 1))
                        ins.then_inc(s_agg[4], 1)

                    _, cnt, cum = group_windows(pe, 0, it * Q + q)
                    wait_reg(pe, s_msg, it * Q + (2 * G + q + 1))
                    window(lambda h: wait_reg(pe, s_oh[4][h], it * Q + (q + 1)))
                    with pe.If(cnt > 1):
                        with pe.Fori(1, cnt) as k:
                            window(lambda h: None if h else wait_reg(pe, s_more, cum + k + 1))
            with pe.Fori(0, NI) as it:
                for u in range(2):
                    b = pe.snap(it * 2 + u)
                    wait_reg(pe, s_xs[u], it * 16 + 16 * (1 + NI * 5))
                    wait_reg(pe, s_stage[5], b + 1)
                    transposes(5, D, lambda t: xs[:, u, t, :])
                    wait_reg(pe, s_stage[5], b + 2)
                    wait_reg(pe, s_xfree[5], b + 1)
                    for t in range(BT):
                        nc.tensor.matmul(p_a[:, u, t * D:(t + 1) * D], tile(xt, u, t, D + 1), wself65[:, :],
                                         start=True, stop=True)
                        ins = nc.tensor.matmul(p_b[:, u, t * HROW:(t + 1) * HROW], tile(stage, u, t, HROW),
                                               ident[0:HROW, 0:HROW], start=True, stop=True)
                    ins.then_inc(s_mid[5], 1)
                    for t in range(BT):
                        k, m = (BT * u + t) % 2, (BT * u + t) // 2
                        wait_reg(pe, s_hc[1][k], it * BT + (m + 1))
                        ins = nc.tensor.matmul(p_sum[:, k, :], tile(xt, u, t, D), wt["wcat"][:, :],
                                               start=True, stop=True)
                        ins.then_inc(s_h[1][k], 1)
                    wait_reg(pe, s_h[1][k], it * BT + (m + 1))
                    pe.sem_inc(s_mm[5], 1)

        @block.vector
        def _(dve):
            ch = Chain(dve, s_vch)
            vec = nc.vector

            for q in range(Q):
                dve.sem_inc(s_free[q], 1)
            for group, credit in ((s_xfree, 2), (s_mm, 2), (s_stage.values(), 1), (s_yfree.values(), 2)):
                for s in group:
                    dve.sem_inc(s, credit)
            for s in (s_tr[2], s_mid[2], s_mid[3]):
                dve.sem_inc(s, 2)
            for n in range(2):
                for k in range(2):
                    dve.sem_inc(s_hc[n][k], 1)
            vec.memset(eps_col[:, :], EPS_LN)
            vec.memset(wones[:, :], 1.0)
            vec.memset(xt[D:D + 1, :, :], 1.0)
            vec.memset(msg[:, :, :, D + 1], 1.0).then_inc(s_vconst, 1)
            vec.memset(xs[:, :, :, :], 0.0).then_inc(s_vconst, 1)

            ch.start()
            dve.wait_ge(s_load[0], 16)
            ch.add(vec.tensor_reduce(out=ends_g[:, 0, :], in_=stat_i, op=ALU.min, axis=AX.X))
            ch(vec.tensor_reduce(out=ends_g[:, 1, :], in_=stat_i, op=ALU.max, axis=AX.X))
            ch(vec.tensor_copy(ends_i[:, 0:2, :], ends_g[:, :, :]))
            for table, shift in ((0, 5), (1, 7)):
                lo, steps = ends_i[:, 2, :], ends_i[:, 3, :]
                ch(vec.tensor_single_scalar(lo, ends_i[:, 0, :], shift, op=ALU.arith_shift_right))
                ch(vec.tensor_copy(wcols[:, 2 * table, :], lo))
                ch(vec.scalar_tensor_tensor(out=steps, in0=wcols[:, 2 * table, :], scalar=-float(1 << shift),
                                            in1=ends_g[:, 1, :], op0=ALU.mult, op1=ALU.add))
                ch(vec.tensor_single_scalar(steps, steps, 7, op=ALU.arith_shift_right))
                ch(vec.tensor_copy(wcols[:, 2 * table + 1, :], steps))
            dve.sem_inc(s_cols, 1)
            dve.wait_ge(s_load[1], 16)
            vec.memset(dstf[:, G, :], 0.0)
            vec.memset(win[:, :, G], 0)
            vec.tensor_copy(dstf[:, 0:G, :].rearrange("p g s -> p (g s)"), dst_i)
            dve.wait_ge(s_rows, 1)
            ch(vec.tensor_copy(wrows[:, 0:2, :], p_a[0:1, 0, 0:2 * G].rearrange("a (c g) -> a c g", c=2)))
            ch(vec.tensor_copy(wrows[:, 2:4, :], p_a[0:1, 1, 0:2 * G].rearrange("a (c g) -> a c g", c=2)))
            for table in range(2):
                first, more, before, upto_g = (wrows[:, 2 * table, :], wrows[:, 2 * table + 1, :],
                                               wrows[:, 4, :], wrows[:, 5, :])
                ch(vec.tensor_scalar_add(upto_g, more, 1.0))
                ch(vec.tensor_tensor_scan(before, wones[:, :], upto_g, 0.0, ALU.mult, ALU.add))
                ch(vec.tensor_tensor(before, before, upto_g, ALU.subtract))
                for c, rowv in enumerate((first, more, before)):
                    ch.add(vec.tensor_copy(wint[:, c, :], rowv))
                ch.wait()
                ch(vec.tensor_single_scalar(wint[:, 0, :], wint[:, 0, :], 7, op=ALU.logical_shift_left))
                ch(vec.tensor_single_scalar(wint[:, 2, :], wint[:, 2, :], 16, op=ALU.logical_shift_left))
                ch(vec.tensor_tensor(wint[:, 0, :], wint[:, 0, :], wint[:, 1, :], ALU.bitwise_or))
                ch(vec.tensor_tensor(win[:, table, 0:G], wint[:, 0, :], wint[:, 2, :], ALU.bitwise_or))
            dve.sem_inc(s_win, 1)

            dve.wait_ge(s_const, 6)
            dve.wait_ge(s_wload, 16 * len(WEIGHTS))
            ch.add(vec.tensor_copy(wn66[:, :], ident[0:D + 2, 0:D + 2]))
            ch(vec.memset(wj66[:, :], 0.0))
            ch.add(vec.tensor_copy(wj66[0:D, :], wt["wj"][:, :]))
            ch.add(vec.tensor_tensor(wd65[0:D, :], wt["wi"][:, :], wt["wj"][:, :], ALU.subtract))
            ch(vec.tensor_reduce(out=brow[0:1, :], in_=wt["rbias"][0:1, :].rearrange("a (r d) -> a d r", r=R),
                                 op=ALU.add, axis=AX.X))
            ch(vec.tensor_tensor(brow[0:1, :], brow[0:1, :], wt["bself"][0:1, :], ALU.add))
            dve.sem_inc(s_prep, 1)
            dve.wait_ge(s_sdw, 1)
            ch(vec.tensor_copy(sdw[:, :].rearrange("d (c r) -> d c r", c=2),
                               p_b[0:D, 0, 0:2 * R].rearrange("d (r c) -> d c r", c=2)))
            dve.wait_ge(s_load[3], 16)
            dve.wait_ge(s_load[4], 16)
            dve.wait_ge(s_load[5], 16)
            vec.memset(typef[:, G, :], 0.0)
            ch.add(vec.tensor_copy(typef[:, 0:G, :].rearrange("p g s -> p (g s)"), type_i))
            ch.add(vec.scalar_tensor_tensor(out=src_i, in0=src_i, scalar=float(R), in1=type_i, op0=ALU.mult, op1=ALU.add))
            ch(vec.tensor_copy(dst16, dstn_i))
            dve.sem_inc(s_key, 1)

            def sum_windows(n, width, g, first, cnt, cum):
                with dve.Fori(0, cnt) as k:
                    at = dve.snap(within(first + k * (W // FW), (N - 1) // FW))
                    half = S // 2
                    for h in range(2):
                        dst = dstf[:, bass.ds(g, 1), h * half:(h + 1) * half].rearrange("p a s -> p (a s)")
                        vec.scalar_tensor_tensor(
                            out=oh[:, 0, h * half:(h + 1) * half, :], in0=bc(dst.unsqueeze(2), P, half, W),
                            scalar=fine_col[0:P, bass.ds(at, 1)], in1=bc(iota[0:P, :].unsqueeze(1), P, half, W),
                            op0=ALU.subtract, op1=ALU.is_equal).then_inc(s_oh[n][h], 1)
                    wait_reg(dve, s_agg[n], cum + k + 1)
                    part = sum_t[0:width, bass.ds(at * FW, W)]
                    vec.tensor_tensor(part, part, p_sum[0:width, 0, 0:W], ALU.add).then_inc(s_acc, 1)

            def piped_pass(width):
                half = S // 2

                def one_hot(u, g, at, h, dones):
                    dst = dstf[:, bass.ds(g, 1), h * half:(h + 1) * half].rearrange("p a s -> p (a s)")
                    ins = vec.scalar_tensor_tensor(
                        out=oh[:, u, h * half:(h + 1) * half, :], in0=bc(dst.unsqueeze(2), P, half, W),
                        scalar=fine_col[0:P, bass.ds(at, 1)], in1=bc(iota[0:P, :].unsqueeze(1), P, half, W),
                        op0=ALU.subtract, op1=ALU.is_equal)
                    if dones[h] is not None:
                        ins.then_inc(dones[h], 1)

                def add(u, at, done):
                    wait_reg(dve, s_agg[4], done)
                    part = sum_t[0:width, bass.ds(at * FW, W)]
                    vec.tensor_tensor(part, part, p_sum[0:width, u, 0:W], ALU.add).then_inc(s_acc, 1)

                def first_window(u, g):
                    at = within(group_windows(dve, 0, g)[0], (N - 1) // FW)
                    vec.tensor_tensor(toh[:, u, :, :], by_tile(of_group(typef, g), R),
                                      bc(rel_col[0:P, :].unsqueeze(1), P, S, R), ALU.is_equal)
                    for h in range(2):
                        one_hot(u, g, at, h, s_oh[4])

                for _ in range(2):
                    dve.sem_inc(s_group, 1)
                ch.start()
                ch(vec.memset(sum_t[0:width, :], 0.0))
                first_window(0, 0)
                with dve.Fori(0, IT) as it:
                    for q in range(Q):
                        g = it * Q + q
                        first, cnt, cum = group_windows(dve, 0, g)
                        first_window(1 - q % 2, g + 1)
                        wait_reg(dve, s_oh[4][1], it * Q + (q + 2))
                        add(q % 2, within(first, (N - 1) // FW), cum + 1)
                        dve.sem_inc(s_more, 1)
                        with dve.If(cnt > 1):
                            with dve.Fori(1, cnt) as k:
                                at = dve.snap(within(first + k * (W // FW), (N - 1) // FW))
                                for h in range(2):
                                    one_hot(q % 2, g, at, h, (None, s_more))
                                add(q % 2, at, cum + k + 1)
                        dve.sem_inc(s_group, 1)
                vec.memset(r1[:, :], 0.0).then_inc(s_sum[4], 1)

            def sum_pass(n, width, prepare, done=None):
                ch.start()
                ch(vec.memset(sum_t[0:max(width, D + 2), :], 0.0))
                with dve.Fori(0, IT) as it:
                    for q in range(Q):
                        g = it * Q + q
                        first, cnt, cum = group_windows(dve, 0, g)
                        prepare(it, q, g)
                        sum_windows(n, width, g, first, cnt, cum)
                        if done:
                            done(q)
                vec.memset(r1[:, :], 0.0).then_inc(s_sum[n], 1)

            def weighted(it, q, g):
                wait_reg(dve, s_gat[q], it * 16 * S + 16 * S)
                w = of_group(edge_w, g)
                vec.tensor_copy(msg[:, q % 2, :, D], w)
                vec.tensor_tensor(msg[:, q % 2, :, 0:D], gat[:, q, :, 0:D], by_tile(w, D), ALU.mult)\
                    .then_inc(s_msg, 1)
                wait_reg(dve, s_msg, it * Q + (q + 1))
                dve.sem_inc(s_free[q], 1)

            def layer_norm(n, b, u):
                ch(vec.tensor_reduce(out=r2[:, :], in_=ya[:, :, :], op=ALU.add, axis=AX.X))
                ch(vec.tensor_scalar(r2[:, :], r2[:, :], 1.0 / D, None, ALU.mult))
                ch(vec.tensor_tensor(ya[:, :, :], ya[:, :, :], bc(r2[:, :].unsqueeze(2), 128, BT, D), ALU.subtract))
                ch(vec.tensor_tensor(yb[:, :, :], ya[:, :, :], ya[:, :, :], ALU.mult))
                ch(vec.tensor_reduce(out=r2[:, :], in_=yb[:, :, :], op=ALU.add, axis=AX.X))
                dve.sem_inc(s_sqrt_in[n], 1)
                wait_reg(dve, s_sqrt[n], b * (2 if n == 0 else 1) + (2 if n == 0 else 1))
                ch(vec.reciprocal(r2[:, :], r2[:, :]))
                wait_reg(dve, s_yfree[n], b + 1)
                vec.tensor_tensor(yo[:, u, :, :], ya[:, :, :], bc(r2[:, :].unsqueeze(2), 128, BT, D), ALU.mult)\
                    .then_inc(s_y[n], 1)
                wait_reg(dve, s_y[n], b + 1)

            def bank(p, u, width):
                return p[:, u, 0:BT * width].rearrange("p (t d) -> p t d", t=BT)

            dve.wait_ge(s_load[2], 16)
            sum_pass(0, D + 2, weighted)
            with dve.Fori(0, NI) as it:
                for u in range(2):
                    b = dve.snap(it * 2 + u)
                    ch.start()
                    wait_reg(dve, s_mm[0], b + 3)
                    own, nb = bank(p_a, u, D), bank(p_b, u, D + 2)
                    ch.add(vec.tensor_copy(deg[:, bass.ds(b * BT, BT)], nb[:, :, D + 1]))
                    ch(vec.tensor_scalar_max(r1[:, :], nb[:, :, D], 1e-8))
                    ch(vec.reciprocal(r1[:, :], r1[:, :]))
                    ch(vec.tensor_tensor(ya[:, :, :], nb[:, :, 0:D], bc(r1[:, :].unsqueeze(2), 128, BT, D), ALU.mult))
                    ch(vec.tensor_tensor(ya[:, :, :], ya[:, :, :], own, ALU.add))
                    ch(vec.tensor_tensor(yb[:, :, :], ya[:, :, :], ya[:, :, :], ALU.mult))
                    ch(vec.tensor_reduce(out=r1[:, :], in_=yb[:, :, :], op=ALU.add, axis=AX.X))
                    dve.sem_inc(s_sqrt_in[0], 1)
                    wait_reg(dve, s_sqrt[0], b * 2 + 1)
                    ch(vec.tensor_scalar_max(r1[:, :], r1[:, :], 1e-12))
                    ch(vec.reciprocal(r1[:, :], r1[:, :]))
                    ch(vec.tensor_tensor(ya[:, :, :], ya[:, :, :], bc(r1[:, :].unsqueeze(2), 128, BT, D), ALU.mult))
                    wait_reg(dve, s_xs[u], it * 16 + 16 * (1 + NI * 0))
                    ch(vec.tensor_tensor(ya[:, :, :], ya[:, :, :], xs[:, u, :, :], ALU.add))
                    dve.sem_inc(s_xfree[0], 1)
                    layer_norm(0, b, u)

            def prepare1(it, q, g):
                wait_reg(dve, s_gat[q], it * 128 + 128 * (1 + IT))
                wait_reg(dve, s_ea[q], it * 16 + 16)
                vec.tensor_tensor(ea[:, q, :, :], ea[:, q, :, :], gat[:, q, :, 0:D], ALU.add).then_inc(s_pre, 1)

            sum_pass(1, D, prepare1)
            def add_sums(it, u, b):
                wait_reg(dve, s_tr[1], b + 1)
                vec.tensor_tensor(stage[0:D, u, :], p_tr_flat[0:D, 0:BC], sum_t[0:D, nodes(b)], ALU.add)\
                    .then_inc(s_stage[1], 1)

            def finish(n, p):
                def residual(it, u, b):
                    ch.start()
                    wait_reg(dve, s_mm[n], b + 3)
                    wait_reg(dve, s_xs[u], it * 16 + 16 * (1 + NI * n))
                    ch(vec.tensor_tensor(ya[:, :, :], bank(p, u, D), xs[:, u, :, :], ALU.add))
                    dve.sem_inc(s_xfree[n], 1)
                    layer_norm(n, b, u)
                return residual

            two_step(dve, add_sums, finish(1, p_a))

            def prepare2(it, q, g):
                pass

            sum_pass(2, D, prepare2, lambda q: dve.sem_inc(s_free[q], 1))

            def scale_rows(it, u, b):
                wait_reg(dve, s_xs[u], it * 16 + 16 * (1 + NI * 2))
                wait_reg(dve, s_tr[2], b + 1)
                dv = deg[:, bass.ds(b * BT, BT)]
                vec.tensor_copy(xd[:, u, :, D], dv)
                vec.tensor_tensor(xd[:, u, :, 0:D], xs[:, u, :, :], bc(dv.unsqueeze(2), 128, BT, D), ALU.mult)\
                    .then_inc(s_act[2], 1)
                wait_reg(dve, s_act[2], b + 1)
                dve.sem_inc(s_xfree[2], 1)

            def keep_h(it, u, b):
                wait_reg(dve, s_mm[2], b + 3)
                vec.tensor_copy(sum_t[0:D, nodes(b, HB)], p_a[0:D, u, 0:HB])
                vec.tensor_copy(sum_t[0:D, nodes(b, HB, HB)], p_b[0:D, u, 0:HB]).then_inc(s_mid[2], 1)

            two_step(dve, scale_rows, keep_h)
            dve.wait_ge(s_mid[2], NB + 2)
            ch.start()
            for c in range(25):
                ch.add(vec.bn_stats(out=bn[:, c, :], in_=sum_t[0:D, c * (N // 25):(c + 1) * (N // 25)]))
            ch.wait()
            ch(vec.bn_aggr(out=bnm[:, 0:2], in_=bn[:, :, :].rearrange("d c k -> d (c k)")))
            dve.sem_inc(s_bn, 1)
            dve.wait_ge(s_bnr, 1)
            ch(vec.reciprocal(bnm[:, 3:4], bnm[:, 2:3]))
            ch(vec.tensor_tensor(bnm[:, 3:4], bnm[:, 3:4], wt["gamma"][:, :], ALU.mult))
            ch(vec.tensor_tensor(bnm[:, 4:5], bnm[:, 0:1], bnm[:, 3:4], ALU.mult))
            ch(vec.tensor_tensor(bnm[:, 4:5], wt["beta"][:, :], bnm[:, 4:5], ALU.subtract))
            dve.sem_inc(s_bnc, 1)
            def leaky(it, u, b):
                wait_reg(dve, s_act[3], b + 1)
                vec.scalar_tensor_tensor(out=xt[0:D, u, :], in0=stage[0:D, u, :], scalar=0.01,
                                         in1=stage[0:D, u, :], op0=ALU.mult, op1=ALU.max).then_inc(s_mid[3], 1)

            two_step(dve, leaky, finish(3, p_b))

            ch.start()
            dve.wait_ge(s_y[3], NB)
            for u in range(2):
                ch(vec.memset(hst[:, u, :, :, D + 1:HROW], 0.0))
            dve.sem_inc(s_zero, 1)
            with dve.Fori(0, NI) as it:
                for u in range(2):
                    b = dve.snap(it * 2 + u)
                    ch.start()
                    wait_reg(dve, s_yfree[4], b + 1)
                    for t in range(1 - u, BT, 2):
                        m = (BT * u + t) // 2
                        wait_reg(dve, s_h[0][1], it * BT + (m + 1))
                        vec.tensor_copy(hst[:, u, t, :, 0:D], p_a[:, 1, :].rearrange("p (r d) -> p r d", r=R))\
                            .then_inc(s_hc[0][1], 1)
                    wait_reg(dve, s_mm[4], b + 3)
                    ch(vec.tensor_copy(sd[:, :, :], bank(p_sum, u, 2 * R)))
                    dve.sem_inc(s_xfree[4], 1)
                    table = dtab[:, bass.ds(b * BT, BT), :]
                    ch.add(vec.tensor_copy(hst[:, u, :, :, D], sd[:, :, 0:R]))
                    ch.add(vec.tensor_copy(table[:, :, 0:R], sd[:, :, R:2 * R]))
                    ch(vec.tensor_tensor(sd[:, :, 0:R], sd[:, :, 0:R], sd[:, :, R:2 * R], ALU.add))
                    ch(vec.scalar_tensor_tensor(out=table[:, :, R:2 * R], in0=sd[:, :, 0:R], scalar=0.2,
                                                in1=sd[:, :, 0:R], op0=ALU.mult, op1=ALU.max))
                    wait_reg(dve, s_hc[0][1], it * BT + (m + 2))
                    dve.sem_inc(s_y[4], 1)

            ch.start()
            ch(vec.memset(oht[:, GE:S * W], 0.0))
            table = dtab[:, :, :].rearrange("p w (c r) -> p w c r", c=2)
            for part in range(3):
                ch(vec.tensor_copy(dtab3[:, :, :, part, :], table))
                if part < 2:
                    ch(vec.tensor_tensor(table, table, dtab3[:, :, :, part, :], ALU.subtract))
            ch(vec.memset(trip_flat, 0.0))
            dve.sem_inc(s_zero, 1)
            dve.wait_ge(s_table, 4)
            dve.wait_ge(s_rld[0], 16)
            dve.wait_ge(s_rld[1], 16)
            ch.add(vec.tensor_copy(val, scan_dst_i))
            ch(vec.tensor_copy(rtype, scan_type_i))
            ch.add(vec.tensor_copy(ends[:, 0:1], val[:, 0:1]))
            ch.add(vec.tensor_copy(ends[:, 1:2], val[:, T - 1:T]))
            ch.add(vec.tensor_tensor(brk_f[:, 1:T], val[:, 1:T], val[:, 0:T - 1], ALU.is_equal))
            ch.add(vec.memset(brk_f[:, 0:1], 1.0))
            ch.add(vec.tensor_tensor(brk_b[:, 0:T - 1], val[:, 1:T], val[:, 0:T - 1], ALU.is_equal))
            ch(vec.memset(brk_b[:, T - 1:T], 1.0))
            ch.add(vec.tensor_scalar(lead, val, ends[:, 0:1], None, ALU.is_equal))
            ch(vec.tensor_scalar(trail, val, ends[:, 1:2], None, ALU.is_equal))
            masks = (brk_f, brk_b, lead, trail)
            for m_ in masks:
                ch.add(vec.tensor_scalar(m_, m_, 1.0, BIG, ALU.subtract, ALU.mult))
            ch.add(vec.tensor_copy(runs[:, 2 * R:2 * R + 2], ends[:, :]))
            ch.wait()

            with dve.Fori(0, IT) as it:
                for q in range(Q):
                    g = it * Q + q
                    first, cnt, cum = group_windows(dve, 1, g)
                    ch.start()
                    ch(vec.tensor_tensor(toh[:, 0, :, :], by_tile(of_group(typef, g), R),
                                         bc(rel_col[0:P, :].unsqueeze(1), P, S, R), ALU.is_equal))
                    wait_reg(dve, s_drow[q % 2], it * 32 + 16 * (1 + q // 2))
                    with dve.Fori(0, cnt) as k:
                        w = dve.snap(within(first + k, NW - 1))
                        ch2 = Chain(dve, s_vch)
                        ch2.start()
                        vec.tensor_scalar(oht[:, 0:GE], drow[:, q % 2, :], node_col[:, bass.ds(w, 1)], None,
                                          ALU.is_equal).then_inc(s_oh[3][0], 1)
                        wait_reg(dve, s_agg[3], cum + k + 1)
                        ch2(vec.tensor_tensor(
                            sel[:, :, :, :].rearrange("p s c (k r) -> p s (c k) r", k=3),
                            p_sum[0:P, 0, 0:S * 6 * R].rearrange("p (s c r) -> p s c r", s=S, c=6),
                            bc(toh[:, 0, :, :].unsqueeze(2), P, S, 6, R), ALU.mult))
                        ch2(vec.tensor_reduce(out=sel2[:, :, :], in_=sel[:, :, :, :], op=ALU.add, axis=AX.X))
                        part = trip[0:P, bass.ds(g, 1), :, 1:3].rearrange("p a s c -> p (a s) c")
                        ch2(vec.tensor_tensor(part, part, sel2[:, :, :], ALU.add))
                    dve.sem_inc(s_drused, 1)
            dve.sem_inc(s_trip, 1)

            ch.start()
            dve.wait_ge(s_scan, 16)
            ch(vec.tensor_tensor(score, score, gap, ALU.add))
            ch(vec.scalar_tensor_tensor(out=score, in0=score, scalar=0.2, in1=score, op0=ALU.mult, op1=ALU.max))
            ch(vec.tensor_copy(best, self_score))

            def exchange(k, maximum):
                neutral = -BIG if maximum else 0.0
                dve.wait_ge(s_rund, 64 * k + 32)
                firsts, lasts = run_row[:, :, 2 * R], run_row[:, :, 2 * R + 1]
                joined, through = link_row[:, 0, :], link_row[:, 1, :]
                ch(vec.memset(link_row[:, :, :], 0.0))
                ch.add(vec.tensor_tensor(joined[:, 1:P], firsts[:, 1:P], lasts[:, 0:P - 1], ALU.is_equal))
                ch(vec.tensor_tensor(through[:, 0:P], firsts, lasts, ALU.is_equal))
                pf, pb = link_row[:, 2, 0:P], link_row[:, 3, 0:P]
                ch.add(vec.tensor_tensor(pf, joined[:, 0:P], through[:, 0:P], ALU.mult))
                ch(vec.tensor_tensor(pb, joined[:, 1:P + 1], through[:, 0:P], ALU.mult))
                if maximum:
                    ch(vec.tensor_scalar(link_row[:, 0, :], link_row[:, 0, :], 1.0, BIG, ALU.subtract, ALU.mult))
                    ch(vec.tensor_scalar(link_row[:, 2:4, :], link_row[:, 2:4, :], 1.0, BIG, ALU.subtract, ALU.mult))
                op0, op1 = (ALU.add, ALU.max) if maximum else (ALU.mult, ALU.add)
                for r in range(R):
                    ch.add(vec.tensor_tensor_scan(carry_row[:, :, r], pf, run_row[:, :, r], neutral, op0, op1))
                    ch.add(vec.tensor_tensor_scan(carry_row[:, ::-1, R + r], pb[:, ::-1], run_row[:, ::-1, R + r],
                                                  neutral, op0, op1))
                ch.wait()
                link_op = ALU.add if maximum else ALU.mult
                ch.add(vec.memset(init_row[:, 0:1, 0:R], neutral))
                ch.add(vec.memset(init_row[:, P - 1:P, R:2 * R], neutral))
                ch.add(vec.tensor_tensor(init_row[:, 1:P, 0:R], carry_row[:, 0:P - 1, 0:R],
                                         bc(joined[:, 1:P].unsqueeze(2), 1, P - 1, R), link_op))
                ch(vec.tensor_tensor(init_row[:, 0:P - 1, R:2 * R], carry_row[:, 1:P, R:2 * R],
                                     bc(joined[:, 1:P].unsqueeze(2), 1, P - 1, R), link_op))
                dve.sem_inc(s_run, 1)
                dve.wait_ge(s_rund, 64 * k + 64)

            ends_of = ((trail, 0), (lead, R))
            with dve.Fori(0, R) as r:
                ch2 = Chain(dve, s_vch)
                ch2.start()
                ch2(vec.tensor_scalar(off, rtype, rel_col[0:P, bass.ds(r, 1)], -BIG, ALU.not_equal, ALU.mult))
                ch2(vec.tensor_tensor(val, score, off, ALU.add))
                for k, (mask, at) in enumerate(ends_of):
                    ch2(vec.tensor_tensor_reduce(out=fwd, in0=val, in1=mask, scale=1.0, scalar=-3 * BIG, op0=ALU.add,
                                                 op1=ALU.max, accum_out=ends[:, k:k + 1]))
                    ch2(vec.tensor_copy(runs[:, bass.ds(r + at, 1)], ends[:, k:k + 1]))
            ch.start()
            dve.sem_inc(s_run, 1)
            exchange(0, True)
            with dve.Fori(0, R) as r:
                ch2 = Chain(dve, s_vch)
                ch2.start()
                ch2(vec.tensor_scalar(off, rtype, rel_col[0:P, bass.ds(r, 1)], -BIG, ALU.not_equal, ALU.mult))
                ch2(vec.tensor_tensor(val, score, off, ALU.add))
                ch2.add(vec.tensor_tensor_scan(fwd, brk_f, val, run_in[:, bass.ds(r, 1)], ALU.add, ALU.max))
                ch2(vec.tensor_tensor_scan(bwd[:, ::-1], brk_b[:, ::-1], val[:, ::-1], run_in[:, bass.ds(r + R, 1)],
                                           ALU.add, ALU.max))
                ch2(vec.tensor_tensor(fwd, fwd, bwd, ALU.max))
                ch2(vec.tensor_tensor(fwd, fwd, off, ALU.add))
                ch2(vec.tensor_tensor(best, best, fwd, ALU.max))
            ch.start()
            ch(vec.tensor_tensor(gap, score, best, ALU.subtract))
            dve.sem_inc(s_ein, 1)
            ch.add(vec.tensor_tensor(self_gap, self_score, best, ALU.subtract))
            for m_ in masks:
                ch.add(vec.tensor_single_scalar(m_, m_, 0.0, op=ALU.is_equal))
            ch.wait()
            dve.sem_inc(s_ein, 1)
            dve.wait_ge(s_eout, 2)
            ch(vec.tensor_copy(best, self_score))
            with dve.Fori(0, R) as r:
                ch2 = Chain(dve, s_vch)
                ch2.start()
                ch2(vec.scalar_tensor_tensor(out=val, in0=rtype, scalar=rel_col[0:P, bass.ds(r, 1)], in1=score,
                                             op0=ALU.is_equal, op1=ALU.mult))
                for k, (mask, at) in enumerate(ends_of):
                    ch2(vec.tensor_tensor_reduce(out=fwd, in0=val, in1=mask, scale=1.0, scalar=0.0, op0=ALU.mult,
                                                 op1=ALU.add, accum_out=ends[:, k:k + 1]))
                    ch2(vec.tensor_copy(runs[:, bass.ds(r + at, 1)], ends[:, k:k + 1]))
            ch.start()
            dve.sem_inc(s_run, 1)
            exchange(1, False)
            with dve.Fori(0, R) as r:
                ch2 = Chain(dve, s_vch)
                ch2.start()
                ch2(vec.scalar_tensor_tensor(out=val, in0=rtype, scalar=rel_col[0:P, bass.ds(r, 1)], in1=score,
                                             op0=ALU.is_equal, op1=ALU.mult))
                ch2.add(vec.tensor_tensor_scan(fwd, brk_f, val, run_in[:, bass.ds(r, 1)], ALU.mult, ALU.add))
                ch2(vec.tensor_tensor_scan(bwd[:, ::-1], brk_b[:, ::-1], val[:, ::-1], run_in[:, bass.ds(r + R, 1)],
                                           ALU.mult, ALU.add))
                ch2(vec.tensor_tensor(fwd, fwd, bwd, ALU.add))
                ch2(vec.tensor_tensor(fwd, fwd, val, ALU.subtract))
                ch2(vec.scalar_tensor_tensor(out=fwd, in0=rtype, scalar=rel_col[0:P, bass.ds(r, 1)], in1=fwd,
                                             op0=ALU.is_equal, op1=ALU.mult))
                ch2(vec.tensor_tensor(best, best, fwd, ALU.add))
            ch.start()
            ch(vec.reciprocal(best, best))
            ch(vec.tensor_tensor(val, score, best, ALU.mult))
            dve.sem_inc(s_alpha, 1)
            dve.wait_ge(s_alphal, 16)

            piped_pass(HROW)

            def scale_self(it, u, b):
                ch.start()
                wait_reg(dve, s_mid[5], b + 1)
                nb = bank(p_b, u, HROW)
                ch(vec.tensor_scalar(self_w[:, :, :], nb[:, :, D:HROW], -1.0, 1.0, ALU.mult, ALU.add))
                for t in range(BT):
                    k, m = (BT * u + t) % 2, (BT * u + t) // 2
                    wait_reg(dve, s_h[1][k], it * BT + (m + 1))
                    vec.tensor_tensor(self_h[u][:, t, :, :], p_sum[:, k, :].rearrange("p (r d) -> p r d", r=R),
                                      bc(self_w[:, t, :].unsqueeze(2), 128, R, D), ALU.mult)\
                        .then_inc(s_hc[1][k], 1)
                for k in range(2):
                    m = (BT * u + BT - 1 - (BT * u + BT - 1 + k) % 2) // 2
                    wait_reg(dve, s_hc[1][k], it * BT + (m + 2))
                dve.sem_inc(s_self, 1)

            def finish5(it, u, b):
                ch.start()
                own, nb = bank(p_a, u, D), bank(p_b, u, HROW)
                wait_reg(dve, s_xs[u], it * 16 + 16 * (1 + NI * 5))
                ch(vec.tensor_tensor(ya[:, :, :], xs[:, u, :, :], own, ALU.add))
                ch(vec.tensor_tensor(ya[:, :, :], ya[:, :, :], nb[:, :, 0:D], ALU.add))
                dve.sem_inc(s_xfree[5], 1)
                wait_reg(dve, s_selfsum, b + 1)
                ch(vec.tensor_tensor(ya[:, :, :], ya[:, :, :], self_h[u][:, :, 0, :], ALU.add))
                layer_norm(5, b, u)

            two_step(dve, scale_self, finish5)


def kernel(**inputs):
    import numpy as np
    import concourse.bacc as bacc
    from concourse.bass_utils import run_bass_kernel_spmd

    nc = bacc.Bacc("TRN2", target_bir_lowering=False, num_devices=1)
    arrays = {}

    def given(name, a):
        a = np.ascontiguousarray(a)
        arrays[f"in_{name}"] = a
        return nc.dram_tensor(f"in_{name}", a.shape, mybir.dt.from_np(a.dtype), kind="ExternalInput").ap()

    i = {k: np.asarray(v) for k, v in inputs.items()}
    grouped = lambda a: a.reshape(G, P, S).transpose(1, 0, 2)
    w2 = i["L2_gnn_W"].T
    laid = {
        "ws65": np.concatenate([i["L0_gnn_W_self"].T, i["L0_gnn_bias"][None]]), "wn": i["L0_gnn_W_neigh"].T,
        "w1": i["L1_gnn_W1"], "b1": i["L1_gnn_b1"][:, None],
        "w2b": np.concatenate([i["L1_gnn_W2"], i["L1_gnn_b2"][None]]),
        "wi": w2[:D], "wj": w2[D:], "b2": i["L2_gnn_b"][None],
        "gamma": i["L2_gnn_gamma"][:, None], "beta": i["L2_gnn_beta"][:, None],
        "wself": i["L3_gnn_W_self"], "bself": i["L3_gnn_b_self"][None],
        "wcat": i["L3_gnn_W"].transpose(1, 0, 2).reshape(D, R * D),
        "wrt": i["L3_gnn_W"].transpose(2, 0, 1).reshape(D, R * D),
        "att": np.stack([i["L3_gnn_att_src"], i["L3_gnn_att_dst"]], -1).transpose(1, 0, 2).reshape(D, 2 * R),
        "rbias": i["L3_gnn_bias"].reshape(1, R * D),
    }
    args = [given("x", i["x"]), given("src_p", grouped(i["src"])), given("dst_p", grouped(i["dst"])),
            given("type_p", grouped(i["edge_type_8"])), given("weight_p", grouped(i["edge_weight"])),
            given("dst_f", i["dst"]), given("type_f", i["edge_type_8"]), given("edge_attr", i["edge_attr_64"]),
            {name: given(name, laid[name]) for name, _ in WEIGHTS}]
    out = nc.dram_tensor("out", (N, D), mybir.dt.float32, kind="ExternalOutput").ap()
    program(nc, *args, out)
    return run_bass_kernel_spmd(nc, [arrays], core_ids=[0]).results[0]["out"]
```

```python
import concourse.bass as bass
from concourse import mybir
from contextlib import ExitStack

N, E, D, R = 12500, 200000, 64, 8
P, S = 125, 8
GE = P * S
G = E // GE
Q = 4
IT = G // Q
W = 128
NW = -(-N // W)
NP = NW * W
FW = 32
BT = 7
NB = NW // BT
BC = BT * W
HB = BC // 2
TAIL = N - (NB - 1) * BC
TAIL_TILES, TAIL_ROWS = TAIL // W, TAIL % W
HROW = 72
T = E // P
SG = 100
BIG = 1e37
NO_EDGE = -1e30
HE = GE // 2
EPS_LN = 1e-5
NORMED = (0, 1, 3, 5)

WEIGHTS = [("ws65", (65, 64)), ("wn", (64, 64)), ("w1", (64, 64)), ("b1", (64, 1)), ("w2b", (65, 64)),
           ("wi", (64, 64)), ("wj", (64, 64)), ("b2", (1, 64)), ("gamma", (64, 1)), ("beta", (64, 1)),
           ("wself", (64, 64)), ("bself", (1, 64)), ("wcat", (64, 512)), ("wrt", (64, 512)),
           ("att", (64, 16)), ("rbias", (1, 512))]


def program(nc, x, src_p, dst_p, type_p, weight_p, dst_f, type_f, edge_attr, weights, out):
    f32, i32, i16, bf16 = mybir.dt.float32, mybir.dt.int32, mybir.dt.int16, mybir.dt.bfloat16
    ALU, ACT, AX = mybir.AluOpType, mybir.ActivationFunctionType, mybir.AxisListType
    dram = lambda n, s, d=f32: nc.dram_tensor(n, s, d, kind="Internal").ap()
    x1_d, x2_d, x3_d = dram("x1_d", (NP, D)), dram("x2_d", (NP, D)), dram("x3_d", (NP, D))
    rel_d = dram("rel_d", (NP * R, HROW))
    he_d = dram("he_d", (G, P, S * HROW))
    key_d = dram("key_d", (P, G, S), i32)
    dst16_d = dram("dst16_d", (E,), i16)
    trip_d = dram("trip_d", (E * 3,))
    alpha_d = dram("alpha_d", (E,))
    run_out_d, run_in_d = dram("run_out_d", (2, P, 2 * R + 2)), dram("run_in_d", (2, P, 2 * R))

    with ExitStack() as ctx:
        sb = lambda n, s, d=f32: ctx.enter_context(nc.sbuf_tensor(n, s, d))
        ps = lambda n, s: ctx.enter_context(nc.psum_tensor(n, s, f32))
        sem = lambda n: ctx.enter_context(nc.semaphore(n))

        ident, iota = sb("ident", [128, 128]), sb("iota", [128, W])
        fine_col, node_col = sb("fine_col", [128, NP // FW]), sb("node_col", [128, NW])
        rel_col = sb("rel_col", [128, R])
        wt = {n: sb("w_" + n, list(s)) for n, s in WEIGHTS}
        wn66, wj66 = sb("wn66", [D + 2, D + 2]), sb("wj66", [D + 2, D])
        wd65, wself65 = sb("wd65", [65, D]), sb("wself65", [65, D])
        sdw, brow = sb("sdw", [D, 2 * R]), sb("brow", [1, D])
        eps_col, root_table = sb("eps_col", [128, 1]), sb("root_table", [128, len(NORMED)])
        idx = sb("idx", [P, Q, S], i32)
        gat = sb("gat", [P, Q, S, HROW])
        ea = sb("ea", [P, Q, S, D])
        msg = sb("msg", [P, 2, S, HROW])
        oh = sb("oh", [P, 2, S, W])
        dstf, edge_w, typef = [sb(n, [P, G + 1, S]) for n in ("dstf", "edge_w", "typef")]
        trip, trip_s = sb("trip", [128, G, S, 3]), sb("trip_s", [128, T, 3])
        drow, oht = sb("drow", [128, 2, GE], i16), sb("oht", [128, S * W], bf16)
        toh, sel, sel2 = sb("toh", [P, 2, S, R]), sb("sel", [P, S, 2, 3 * R]), sb("sel2", [P, S, 2])
        ends, runs, run_in = sb("ends", [P, 3]), sb("runs", [P, 2 * R + 2]), sb("run_in", [P, 2 * R])
        sum_t = sb("sum_t", [128, NP + W - FW])
        deg = sb("deg", [128, NW])
        dtab = sb("dtab", [128, NW, 2 * R])
        win = sb("win", [1, 2, G + 1], i32)
        falls, falls_i = sb("falls", [1, 2]), sb("falls_i", [1, 1], i32)
        ones_col = sb("ones_col", [128, 1])
        link_row = sb("link_row", [1, 4, P + 1])
        ends_g, ends_i = sb("ends_g", [SG, 2, 2]), sb("ends_i", [SG, 4, 2], i32)
        wcols, wrows, wones = sb("wcols", [SG, 4, 2]), sb("wrows", [1, 6, G]), sb("wones", [1, G])
        wint = sb("wint", [1, 3, G], i32)
        xs, xd = sb("xs", [128, 2, BT, D]), sb("xd", [128, 2, BT, D + 1])
        stage, xt = sb("stage", [128, 2, BC]), sb("xt", [65, 2, BC])
        ya, yb, yo = sb("ya", [128, BT, D]), sb("yb", [128, BT, D]), sb("yo", [128, 2, BT, D])
        r1, r2 = sb("r1", [128, BT]), sb("r2", [128, BT])
        sd, self_w = sb("sd", [128, BT, 2 * R]), sb("self_w", [128, BT, R])
        bn, bnm = sb("bn", [D, 25, 6]), sb("bnm", [D, 6])
        trip_flat = trip[0:P, :, :, :].rearrange("p g s c -> p (g s c)")
        scan_flat = trip_s[0:P, :, :].rearrange("p t c -> p (t c)")
        dtab3 = trip_s[:, :, :].rearrange("p t c -> p (t c)").bitcast(bf16)[:, 0:NW * 6 * R]\
            .rearrange("p (w c k r) -> p w c k r", w=NW, c=2, k=3)
        src_i, type_i, dst_i = [trip_flat.bitcast(i32)[:, k * T:(k + 1) * T] for k in range(3)]
        dstn_i = scan_flat.bitcast(i32)[:, 0:T]
        dst16 = scan_flat[:, 2 * T:2 * T + T // 2].bitcast(i16)
        stat_i = oh[0:SG, :, :, :].rearrange("p a s w -> p (a s w)")[:, 0:2 * GE].bitcast(i32)
        stat_i = stat_i.rearrange("p (a e) -> p a e", a=2)
        self_h = [flat[:, 0:BT * R * D].rearrange("p (t r d) -> p t r d", t=BT, r=R)
                  for flat in (trip[:, :, :, :].rearrange("p g s c -> p (g s c)"),
                               trip_s[:, :, :].rearrange("p t c -> p (t c)"))]
        self_y = [flat[:, BT * R * D:BT * (R + 1) * D].rearrange("p (t d) -> p t d", t=BT)
                  for flat in (trip[:, :, :, :].rearrange("p g s c -> p (g s c)"),
                               trip_s[:, :, :].rearrange("p t c -> p (t c)"))]
        hst = sum_t[:, 0:2 * BT * R * HROW].rearrange("p (u t r c) -> p u t r c", u=2, t=BT, r=R)
        rtype, brk_f, brk_b, lead, trail, val, fwd = [sum_t[0:P, k * T:(k + 1) * T] for k in range(7)]
        bwd, best, off = [trip_flat[:, k * T:(k + 1) * T] for k in range(3)]
        scan_dst_i, scan_type_i = fwd.bitcast(i32), rtype.bitcast(i32)
        run_row = gat[0:1, :, :, :].rearrange("a q s c -> a (q s c)")[:, 0:P * (2 * R + 2)]\
            .rearrange("a (p c) -> a p c", p=P)
        carry_row = ea[0:1, :, :, :].rearrange("a q s d -> a (q s d)")[:, 0:P * 2 * R].rearrange("a (p c) -> a p c", p=P)
        init_row = oh[0:1, :, :, :].rearrange("a u s w -> a (u s w)")[:, 0:P * 2 * R].rearrange("a (p c) -> a p c", p=P)
        score, gap, self_score, self_gap = trip_s[0:P, :, 0], trip_s[0:P, :, 1], trip_s[0:P, :, 2], off
        oht_tile = oht[:, :].rearrange("n (p s) -> n p s", s=S)
        any_cut = [sum_t[:, k * HE:(k + 1) * HE] for k in range(24)]
        any_trip = sum_t[:, 0:3 * HE].rearrange("p (e c) -> p e c", c=3)
        any_type_i, any_type, any_score, any_off, any_alpha = any_cut[3].bitcast(i32), *any_cut[4:8]
        any_mask, any_val = [sum_t[:, k * HE:(k + R) * HE].rearrange("p (r e) -> p r e", r=R) for k in (8, 16)]
        any_dst = drow[:, 0, 0:HE]
        any_max, any_self = dtab[:, :, 0:R], dtab[:, :, R:2 * R]
        any_den = trip_s[:, :, :].rearrange("p t c -> p (t c)")[:, 0:NW * R].rearrange("p (w r) -> p w r", w=NW)
        any_col = trip_s[:, :, :].rearrange("p t c -> p (t c)")[:, NW * R:(NW + 1) * R].unsqueeze(1)
        any_row = ea[0:1, 0, :, :].rearrange("a s d -> a (s d)")[:, 0:HE]
        p_sum, p_tr = ps("p_sum", [128, 2, 512]), ps("p_tr", [128, 2, 512])
        p_a, p_b = ps("p_a", [128, 2, 512]), ps("p_b", [128, 2, 512])
        p_tr_flat = p_tr[:, :, :].rearrange("p a c -> p (a c)")

        s_load = [sem(f"s_load{k}") for k in range(4)]
        s_wload, s_const, s_vconst = sem("s_wload"), sem("s_const"), sem("s_vconst")
        s_cols, s_rows, s_win = sem("s_cols"), sem("s_rows"), sem("s_win")
        s_prep, s_patch, s_sdw = sem("s_prep"), sem("s_patch"), sem("s_sdw")
        s_key, s_keyst, s_zero = sem("s_key"), sem("s_keyst"), sem("s_zero")
        s_idx = [sem(f"s_idx{q}") for q in range(Q)]
        s_gat = [sem(f"s_gat{q}") for q in range(Q)]
        s_free = [sem(f"s_free{q}") for q in range(Q)]
        s_ea = [sem(f"s_ea{q}") for q in range(Q)]
        s_hest = [sem(f"s_hest{q}") for q in range(Q)]
        s_held = [sem(f"s_held{q}") for q in range(Q)]
        s_pre, s_msg = sem("s_pre"), sem("s_msg")
        s_oh = [[sem(f"s_oh{n}_{h}") for h in range(1 if n == 3 else 2)] for n in range(5)]
        s_agg = [sem(f"s_agg{n}") for n in range(5)]
        s_sum = {n: sem(f"s_sum{n}") for n in (0, 1, 2, 4)}
        s_acc, s_scan_copy = sem("s_acc"), sem("s_scan_copy")
        s_drow = [sem(f"s_drow{u}") for u in range(2)]
        s_drused, s_trip, s_tripd = sem("s_drused"), sem("s_trip"), sem("s_tripd")
        s_rld = sem("s_rld")
        s_scan, s_run, s_rund = sem("s_scan"), sem("s_run"), sem("s_rund")
        s_ein, s_eout, s_alpha, s_alphad, s_alphal = [sem(n) for n in
                                                      ("s_ein", "s_eout", "s_alpha", "s_alphad", "s_alphal")]
        s_any_dma, s_any_in, s_any_used = sem("s_any_dma"), sem("s_any_in"), sem("s_any_used")
        s_any_acc, s_any_sum = sem("s_any_acc"), sem("s_any_sum")
        s_any_gap, s_any_exp = [[sem(f"s_any_{n}{k}") for k in range(2)] for n in ("gap", "exp")]
        NS = 6
        s_tail = sem("s_tail")
        s_xs = [sem(f"s_xs{u}") for u in range(2)]
        s_xfree = [sem(f"s_xfree{n}") for n in range(NS)]
        s_tr = {n: sem(f"s_tr{n}") for n in (0, 1, 2, 4, 5)}
        s_stage = {n: sem(f"s_stage{n}") for n in (0, 1, 2, 4, 5)}
        s_mid = {n: sem(f"s_mid{n}") for n in (1, 2, 3, 5)}
        s_act = {n: sem(f"s_act{n}") for n in (1, 2, 3, 4)}
        s_mm = [sem(f"s_mm{n}") for n in range(NS)]
        s_sqrt_in, s_sqrt = [{n: sem(f"s_{k}{n}") for n in NORMED} for k in ("sqrt_in", "sqrt")]
        s_y = {n: sem(f"s_y{n}") for n in (0, 1, 3, 4, 5)}
        s_yst = [sem(f"s_yst{u}") for u in range(2)]
        s_yfree = {n: sem(f"s_yfree{n}") for n in (0, 1, 3, 4, 5)}
        s_table = sem("s_table")
        s_bn, s_bnr, s_bnc = sem("s_bn"), sem("s_bnr"), sem("s_bnc")
        s_h = [[sem(f"s_h{n}_{k}") for k in range(2)] for n in range(2)]
        s_hc = [[sem(f"s_hc{n}_{k}") for k in range(2)] for n in range(2)]
        s_more = sem("s_more")
        s_group = sem("s_group")
        s_self, s_selfsum = sem("s_self"), sem("s_selfsum")
        s_vch, s_pch = sem("s_vch"), sem("s_pch")
        s_turn = sem("s_turn")
        block = ctx.enter_context(nc.Block())

        class Chain:

            def __init__(self, eng, s):
                self.eng, self.s, self.n = eng, s, 0

            def start(self):
                self.eng.sem_clear(self.s)
                self.n = 0

            def add(self, ins):
                ins.then_inc(self.s, 1)
                self.n += 1

            def wait(self):
                self.eng.wait_ge(self.s, self.n)

            def __call__(self, ins):
                self.add(ins)
                self.wait()

        def wait_reg(eng, s, v):
            eng.wait_ge(s, v)
            eng.sem_inc(s_turn, 1)

        def group_windows(eng, table, g):
            v = eng.value_load(win[0:1, table, bass.ds(g, 1)], min_val=0, max_val=(NW * G << 16) - 1)
            return eng.snap((v >> 7) & 511), eng.snap((v & 127) + 1), eng.snap(v >> 16)

        def within(v, most):
            return nc.s_assert_within(v, 0, most, skip_runtime_bounds_check_because=(
                "a group's last window holds its largest dst, which is below N"))

        def out_of_order(eng):
            eng.wait_ge(s_alphad, 16)
            return eng.value_load(falls_i[0:1, 0:1], min_val=1, max_val=2) > 1

        def two_step(eng, first, second):
            def snap(v):
                return v if isinstance(v, int) else eng.snap(v)

            first(0, 0, 0)
            with eng.Fori(0, NI - 1) as it:
                first(it, 1, snap(it * 2 + 1))
                second(it, 0, snap(it * 2))
                first(snap(it + 1), 0, snap(it * 2 + 2))
                second(it, 1, snap(it * 2 + 1))
            first(NI - 1, 1, NB - 1)
            for u in range(2):
                second(NI - 1, u, NB - 2 + u)

        def rows(table, b):
            return table[bass.ds(b * BC, BC), :].rearrange("(t p) d -> p t d", p=W)

        def of_group(buf, g):
            return buf[:, bass.ds(g, 1), :].rearrange("p a s -> p (a s)")

        def bc(ap, *shape):
            return ap.to_broadcast(list(shape))

        def by_tile(ap, width):
            return bc(ap.unsqueeze(2), P, S, width)

        def nodes(b, width=BC, at=0):
            return bass.ds(b * BC + at, width)

        X = [x, x1_d, x2_d, x2_d, x3_d, x3_d]
        Y = {0: x1_d, 1: x2_d, 3: x3_d, 5: out}
        NI = NB // 2
        stored = {0: 0, 1: 1, 3: 2, 4: 3, 5: 4}

        @block.sync
        def _(sp):
            flat = "p g s -> p (g s)"
            sp.dma_start(stat_i, dst_f.rearrange("(a g e) -> g a e", a=2, g=SG)).then_inc(s_load[0], 16)
            sp.dma_start(dst_i, dst_p.rearrange(flat)).then_inc(s_load[1], 16)
            sp.dma_start(edge_w[:, 0:G, :].rearrange(flat), weight_p.rearrange(flat)).then_inc(s_load[2], 16)
            for q in range(Q):
                sp.dma_start(idx[:, q, :], src_p[:, q, :]).then_inc(s_idx[q], 16)
            sp.dma_start(src_i, src_p.rearrange(flat)).then_inc(s_load[3], 16)
            sp.dma_start(type_i, type_p.rearrange(flat)).then_inc(s_load[3], 16)
            sp.dma_start(dstn_i, dst_f.rearrange("(p t) -> p t", p=P)).then_inc(s_load[3], 16)
            for name, _ in WEIGHTS:
                sp.dma_start(wt[name][:, :], weights[name]).then_inc(s_wload, 16)
            sp.wait_ge(s_prep, 1)
            sp.dma_start(wn66[0:D, 0:D], weights["wn"]).then_inc(s_patch, 16)
            sp.dma_start(wself65[D:D + 1, :], brow[0:1, :]).then_inc(s_patch, 16)
            sp.dma_start(wself65[0:D, :], weights["wself"]).then_inc(s_patch, 16)
            sp.dma_start(wd65[D:D + 1, :], weights["b2"]).then_inc(s_patch, 16)
            sp.wait_ge(s_key, 1)
            sp.dma_start(key_d.rearrange(flat), src_i).then_inc(s_keyst, 16)
            sp.dma_start(dst16_d.rearrange("(p t) -> p t", p=P), dst16).then_inc(s_keyst, 16)

            def refill(n, q, it, source):
                wait_reg(sp, s_free[q], it + (2 + IT * n))
                sp.dma_start(idx[:, q, :], source[:, bass.ds(it * Q + (Q + q), 1), :]
                             .rearrange("p a s -> p (a s)")).then_inc(s_idx[q], 16)

            def first_indices(n, source):
                for q in range(Q):
                    sp.wait_ge(s_free[q], IT * n + 1)
                    sp.dma_start(idx[:, q, :], source[:, q, :]).then_inc(s_idx[q], 16)

            def dense_io(n):
                r0 = (NB - 1) * BC

                def load(u, b):
                    sp.dma_start(xs[:, u, :, :], rows(X[n], b)).then_inc(s_xs[u], 16)

                def load_last():
                    if X[n] is not x:
                        return load(1, NB - 1)
                    sp.dma_start(xs[0:TAIL_ROWS, 1, TAIL_TILES, :], x[r0 + TAIL_TILES * W:N, :])\
                        .then_inc(s_tail, 16)
                    sp.wait_ge(s_tail, 16)
                    sp.dma_start(xs[:, 1, 0:TAIL_TILES, :], x[r0:r0 + TAIL_TILES * W, :]
                                 .rearrange("(t p) d -> p t d", p=W)).then_inc(s_xs[1], 16)

                def store(u, it, b):
                    if n in Y:
                        sp.dma_start(rows(Y[n], b), yo[:, u, :, :]).then_inc(s_yst[u], 16)
                    elif n == 4:
                        sp.dma_start(rel_d[bass.ds(b * BC * R, BC * R), :]
                                     .rearrange("(t p r) c -> p t (r c)", p=W, r=R),
                                     hst[:, u, :, :, :].rearrange("p t r c -> p t (r c)")).then_inc(s_yst[u], 16)

                def store_last():
                    if Y.get(n) is not out:
                        return store(1, NI - 1, NB - 1)
                    sp.dma_start(out[r0:r0 + TAIL_TILES * W, :].rearrange("(t p) d -> p t d", p=W),
                                 yo[:, 1, 0:TAIL_TILES, :]).then_inc(s_yst[1], 16)
                    sp.dma_start(out[r0 + TAIL_TILES * W:N, :], yo[0:TAIL_ROWS, 1, TAIL_TILES, :])\
                        .then_inc(s_tail, 16)

                def give(u, it, b, last=False):
                    if n == 2:
                        return
                    wait = wait_reg if not isinstance(b, int) else (lambda e, s, v: e.wait_ge(s, v))
                    wait(sp, s_y[n], b + 1)
                    if n == 4:
                        wait(sp, s_act[n], b + 1)
                    if last:
                        store_last()
                    else:
                        store(u, it, b)
                    wait(sp, s_yst[u], it * 16 + 16 * (1 + NI * stored[n]))
                    sp.sem_inc(s_yfree[n], 1)

                used, credit = (s_tr[4], 0) if n == 4 else (s_xfree[n], 2)
                if n:
                    sp.wait_ge(s_xfree[n - 1], NB + 2)
                for u in range(2):
                    load(u, u)
                sp.wait_ge(used, 1 + credit)
                load(0, 2)
                with sp.Fori(0, NI - 2) as it:
                    for u in range(2):
                        b = it * 2 + u
                        wait_reg(sp, used, b + (2 + credit))
                        load(1 - u, b + 3)
                        give(u, it, b)
                sp.wait_ge(used, NB - 2 + credit)
                load_last()
                for b in range(NB - 4, NB):
                    give(b % 2, b // 2, b, b == NB - 1)
                if n == 2:
                    return
                if n == 5:
                    sp.wait_ge(s_tail, 32)
                sp.sem_inc(s_table, 1)

            with sp.Fori(0, IT - 1) as it:
                for q in range(Q):
                    refill(0, q, it, src_p)
            sp.wait_ge(s_keyst, 32)
            dense_io(0)
            first_indices(1, src_p)
            ea_d = edge_attr.rearrange("(g p s) d -> g p (s d)", p=P, s=S)
            ea_slot = [ea[:, q, :, :].rearrange("p s d -> p (s d)") for q in range(Q)]
            for q in range(Q):
                sp.dma_start(ea_slot[q], ea_d[q, :, :]).then_inc(s_ea[q], 16)
            with sp.Fori(0, IT - 1) as it:
                for q in range(Q):
                    refill(1, q, it, src_p)
                    sp.dma_start(ea_slot[q], ea_d[bass.ds(it * Q + (Q + q), 1), :, :]
                                 .rearrange("a p e -> (a p) e")).then_inc(s_ea[q], 16)
            dense_io(1)
            first_indices(2, src_p)
            with sp.Fori(0, IT - 1) as it:
                for q in range(Q):
                    refill(2, q, it, src_p)
            dense_io(2)
            dense_io(3)
            dense_io(4)
            first_indices(3, key_d)

            def dst_row(u, g):
                sp.dma_start(drow[:, u, :], dst16_d[bass.ds(g * GE, GE)].unsqueeze(0).to_broadcast([128, GE]))\
                    .then_inc(s_drow[u], 16)

            for u in range(2):
                dst_row(u, u)
            sp.dma_start(scan_dst_i, dst_f.rearrange("(p t) -> p t", p=P)).then_inc(s_rld, 16)
            sp.dma_start(scan_type_i, type_f.rearrange("(p t) -> p t", p=P)).then_inc(s_rld, 16)

            def pass3(it, final):
                for q in range(Q):
                    if not (final and q >= Q - 2):
                        wait_reg(sp, s_drused, it * Q + (q + 1))
                        dst_row(q % 2, it * Q + (q + 2))
                    if not final:
                        refill(3, q, it, key_d)

            with sp.Fori(0, IT - 1) as it:
                pass3(it, False)
            pass3(IT - 1, True)
            sp.wait_ge(s_trip, 2)
            sp.dma_start(trip_d.rearrange("(g p e) -> p g e", g=G, p=P),
                         trip[0:P, :, :, :].rearrange("p g s c -> p g (s c)")).then_inc(s_tripd, 16)
            sp.wait_ge(s_tripd, 16)
            sp.dma_start(scan_flat, trip_d.rearrange("(p e) -> p e", p=P)).then_inc(s_scan, 16)
            for k in range(2):
                sp.wait_ge(s_run, 2 * k + 1)
                sp.dma_start(run_out_d[k, :, :], runs[:, :]).then_inc(s_rund, 16)
                sp.wait_ge(s_rund, 64 * k + 16)
                sp.dma_start(run_row.rearrange("a p c -> a (p c)"),
                             run_out_d[k:k + 1, :, :].rearrange("a p c -> a (p c)")).then_inc(s_rund, 16)
                sp.wait_ge(s_run, 2 * k + 2)
                sp.dma_start(run_in_d[k:k + 1, :, :].rearrange("a p c -> a (p c)"),
                             init_row.rearrange("a p c -> a (p c)")).then_inc(s_rund, 16)
                sp.wait_ge(s_rund, 64 * k + 48)
                sp.dma_start(run_in[:, :], run_in_d[k, :, :]).then_inc(s_rund, 16)
            sp.wait_ge(s_alpha, 1)
            sp.dma_start(alpha_d.rearrange("(p t) -> p t", p=P), val).then_inc(s_alphad, 16)
            with sp.If(out_of_order(sp)):
                for k in range(3):
                    with sp.Fori(0, G) as g:
                        for h in range(2):
                            e = g * GE + h * HE
                            sp.sem_clear(s_any_dma)
                            sp.dma_start(any_dst, dst16_d[bass.ds(e, HE)].unsqueeze(0).to_broadcast([128, HE]))\
                                .then_inc(s_any_dma, 16)
                            sp.dma_start(any_type_i, type_f[bass.ds(e, HE)].unsqueeze(0).to_broadcast([128, HE]))\
                                .then_inc(s_any_dma, 16)
                            sp.dma_start(sum_t[:, 0:3 * HE], trip_d[bass.ds(e * 3, 3 * HE)].unsqueeze(0)
                                         .to_broadcast([128, 3 * HE])).then_inc(s_any_dma, 16)
                            sp.wait_ge(s_any_dma, 48)
                            sp.sem_inc(s_any_in, 1)
                            wait_reg(sp, s_any_used, g * 2 + (k * 2 * G + h + 1))
                            if k == 2:
                                sp.dma_start(alpha_d[bass.ds(e, HE)].unsqueeze(0), any_row).then_inc(s_any_dma, 16)
                                sp.wait_ge(s_any_dma, 64)
            sp.dma_start(edge_w[:, 0:G, :], alpha_d.rearrange("(g p s) -> p g s", g=G, p=P)).then_inc(s_alphal, 16)
            he_slot = [gat[:, q, :, :].rearrange("p s c -> p (s c)") for q in range(Q)]
            for q in range(Q):
                sp.dma_start(he_slot[q], he_d[q, :, :]).then_inc(s_held[q], 16)
            with sp.Fori(0, IT - 1) as it:
                for q in range(Q):
                    wait_reg(sp, s_free[q], it + (2 + 4 * IT))
                    sp.dma_start(he_slot[q], he_d[bass.ds(it * Q + (Q + q), 1), :, :]
                                 .rearrange("a p e -> (a p) e")).then_inc(s_held[q], 16)
            dense_io(5)

        @block.gpsimd
        def _(pool):
            nc.gpsimd.memset(ident[:, :], 0.0).then_inc(s_const, 1)
            pool.wait_ge(s_const, 1)
            exact = dict(allow_small_or_imprecise_dtypes=True)
            nc.gpsimd.affine_select(out=ident[:, :], in_=ident[:, :], compare_op=ALU.not_equal, fill=1.0, base=0,
                                    pattern=[[-1, 128]], channel_multiplier=1).then_inc(s_const, 1)
            nc.gpsimd.iota(iota[:, :], pattern=[[1, W]], base=0, channel_multiplier=0, **exact).then_inc(s_const, 1)
            nc.gpsimd.iota(fine_col[:, :], pattern=[[FW, NP // FW]], base=0, channel_multiplier=0, **exact)\
                .then_inc(s_const, 1)
            nc.gpsimd.iota(node_col[:, :], pattern=[[W, NW]], base=0, channel_multiplier=1, **exact)\
                .then_inc(s_const, 1)
            nc.gpsimd.iota(rel_col[:, :], pattern=[[1, R]], base=0, channel_multiplier=0, **exact).then_inc(s_const, 1)

            def gather_pass(n, table, width):
                with pool.Fori(0, IT) as it:
                    for q in range(Q):
                        wait_reg(pool, s_idx[q], it * 16 + 16 * (1 + IT * n))
                        wait_reg(pool, s_free[q], it + (1 + IT * n))
                        for s in range(S):
                            nc.gpsimd.indirect_dma_start(
                                out=gat[:, q, s, 0:width], out_offset=None, in_=table,
                                in_offset=bass.IndirectOffsetOnAxis(ap=idx[:, q, s:s + 1], axis=0),
                            ).then_inc(s_gat[q], 16)

            gather_pass(0, x, D)
            for n, table in ((1, x1_d), (2, x2_d)):
                pool.wait_ge(s_table, n)
                gather_pass(n, table, D)
            pool.wait_ge(s_table, 4)
            pool.wait_ge(s_keyst, 32)
            gather_pass(3, rel_d, HROW)
            pool.wait_ge(s_alphal, 16)
            with pool.Fori(0, IT) as it:
                for q in range(Q):
                    g = it * Q + q
                    alpha = of_group(edge_w, g)
                    wait_reg(pool, s_group, it * Q + (q + 1))
                    wait_reg(pool, s_held[q], it * 16 + 16)
                    nc.gpsimd.tensor_tensor(msg[:, q % 2, :, 0:D], gat[:, q, :, 0:D], by_tile(alpha, D), ALU.mult)
                    wait_reg(pool, s_oh[4][0], it * Q + (q + 1))
                    nc.gpsimd.tensor_tensor(msg[:, q % 2, :, D:HROW], toh[:, q % 2, :, :], by_tile(alpha, R), ALU.mult)\
                        .then_inc(s_msg, 1)
                    wait_reg(pool, s_msg, it * Q + (2 * G + q + 1))
                    pool.sem_inc(s_free[q], 1)
            with pool.Fori(0, NI) as it:
                for u in range(2):
                    wait_reg(pool, s_self, it * 2 + (u + 1))
                    width = R * D // 2
                    v = self_h[u].rearrange("p t r d -> p t (r d)")
                    for step in range(3):
                        nc.gpsimd.tensor_tensor(v[:, :, 0:width], v[:, :, 0:width], v[:, :, width:2 * width], ALU.add)\
                            .then_inc(s_pch, 1)
                        wait_reg(pool, s_pch, it * 6 + (u * 3 + step + 1))
                        width //= 2
                    pool.sem_inc(s_selfsum, 1)

        @block.scalar
        def _(act):
            def square_root(n, b, k, per):
                wait_reg(act, s_sqrt_in[n], b * per + (k + 1))
                if k == per - 1:
                    nc.scalar.activation(r2[:, :], r2[:, :], ACT.Sqrt, bias=eps_col[:, 0:1], scale=1.0 / D)\
                        .then_inc(s_sqrt[n], 1)
                else:
                    nc.scalar.activation(r1[:, :], r1[:, :], ACT.Sqrt).then_inc(s_sqrt[n], 1)

            act.wait_ge(s_vconst, 2)
            act.wait_ge(s_sum[0], 1)
            def stage_in(n, width):
                def copies(it, u, b):
                    wait_reg(act, s_mm[n], b + 1)
                    nc.scalar.activation(stage[0:width, u, :], sum_t[0:width, nodes(b)], ACT.Copy)
                    wait_reg(act, s_tr[n], b + 1)
                    nc.scalar.activation(xt[0:D, u, :], p_tr_flat[0:D, 0:BC], ACT.Copy).then_inc(s_stage[n], 1)
                return copies

            def roots(n, per):
                at = NORMED.index(n)
                nc.scalar.activation(root_table[:, at:at + 1], eps_col[:, 0:1], ACT.Sqrt)

                def take(it, u, b):
                    for k in range(per):
                        square_root(n, b, k, per)
                return take

            two_step(act, stage_in(0, D + 2), roots(0, 2))
            with act.Fori(0, IT) as it:
                for q in range(Q):
                    wait_reg(act, s_pre, it * Q + (q + 1))
                    nc.scalar.activation(msg[:, q % 2, :, 0:D], ea[:, q, :, :], ACT.Relu).then_inc(s_msg, 1)
                    wait_reg(act, s_msg, it * Q + (G + q + 1))
                    act.sem_inc(s_free[q], 1)
            def hidden(it, u, b):
                wait_reg(act, s_mid[1], b + 1)
                for h, bank in ((0, p_a), (1, p_b)):
                    ins = nc.scalar.activation(xt[0:D, u, h * HB:(h + 1) * HB], bank[0:D, u, 0:HB], ACT.Relu,
                                               bias=wt["b1"][:, 0:1])
                ins.then_inc(s_act[1], 1)

            two_step(act, hidden, roots(1, 1))
            with act.Fori(0, NI) as it:
                for u in range(2):
                    b = act.snap(it * 2 + u)
                    wait_reg(act, s_mm[2], b + 1)
                    wait_reg(act, s_tr[2], b + 3)
                    nc.scalar.activation(stage[0:D + 1, u, :], p_tr_flat[0:D + 1, 0:BC], ACT.Copy)\
                        .then_inc(s_stage[2], 1)
            act.wait_ge(s_bn, 1)
            nc.scalar.activation(bnm[:, 2:3], bnm[:, 1:2], ACT.Sqrt, bias=eps_col[0:D, 0:1]).then_inc(s_bnr, 1)
            act.wait_ge(s_bnc, 1)
            def scale_shift(it, u, b):
                wait_reg(act, s_mid[3], b + 1)
                nc.scalar.activation(stage[0:D, u, :], sum_t[0:D, nodes(b)], ACT.Identity,
                                     bias=bnm[:, 4:5], scale=bnm[:, 3:4]).then_inc(s_act[3], 1)

            two_step(act, scale_shift, roots(3, 1))
            act.wait_ge(s_zero, 1)
            def turned(it, u, b):
                wait_reg(act, s_mm[4], b + 1)
                wait_reg(act, s_tr[4], b + 1)
                nc.scalar.activation(xt[0:D, u, :], p_tr_flat[0:D, 0:BC], ACT.Copy).then_inc(s_stage[4], 1)

            def even_tiles(it, u, b):
                wait_reg(act, s_yfree[4], b + 1)
                for t in range(u, BT, 2):
                    m = (BT * u + t) // 2
                    wait_reg(act, s_h[0][0], it * BT + (m + 1))
                    nc.scalar.activation(hst[:, u, t, :, 0:D],
                                         p_a[:, 0, :].rearrange("p (r d) -> p r d", r=R), ACT.Copy)\
                        .then_inc(s_hc[0][0], 1)
                wait_reg(act, s_hc[0][0], it * BT + (m + 2))
                act.sem_inc(s_act[4], 1)

            two_step(act, turned, even_tiles)
            act.wait_ge(s_zero, 2)

            def free_slot(q, it):
                wait_reg(act, s_scan_copy, it * Q + (q + 1))
                wait_reg(act, s_hest[q], it * 16 + 16)
                act.sem_inc(s_free[q], 1)

            with act.Fori(0, IT) as it:
                for q in range(Q):
                    wait_reg(act, s_gat[q], it * 128 + 128 * (1 + 3 * IT))
                    act.dma_start(he_d[bass.ds(it * Q + q, 1), :, :].rearrange("a p e -> (a p) e"),
                                  gat[:, q, :, :].rearrange("p s c -> p (s c)")).then_inc(s_hest[q], 16)
                    nc.scalar.activation(trip[0:P, bass.ds(it * Q + q, 1), :, 0].rearrange("p a s -> p (a s)"),
                                         gat[:, q, :, D], ACT.Copy).then_inc(s_scan_copy, 1)
                    if q:
                        free_slot(q - 1, it)
                free_slot(Q - 1, it)
            act.wait_ge(s_scan_copy, G)
            act.sem_inc(s_trip, 1)
            for k, (dst, srcv) in enumerate(((score, gap), (self_score, self_gap))):
                act.wait_ge(s_ein, k + 1)
                nc.scalar.activation(dst, srcv, ACT.Exp).then_inc(s_eout, 1)
            with act.If(out_of_order(act)):
                act.wait_ge(s_ein, 3)
                nc.scalar.activation(any_den, any_self, ACT.Exp).then_inc(s_eout, 1)
                for k in range(2):
                    with act.Fori(0, G) as g:
                        _, cnt, cum = group_windows(act, 1, g)
                        for h in range(2):
                            with act.Fori(0, cnt) as i:
                                wait_reg(act, s_any_gap[k], cum * 2 + cnt * h + i + 1)
                                nc.scalar.activation(any_val, any_val, ACT.Exp).then_inc(s_any_exp[k], 1)
            act.wait_ge(s_sum[4], 1)
            two_step(act, stage_in(5, HROW), roots(5, 1))

        @block.tensor
        def _(pe):
            pe.wait_ge(s_const, 2)
            pe.wait_ge(s_cols, 1)
            for c in range(4):
                for a in range(2):
                    at = (c % 2) * G + a * SG
                    ins = nc.tensor.matmul(p_a[0:1, c // 2, at:at + SG], wcols[:, c, a:a + 1], ident[0:SG, 0:SG],
                                           start=True, stop=True)
            ins.then_inc(s_rows, 1)
            pe.wait_ge(s_wload, 16 * len(WEIGHTS))
            for r in range(R):
                ins = nc.tensor.matmul(p_b[0:D, 0, 2 * r:2 * r + 2], wt["wrt"][:, r * D:(r + 1) * D],
                                       wt["att"][:, 2 * r:2 * r + 2], start=True, stop=True)
            ins.then_inc(s_sdw, 1)
            pe.wait_ge(s_win, 1)
            pe.wait_ge(s_patch, 64)

            def sum_pass(n, width, ready, lhs):
                with pe.Fori(0, IT) as it:
                    for q in range(Q):
                        _, cnt, cum = group_windows(pe, 0, it * Q + q)
                        ready(it, q)
                        with pe.Fori(0, cnt) as k:
                            for s in range(S):
                                if s % (S // 2) == 0:
                                    pe.wait_ge(s_oh[n][s // (S // 2)], cum + k + 1)
                                ins = nc.tensor.matmul(p_sum[0:width, 0, 0:W], lhs(q, s), oh[:, 0, s, :],
                                                       start=(s == 0), stop=(s == S - 1))
                            ins.then_inc(s_agg[n], 1)

            def transposes(n, width, src):
                for t in range(BT):
                    ins = nc.tensor.transpose(p_tr[0:width, t // 4, (t % 4) * W:(t % 4 + 1) * W], src(t), ident[:, :])
                ins.then_inc(s_tr[n], 1)

            def tile(buf, u, t, k):
                return buf[0:k, u, t * W:(t + 1) * W]

            sum_pass(0, D + 2, lambda it, q: wait_reg(pe, s_msg, it * Q + (q + 1)), lambda q, s: msg[:, q % 2, s, 0:D + 2])
            def turn_rows(n):
                def take(it, u, b):
                    wait_reg(pe, s_xs[u], it * 16 + 16 * (1 + NI * n))
                    wait_reg(pe, s_stage[n], b + 1)
                    transposes(n, D, lambda t: xs[:, u, t, :])
                return take

            def products0(it, u, b):
                wait_reg(pe, s_stage[0], b + 2)
                wait_reg(pe, s_xfree[0], b + 1)
                for t in range(BT):
                    nc.tensor.matmul(p_a[:, u, t * D:(t + 1) * D], tile(xt, u, t, D + 1), wt["ws65"][:, :],
                                     start=True, stop=True)
                    ins = nc.tensor.matmul(p_b[:, u, t * 66:(t + 1) * 66], tile(stage, u, t, 66), wn66[:, :],
                                           start=True, stop=True)
                ins.then_inc(s_mm[0], 1)

            with pe.Fori(0, NI) as it:
                for u in range(2):
                    b = pe.snap(it * 2 + u)
                    turn_rows(0)(it, u, b)
                    products0(it, u, b)
            sum_pass(1, D, lambda it, q: wait_reg(pe, s_msg, it * Q + (G + q + 1)), lambda q, s: msg[:, q % 2, s, 0:D])
            def layer1(it, u, b):
                wait_reg(pe, s_xs[u], it * 16 + 16 * (1 + NI * 1))
                wait_reg(pe, s_stage[1], b + 1)
                transposes(1, D, lambda t: xs[:, u, t, :])
                wait_reg(pe, s_stage[1], b + 2)
                wait_reg(pe, s_xfree[1], b + 1)
                for h, bank in ((0, p_a), (1, p_b)):
                    ins = nc.tensor.matmul(bank[0:D, u, 0:HB], wt["w1"][:, :],
                                           stage[0:D, u, h * HB:(h + 1) * HB], start=True, stop=True)
                ins.then_inc(s_mid[1], 1)

            def layer2(it, u, b):
                wait_reg(pe, s_act[1], b + 1)
                for t in range(BT):
                    ins = nc.tensor.matmul(p_a[:, u, t * D:(t + 1) * D], tile(xt, u, t, D + 1),
                                           wt["w2b"][:, :], start=True, stop=True)
                ins.then_inc(s_mm[1], 1)

            with pe.Fori(0, NI) as it:
                for u in range(2):
                    b = pe.snap(it * 2 + u)
                    layer1(it, u, b)
                    layer2(it, u, b)
            sum_pass(2, D, lambda it, q: wait_reg(pe, s_gat[q], it * 128 + 128 * (1 + 2 * IT)),
                     lambda q, s: gat[:, q, s, 0:D])
            pe.wait_ge(s_sum[2], 1)
            with pe.Fori(0, NI) as it:
                for u in range(2):
                    b = pe.snap(it * 2 + u)
                    wait_reg(pe, s_act[2], b + 1)
                    wait_reg(pe, s_stage[2], b + 1)
                    transposes(2, D + 1, lambda t: xd[:, u, t, :])
                    wait_reg(pe, s_stage[2], b + 2)
                    wait_reg(pe, s_mid[2], b + 1)
                    for h, bank in ((0, p_a), (1, p_b)):
                        nc.tensor.matmul(bank[0:D, u, 0:HB], wd65[:, :], stage[0:D + 1, u, h * HB:(h + 1) * HB],
                                         start=True, stop=False)
                        ins = nc.tensor.matmul(bank[0:D, u, 0:HB], wj66[:, :], sum_t[0:D + 2, nodes(b, HB, h * HB)],
                                               start=False, stop=True)
                    ins.then_inc(s_mm[2], 1)
            with pe.Fori(0, NI) as it:
                for u in range(2):
                    b = pe.snap(it * 2 + u)
                    wait_reg(pe, s_mid[3], b + 3)
                    wait_reg(pe, s_xfree[3], b + 1)
                    for t in range(BT):
                        ins = nc.tensor.transpose(p_b[:, u, t * D:(t + 1) * D], tile(xt, u, t, D), ident[0:D, 0:D])
                    ins.then_inc(s_mm[3], 1)
            def products4(it, u, b):
                wait_reg(pe, s_stage[4], b + 2)
                wait_reg(pe, s_xfree[4], b + 1)
                for t in range(BT):
                    nc.tensor.matmul(p_sum[:, u, t * 16:(t + 1) * 16], tile(xt, u, t, D), sdw[:, :],
                                     start=True, stop=True)
                for t in range(BT):
                    k, m = (BT * u + t) % 2, (BT * u + t) // 2
                    wait_reg(pe, s_hc[0][k], it * BT + (m + 1))
                    ins = nc.tensor.matmul(p_a[:, k, :], tile(xt, u, t, D), wt["wcat"][:, :],
                                           start=True, stop=True)
                    ins.then_inc(s_h[0][k], 1)
                wait_reg(pe, s_h[0][k], it * BT + (m + 1))
                pe.sem_inc(s_mm[4], 1)

            two_step(pe, turn_rows(4), products4)
            with pe.Fori(0, IT) as it:
                for q in range(Q):
                    first, cnt, cum = group_windows(pe, 1, it * Q + q)
                    with pe.Fori(0, cnt) as k:
                        wait_reg(pe, s_oh[3][0], cum + k + 1)
                        w = within(first + k, NW - 1)
                        table = dtab3[:, bass.ds(w, 1), :, :, :].rearrange("p a c k r -> p (a c k r)")
                        for s in range(S):
                            ins = nc.tensor.matmul(p_sum[:, 0, s * 6 * R:(s + 1) * 6 * R], oht_tile[:, :, s], table,
                                                   start=True, stop=True)
                        ins.then_inc(s_agg[3], 1)
            with pe.If(out_of_order(pe)):
                with pe.Fori(0, G) as g:
                    for h in range(2):
                        wait_reg(pe, s_any_acc, g * 2 + (h + 1))
                        nc.tensor.matmul(p_a[0:1, 0, 0:HE], ones_col[:, :], any_alpha, start=True, stop=True)\
                            .then_inc(s_any_sum, 1)
            with pe.Fori(0, IT) as it:
                for q in range(Q):
                    u = q % 2

                    def window(ready):
                        for s in range(S):
                            if s % (S // 2) == 0:
                                ready(s // (S // 2))
                            ins = nc.tensor.matmul(p_sum[0:HROW, u, 0:W], msg[:, u, s, :], oh[:, u, s, :],
                                                   start=(s == 0), stop=(s == S - 1))
                        ins.then_inc(s_agg[4], 1)

                    _, cnt, cum = group_windows(pe, 0, it * Q + q)
                    wait_reg(pe, s_msg, it * Q + (2 * G + q + 1))
                    window(lambda h: wait_reg(pe, s_oh[4][h], it * Q + (q + 1)))
                    with pe.If(cnt > 1):
                        with pe.Fori(1, cnt) as k:
                            window(lambda h: None if h else wait_reg(pe, s_more, cum + k + 1))
            def products5(it, u, b):
                wait_reg(pe, s_stage[5], b + 2)
                wait_reg(pe, s_xfree[5], b + 1)
                for t in range(BT):
                    nc.tensor.matmul(p_a[:, u, t * D:(t + 1) * D], tile(xt, u, t, D + 1), wself65[:, :],
                                     start=True, stop=True)
                    ins = nc.tensor.matmul(p_b[:, u, t * HROW:(t + 1) * HROW], tile(stage, u, t, HROW),
                                           ident[0:HROW, 0:HROW], start=True, stop=True)
                ins.then_inc(s_mid[5], 1)
                for t in range(BT):
                    k, m = (BT * u + t) % 2, (BT * u + t) // 2
                    wait_reg(pe, s_hc[1][k], it * BT + (m + 1))
                    ins = nc.tensor.matmul(p_sum[:, k, :], tile(xt, u, t, D), wt["wcat"][:, :],
                                           start=True, stop=True)
                    ins.then_inc(s_h[1][k], 1)
                wait_reg(pe, s_h[1][k], it * BT + (m + 1))
                pe.sem_inc(s_mm[5], 1)

            two_step(pe, turn_rows(5), products5)

        @block.vector
        def _(dve):
            ch = Chain(dve, s_vch)
            vec = nc.vector

            for q in range(Q):
                dve.sem_inc(s_free[q], 1)
            for group, credit in ((s_xfree, 2), (s_mm, 2), (s_stage.values(), 1), (s_yfree.values(), 2)):
                for s in group:
                    dve.sem_inc(s, credit)
            for s in (s_tr[2], s_mid[2], s_mid[3]):
                dve.sem_inc(s, 2)
            for n in range(2):
                for k in range(2):
                    dve.sem_inc(s_hc[n][k], 1)
            vec.memset(eps_col[:, :], EPS_LN)
            vec.memset(wones[:, :], 1.0)
            vec.memset(xt[D:D + 1, :, :], 1.0)
            vec.memset(msg[:, :, :, D + 1], 1.0).then_inc(s_vconst, 1)
            vec.memset(xs[:, :, :, :], 0.0).then_inc(s_vconst, 1)

            ch.start()
            dve.wait_ge(s_load[0], 16)
            ch.add(vec.tensor_reduce(out=ends_g[:, 0, :], in_=stat_i, op=ALU.min, axis=AX.X))
            ch(vec.tensor_reduce(out=ends_g[:, 1, :], in_=stat_i, op=ALU.max, axis=AX.X))
            ch(vec.tensor_copy(ends_i[:, 0:2, :], ends_g[:, :, :]))
            for table, shift in ((0, 5), (1, 7)):
                lo, steps = ends_i[:, 2, :], ends_i[:, 3, :]
                ch(vec.tensor_single_scalar(lo, ends_i[:, 0, :], shift, op=ALU.arith_shift_right))
                ch(vec.tensor_copy(wcols[:, 2 * table, :], lo))
                ch(vec.scalar_tensor_tensor(out=steps, in0=wcols[:, 2 * table, :], scalar=-float(1 << shift),
                                            in1=ends_g[:, 1, :], op0=ALU.mult, op1=ALU.add))
                ch(vec.tensor_single_scalar(steps, steps, 7, op=ALU.arith_shift_right))
                ch(vec.tensor_copy(wcols[:, 2 * table + 1, :], steps))
            dve.sem_inc(s_cols, 1)
            dve.wait_ge(s_load[1], 16)
            vec.memset(dstf[:, G, :], 0.0)
            vec.memset(win[:, :, G], 0)
            vec.tensor_copy(dstf[:, 0:G, :].rearrange("p g s -> p (g s)"), dst_i)
            dve.wait_ge(s_rows, 1)
            ch(vec.tensor_copy(wrows[:, 0:2, :], p_a[0:1, 0, 0:2 * G].rearrange("a (c g) -> a c g", c=2)))
            ch(vec.tensor_copy(wrows[:, 2:4, :], p_a[0:1, 1, 0:2 * G].rearrange("a (c g) -> a c g", c=2)))
            for table in range(2):
                first, more, before, upto_g = (wrows[:, 2 * table, :], wrows[:, 2 * table + 1, :],
                                               wrows[:, 4, :], wrows[:, 5, :])
                ch(vec.tensor_scalar_add(upto_g, more, 1.0))
                ch(vec.tensor_tensor_scan(before, wones[:, :], upto_g, 0.0, ALU.mult, ALU.add))
                ch(vec.tensor_tensor(before, before, upto_g, ALU.subtract))
                for c, rowv in enumerate((first, more, before)):
                    ch.add(vec.tensor_copy(wint[:, c, :], rowv))
                ch.wait()
                ch(vec.tensor_single_scalar(wint[:, 0, :], wint[:, 0, :], 7, op=ALU.logical_shift_left))
                ch(vec.tensor_single_scalar(wint[:, 2, :], wint[:, 2, :], 16, op=ALU.logical_shift_left))
                ch(vec.tensor_tensor(wint[:, 0, :], wint[:, 0, :], wint[:, 1, :], ALU.bitwise_or))
                ch(vec.tensor_tensor(win[:, table, 0:G], wint[:, 0, :], wint[:, 2, :], ALU.bitwise_or))
            dve.sem_inc(s_win, 1)

            dve.wait_ge(s_const, 6)
            dve.wait_ge(s_wload, 16 * len(WEIGHTS))
            ch.add(vec.tensor_copy(wn66[:, :], ident[0:D + 2, 0:D + 2]))
            ch(vec.memset(wj66[:, :], 0.0))
            ch.add(vec.tensor_copy(wj66[0:D, :], wt["wj"][:, :]))
            ch.add(vec.tensor_tensor(wd65[0:D, :], wt["wi"][:, :], wt["wj"][:, :], ALU.subtract))
            ch(vec.tensor_reduce(out=brow[0:1, :], in_=wt["rbias"][0:1, :].rearrange("a (r d) -> a d r", r=R),
                                 op=ALU.add, axis=AX.X))
            ch(vec.tensor_tensor(brow[0:1, :], brow[0:1, :], wt["bself"][0:1, :], ALU.add))
            dve.sem_inc(s_prep, 1)
            dve.wait_ge(s_sdw, 1)
            ch(vec.tensor_copy(sdw[:, :].rearrange("d (c r) -> d c r", c=2),
                               p_b[0:D, 0, 0:2 * R].rearrange("d (r c) -> d c r", c=2)))
            dve.wait_ge(s_load[3], 48)
            vec.memset(typef[:, G, :], 0.0)
            ch.add(vec.tensor_copy(typef[:, 0:G, :].rearrange("p g s -> p (g s)"), type_i))
            ch.add(vec.scalar_tensor_tensor(out=src_i, in0=src_i, scalar=float(R), in1=type_i, op0=ALU.mult, op1=ALU.add))
            ch(vec.tensor_copy(dst16, dstn_i))
            dve.sem_inc(s_key, 1)

            def sum_windows(n, width, g, first, cnt, cum):
                with dve.Fori(0, cnt) as k:
                    at = dve.snap(within(first + k * (W // FW), (N - 1) // FW))
                    half = S // 2
                    for h in range(2):
                        dst = dstf[:, bass.ds(g, 1), h * half:(h + 1) * half].rearrange("p a s -> p (a s)")
                        vec.scalar_tensor_tensor(
                            out=oh[:, 0, h * half:(h + 1) * half, :], in0=bc(dst.unsqueeze(2), P, half, W),
                            scalar=fine_col[0:P, bass.ds(at, 1)], in1=bc(iota[0:P, :].unsqueeze(1), P, half, W),
                            op0=ALU.subtract, op1=ALU.is_equal).then_inc(s_oh[n][h], 1)
                    wait_reg(dve, s_agg[n], cum + k + 1)
                    part = sum_t[0:width, bass.ds(at * FW, W)]
                    vec.tensor_tensor(part, part, p_sum[0:width, 0, 0:W], ALU.add).then_inc(s_acc, 1)

            def piped_pass(width):
                half = S // 2

                def one_hot(u, g, at, h, dones):
                    dst = dstf[:, bass.ds(g, 1), h * half:(h + 1) * half].rearrange("p a s -> p (a s)")
                    ins = vec.scalar_tensor_tensor(
                        out=oh[:, u, h * half:(h + 1) * half, :], in0=bc(dst.unsqueeze(2), P, half, W),
                        scalar=fine_col[0:P, bass.ds(at, 1)], in1=bc(iota[0:P, :].unsqueeze(1), P, half, W),
                        op0=ALU.subtract, op1=ALU.is_equal)
                    if dones[h] is not None:
                        ins.then_inc(dones[h], 1)

                def add(u, at, done):
                    wait_reg(dve, s_agg[4], done)
                    part = sum_t[0:width, bass.ds(at * FW, W)]
                    vec.tensor_tensor(part, part, p_sum[0:width, u, 0:W], ALU.add).then_inc(s_acc, 1)

                def first_window(u, g, at):
                    vec.tensor_tensor(toh[:, u, :, :], by_tile(of_group(typef, g), R),
                                      bc(rel_col[0:P, :].unsqueeze(1), P, S, R), ALU.is_equal)
                    for h in range(2):
                        one_hot(u, g, at, h, s_oh[4])

                for _ in range(2):
                    dve.sem_inc(s_group, 1)
                ch.start()
                ch(vec.memset(sum_t[0:width, :], 0.0))
                first_window(0, 0, within(group_windows(dve, 0, 0)[0], (N - 1) // FW))
                with dve.Fori(0, IT) as it:
                    following = group_windows(dve, 0, it * Q)
                    for q in range(Q):
                        g = it * Q + q
                        first, cnt, cum = following
                        following = group_windows(dve, 0, g + 1)
                        first_window(1 - q % 2, g + 1, within(following[0], (N - 1) // FW))
                        wait_reg(dve, s_oh[4][1], it * Q + (q + 2))
                        add(q % 2, within(first, (N - 1) // FW), cum + 1)
                        dve.sem_inc(s_more, 1)
                        with dve.If(cnt > 1):
                            with dve.Fori(1, cnt) as k:
                                at = dve.snap(within(first + k * (W // FW), (N - 1) // FW))
                                for h in range(2):
                                    one_hot(q % 2, g, at, h, (None, s_more))
                                add(q % 2, at, cum + k + 1)
                        dve.sem_inc(s_group, 1)
                vec.memset(r1[:, :], 0.0).then_inc(s_sum[4], 1)

            def sum_pass(n, width, prepare, done=None):
                ch.start()
                ch(vec.memset(sum_t[0:max(width, D + 2), :], 0.0))
                with dve.Fori(0, IT) as it:
                    for q in range(Q):
                        g = it * Q + q
                        first, cnt, cum = group_windows(dve, 0, g)
                        prepare(it, q, g)
                        sum_windows(n, width, g, first, cnt, cum)
                        if done:
                            done(q)
                vec.memset(r1[:, :], 0.0).then_inc(s_sum[n], 1)

            def weighted(it, q, g):
                wait_reg(dve, s_gat[q], it * 16 * S + 16 * S)
                w = of_group(edge_w, g)
                vec.tensor_copy(msg[:, q % 2, :, D], w)
                vec.tensor_tensor(msg[:, q % 2, :, 0:D], gat[:, q, :, 0:D], by_tile(w, D), ALU.mult)\
                    .then_inc(s_msg, 1)
                wait_reg(dve, s_msg, it * Q + (q + 1))
                dve.sem_inc(s_free[q], 1)

            def layer_norm(n, b, u):
                ch(vec.tensor_reduce(out=r2[:, :], in_=ya[:, :, :], op=ALU.add, axis=AX.X))
                ch(vec.scalar_tensor_tensor(out=ya[:, :, :], in0=bc(r2[:, :].unsqueeze(2), 128, BT, D), scalar=-1.0 / D,
                                            in1=ya[:, :, :], op0=ALU.mult, op1=ALU.add))
                ch(vec.tensor_tensor(yb[:, :, :], ya[:, :, :], ya[:, :, :], ALU.mult))
                ch(vec.tensor_reduce(out=r2[:, :], in_=yb[:, :, :], op=ALU.add, axis=AX.X))
                dve.sem_inc(s_sqrt_in[n], 1)
                wait_reg(dve, s_sqrt[n], b * (2 if n == 0 else 1) + (2 if n == 0 else 1))
                ch(vec.reciprocal(r2[:, :], r2[:, :]))
                wait_reg(dve, s_yfree[n], b + 1)
                vec.tensor_tensor(yo[:, u, :, :], ya[:, :, :], bc(r2[:, :].unsqueeze(2), 128, BT, D), ALU.mult)\
                    .then_inc(s_y[n], 1)
                wait_reg(dve, s_y[n], b + 1)

            def bank(p, u, width):
                return p[:, u, 0:BT * width].rearrange("p (t d) -> p t d", t=BT)

            dve.wait_ge(s_load[2], 16)
            sum_pass(0, D + 2, weighted)
            with dve.Fori(0, NI) as it:
                for u in range(2):
                    b = dve.snap(it * 2 + u)
                    ch.start()
                    wait_reg(dve, s_mm[0], b + 3)
                    own, nb = bank(p_a, u, D), bank(p_b, u, D + 2)
                    ch.add(vec.tensor_copy(deg[:, bass.ds(b * BT, BT)], nb[:, :, D + 1]))
                    ch(vec.tensor_scalar_max(r1[:, :], nb[:, :, D], 1e-8))
                    ch(vec.reciprocal(r1[:, :], r1[:, :]))
                    ch(vec.tensor_tensor(ya[:, :, :], nb[:, :, 0:D], bc(r1[:, :].unsqueeze(2), 128, BT, D), ALU.mult))
                    ch(vec.tensor_tensor(ya[:, :, :], ya[:, :, :], own, ALU.add))
                    ch(vec.tensor_tensor(yb[:, :, :], ya[:, :, :], ya[:, :, :], ALU.mult))
                    ch(vec.tensor_reduce(out=r1[:, :], in_=yb[:, :, :], op=ALU.add, axis=AX.X))
                    dve.sem_inc(s_sqrt_in[0], 1)
                    wait_reg(dve, s_sqrt[0], b * 2 + 1)
                    ch(vec.tensor_scalar_max(r1[:, :], r1[:, :], 1e-12))
                    ch(vec.reciprocal(r1[:, :], r1[:, :]))
                    ch(vec.tensor_tensor(ya[:, :, :], ya[:, :, :], bc(r1[:, :].unsqueeze(2), 128, BT, D), ALU.mult))
                    wait_reg(dve, s_xs[u], it * 16 + 16 * (1 + NI * 0))
                    ch(vec.tensor_tensor(ya[:, :, :], ya[:, :, :], xs[:, u, :, :], ALU.add))
                    dve.sem_inc(s_xfree[0], 1)
                    layer_norm(0, b, u)

            def prepare1(it, q, g):
                wait_reg(dve, s_gat[q], it * 128 + 128 * (1 + IT))
                wait_reg(dve, s_ea[q], it * 16 + 16)
                vec.tensor_tensor(ea[:, q, :, :], ea[:, q, :, :], gat[:, q, :, 0:D], ALU.add).then_inc(s_pre, 1)

            sum_pass(1, D, prepare1)
            def add_sums(it, u, b):
                wait_reg(dve, s_tr[1], b + 1)
                vec.tensor_tensor(stage[0:D, u, :], p_tr_flat[0:D, 0:BC], sum_t[0:D, nodes(b)], ALU.add)\
                    .then_inc(s_stage[1], 1)

            def finish(n, p):
                def residual(it, u, b):
                    ch.start()
                    wait_reg(dve, s_mm[n], b + 3)
                    wait_reg(dve, s_xs[u], it * 16 + 16 * (1 + NI * n))
                    ch(vec.tensor_tensor(ya[:, :, :], bank(p, u, D), xs[:, u, :, :], ALU.add))
                    dve.sem_inc(s_xfree[n], 1)
                    layer_norm(n, b, u)
                return residual

            two_step(dve, add_sums, finish(1, p_a))

            def prepare2(it, q, g):
                pass

            sum_pass(2, D, prepare2, lambda q: dve.sem_inc(s_free[q], 1))

            def scale_rows(it, u, b):
                wait_reg(dve, s_xs[u], it * 16 + 16 * (1 + NI * 2))
                wait_reg(dve, s_tr[2], b + 1)
                dv = deg[:, bass.ds(b * BT, BT)]
                vec.tensor_copy(xd[:, u, :, D], dv)
                vec.tensor_tensor(xd[:, u, :, 0:D], xs[:, u, :, :], bc(dv.unsqueeze(2), 128, BT, D), ALU.mult)\
                    .then_inc(s_act[2], 1)
                wait_reg(dve, s_act[2], b + 1)
                dve.sem_inc(s_xfree[2], 1)

            def keep_h(it, u, b):
                wait_reg(dve, s_mm[2], b + 3)
                vec.tensor_copy(sum_t[0:D, nodes(b, HB)], p_a[0:D, u, 0:HB])
                vec.tensor_copy(sum_t[0:D, nodes(b, HB, HB)], p_b[0:D, u, 0:HB]).then_inc(s_mid[2], 1)

            two_step(dve, scale_rows, keep_h)
            dve.wait_ge(s_mid[2], NB + 2)
            ch.start()
            for c in range(25):
                ch.add(vec.bn_stats(out=bn[:, c, :], in_=sum_t[0:D, c * (N // 25):(c + 1) * (N // 25)]))
            ch.wait()
            ch(vec.bn_aggr(out=bnm[:, 0:2], in_=bn[:, :, :].rearrange("d c k -> d (c k)")))
            dve.sem_inc(s_bn, 1)
            dve.wait_ge(s_bnr, 1)
            ch(vec.reciprocal(bnm[:, 3:4], bnm[:, 2:3]))
            ch(vec.tensor_tensor(bnm[:, 3:4], bnm[:, 3:4], wt["gamma"][:, :], ALU.mult))
            ch(vec.tensor_tensor(bnm[:, 4:5], bnm[:, 0:1], bnm[:, 3:4], ALU.mult))
            ch(vec.tensor_tensor(bnm[:, 4:5], wt["beta"][:, :], bnm[:, 4:5], ALU.subtract))
            dve.sem_inc(s_bnc, 1)
            def leaky(it, u, b):
                wait_reg(dve, s_act[3], b + 1)
                vec.scalar_tensor_tensor(out=xt[0:D, u, :], in0=stage[0:D, u, :], scalar=0.01,
                                         in1=stage[0:D, u, :], op0=ALU.mult, op1=ALU.max).then_inc(s_mid[3], 1)

            two_step(dve, leaky, finish(3, p_b))

            ch.start()
            dve.wait_ge(s_y[3], NB)
            for u in range(2):
                ch(vec.memset(hst[:, u, :, :, D + 1:HROW], 0.0))
            dve.sem_inc(s_zero, 1)
            with dve.Fori(0, NI) as it:
                for u in range(2):
                    b = dve.snap(it * 2 + u)
                    ch.start()
                    wait_reg(dve, s_yfree[4], b + 1)
                    for t in range(1 - u, BT, 2):
                        m = (BT * u + t) // 2
                        wait_reg(dve, s_h[0][1], it * BT + (m + 1))
                        vec.tensor_copy(hst[:, u, t, :, 0:D], p_a[:, 1, :].rearrange("p (r d) -> p r d", r=R))\
                            .then_inc(s_hc[0][1], 1)
                    wait_reg(dve, s_mm[4], b + 3)
                    ch(vec.tensor_copy(sd[:, :, :], bank(p_sum, u, 2 * R)))
                    dve.sem_inc(s_xfree[4], 1)
                    table = dtab[:, bass.ds(b * BT, BT), :]
                    ch.add(vec.tensor_copy(hst[:, u, :, :, D], sd[:, :, 0:R]))
                    ch.add(vec.tensor_copy(table[:, :, 0:R], sd[:, :, R:2 * R]))
                    ch(vec.tensor_tensor(sd[:, :, 0:R], sd[:, :, 0:R], sd[:, :, R:2 * R], ALU.add))
                    ch(vec.scalar_tensor_tensor(out=table[:, :, R:2 * R], in0=sd[:, :, 0:R], scalar=0.2,
                                                in1=sd[:, :, 0:R], op0=ALU.mult, op1=ALU.max))
                    wait_reg(dve, s_hc[0][1], it * BT + (m + 2))
                    dve.sem_inc(s_y[4], 1)

            ch.start()
            ch(vec.memset(oht[:, GE:S * W], 0.0))
            table = dtab[:, :, :].rearrange("p w (c r) -> p w c r", c=2)
            for part in range(3):
                ch(vec.tensor_copy(dtab3[:, :, :, part, :], table))
                if part < 2:
                    ch(vec.tensor_tensor(table, table, dtab3[:, :, :, part, :], ALU.subtract))
            ch(vec.memset(trip_flat, 0.0))
            dve.sem_inc(s_zero, 1)
            dve.wait_ge(s_table, 4)
            dve.wait_ge(s_rld, 32)
            ch.add(vec.tensor_copy(val, scan_dst_i))
            ch(vec.tensor_copy(rtype, scan_type_i))
            ch.add(vec.tensor_copy(ends[:, 0:1], val[:, 0:1]))
            ch.add(vec.tensor_copy(ends[:, 1:2], val[:, T - 1:T]))
            ch(vec.tensor_tensor(brk_b[:, 0:T - 1], val[:, 1:T], val[:, 0:T - 1], ALU.is_lt))
            ch(vec.tensor_reduce(out=ends[:, 2:3], in_=brk_b[:, 0:T - 1], op=ALU.max, axis=AX.X))
            ch.add(vec.tensor_tensor(brk_f[:, 1:T], val[:, 1:T], val[:, 0:T - 1], ALU.is_equal))
            ch.add(vec.memset(brk_f[:, 0:1], 1.0))
            ch.add(vec.tensor_tensor(brk_b[:, 0:T - 1], val[:, 1:T], val[:, 0:T - 1], ALU.is_equal))
            ch(vec.memset(brk_b[:, T - 1:T], 1.0))
            ch.add(vec.tensor_scalar(lead, val, ends[:, 0:1], None, ALU.is_equal))
            ch(vec.tensor_scalar(trail, val, ends[:, 1:2], None, ALU.is_equal))
            masks = (brk_f, brk_b, lead, trail)
            for m_ in masks:
                ch.add(vec.tensor_scalar(m_, m_, 1.0, BIG, ALU.subtract, ALU.mult))
            ch(vec.tensor_copy(runs[:, 2 * R:2 * R + 2], ends[:, 0:2]))
            ch.add(vec.scalar_tensor_tensor(out=runs[:, 2 * R:2 * R + 1], in0=ends[:, 2:3], scalar=-float(2 * N),
                                            in1=ends[:, 0:1], op0=ALU.mult, op1=ALU.add))
            ch.wait()

            with dve.Fori(0, IT) as it:
                for q in range(Q):
                    g = it * Q + q
                    first, cnt, cum = group_windows(dve, 1, g)
                    ch.start()
                    ch(vec.tensor_tensor(toh[:, 0, :, :], by_tile(of_group(typef, g), R),
                                         bc(rel_col[0:P, :].unsqueeze(1), P, S, R), ALU.is_equal))
                    wait_reg(dve, s_drow[q % 2], it * 32 + 16 * (1 + q // 2))
                    with dve.Fori(0, cnt) as k:
                        w = dve.snap(within(first + k, NW - 1))
                        ch2 = Chain(dve, s_vch)
                        ch2.start()
                        vec.tensor_scalar(oht[:, 0:GE], drow[:, q % 2, :], node_col[:, bass.ds(w, 1)], None,
                                          ALU.is_equal).then_inc(s_oh[3][0], 1)
                        wait_reg(dve, s_agg[3], cum + k + 1)
                        ch2(vec.tensor_tensor(
                            sel[:, :, :, :].rearrange("p s c (k r) -> p s (c k) r", k=3),
                            p_sum[0:P, 0, 0:S * 6 * R].rearrange("p (s c r) -> p s c r", s=S, c=6),
                            bc(toh[:, 0, :, :].unsqueeze(2), P, S, 6, R), ALU.mult))
                        ch2(vec.tensor_reduce(out=sel2[:, :, :], in_=sel[:, :, :, :], op=ALU.add, axis=AX.X))
                        part = trip[0:P, bass.ds(g, 1), :, 1:3].rearrange("p a s c -> p (a s) c")
                        ch2(vec.tensor_tensor(part, part, sel2[:, :, :], ALU.add))
                    dve.sem_inc(s_drused, 1)
            dve.sem_inc(s_trip, 1)

            ch.start()
            dve.wait_ge(s_scan, 16)
            ch(vec.tensor_tensor(score, score, gap, ALU.add))
            ch(vec.scalar_tensor_tensor(out=score, in0=score, scalar=0.2, in1=score, op0=ALU.mult, op1=ALU.max))
            ch(vec.tensor_copy(best, self_score))

            def exchange(k, maximum):
                neutral = -BIG if maximum else 0.0
                dve.wait_ge(s_rund, 64 * k + 32)
                firsts, lasts = run_row[:, :, 2 * R], run_row[:, :, 2 * R + 1]
                joined, through = link_row[:, 0, :], link_row[:, 1, :]
                ch(vec.memset(link_row[:, :, :], 0.0))
                ch.add(vec.tensor_tensor(joined[:, 1:P], firsts[:, 1:P], lasts[:, 0:P - 1], ALU.is_equal))
                ch(vec.tensor_tensor(through[:, 0:P], firsts, lasts, ALU.is_equal))
                pf, pb = link_row[:, 2, 0:P], link_row[:, 3, 0:P]
                ch.add(vec.tensor_tensor(pf, joined[:, 0:P], through[:, 0:P], ALU.mult))
                ch(vec.tensor_tensor(pb, joined[:, 1:P + 1], through[:, 0:P], ALU.mult))
                if maximum:
                    ch(vec.tensor_scalar(link_row[:, 0, :], link_row[:, 0, :], 1.0, BIG, ALU.subtract, ALU.mult))
                    ch(vec.tensor_scalar(link_row[:, 2:4, :], link_row[:, 2:4, :], 1.0, BIG, ALU.subtract, ALU.mult))
                op0, op1 = (ALU.add, ALU.max) if maximum else (ALU.mult, ALU.add)
                for r in range(R):
                    ch.add(vec.tensor_tensor_scan(carry_row[:, :, r], pf, run_row[:, :, r], neutral, op0, op1))
                    ch.add(vec.tensor_tensor_scan(carry_row[:, ::-1, R + r], pb[:, ::-1], run_row[:, ::-1, R + r],
                                                  neutral, op0, op1))
                ch.wait()
                link_op = ALU.add if maximum else ALU.mult
                ch.add(vec.memset(init_row[:, 0:1, 0:R], neutral))
                ch.add(vec.memset(init_row[:, P - 1:P, R:2 * R], neutral))
                ch.add(vec.tensor_tensor(init_row[:, 1:P, 0:R], carry_row[:, 0:P - 1, 0:R],
                                         bc(joined[:, 1:P].unsqueeze(2), 1, P - 1, R), link_op))
                ch(vec.tensor_tensor(init_row[:, 0:P - 1, R:2 * R], carry_row[:, 1:P, R:2 * R],
                                     bc(joined[:, 1:P].unsqueeze(2), 1, P - 1, R), link_op))
                dve.sem_inc(s_run, 1)
                dve.wait_ge(s_rund, 64 * k + 64)

            ends_of = ((trail, 0), (lead, R))
            with dve.Fori(0, R) as r:
                ch2 = Chain(dve, s_vch)
                ch2.start()
                ch2(vec.tensor_scalar(off, rtype, rel_col[0:P, bass.ds(r, 1)], -BIG, ALU.not_equal, ALU.mult))
                ch2(vec.tensor_tensor(val, score, off, ALU.add))
                for k, (mask, at) in enumerate(ends_of):
                    ch2(vec.tensor_tensor_reduce(out=fwd, in0=val, in1=mask, scale=1.0, scalar=-3 * BIG, op0=ALU.add,
                                                 op1=ALU.max, accum_out=ends[:, k:k + 1]))
                    ch2(vec.tensor_copy(runs[:, bass.ds(r + at, 1)], ends[:, k:k + 1]))
            ch.start()
            dve.sem_inc(s_run, 1)
            exchange(0, True)
            with dve.Fori(0, R) as r:
                ch2 = Chain(dve, s_vch)
                ch2.start()
                ch2(vec.tensor_scalar(off, rtype, rel_col[0:P, bass.ds(r, 1)], -BIG, ALU.not_equal, ALU.mult))
                ch2(vec.tensor_tensor(val, score, off, ALU.add))
                ch2.add(vec.tensor_tensor_scan(fwd, brk_f, val, run_in[:, bass.ds(r, 1)], ALU.add, ALU.max))
                ch2(vec.tensor_tensor_scan(bwd[:, ::-1], brk_b[:, ::-1], val[:, ::-1], run_in[:, bass.ds(r + R, 1)],
                                           ALU.add, ALU.max))
                ch2(vec.tensor_tensor(fwd, fwd, bwd, ALU.max))
                ch2(vec.tensor_tensor(fwd, fwd, off, ALU.add))
                ch2(vec.tensor_tensor(best, best, fwd, ALU.max))
            ch.start()
            ch(vec.tensor_tensor(gap, score, best, ALU.subtract))
            dve.sem_inc(s_ein, 1)
            ch.add(vec.tensor_tensor(self_gap, self_score, best, ALU.subtract))
            for m_ in masks:
                ch.add(vec.tensor_single_scalar(m_, m_, 0.0, op=ALU.is_equal))
            ch.wait()
            dve.sem_inc(s_ein, 1)
            dve.wait_ge(s_eout, 2)
            ch(vec.tensor_copy(best, self_score))
            with dve.Fori(0, R) as r:
                ch2 = Chain(dve, s_vch)
                ch2.start()
                ch2(vec.scalar_tensor_tensor(out=val, in0=rtype, scalar=rel_col[0:P, bass.ds(r, 1)], in1=score,
                                             op0=ALU.is_equal, op1=ALU.mult))
                for k, (mask, at) in enumerate(ends_of):
                    ch2(vec.tensor_tensor_reduce(out=fwd, in0=val, in1=mask, scale=1.0, scalar=0.0, op0=ALU.mult,
                                                 op1=ALU.add, accum_out=ends[:, k:k + 1]))
                    ch2(vec.tensor_copy(runs[:, bass.ds(r + at, 1)], ends[:, k:k + 1]))
            ch.start()
            dve.sem_inc(s_run, 1)
            exchange(1, False)
            with dve.Fori(0, R) as r:
                ch2 = Chain(dve, s_vch)
                ch2.start()
                ch2(vec.scalar_tensor_tensor(out=val, in0=rtype, scalar=rel_col[0:P, bass.ds(r, 1)], in1=score,
                                             op0=ALU.is_equal, op1=ALU.mult))
                ch2.add(vec.tensor_tensor_scan(fwd, brk_f, val, run_in[:, bass.ds(r, 1)], ALU.mult, ALU.add))
                ch2(vec.tensor_tensor_scan(bwd[:, ::-1], brk_b[:, ::-1], val[:, ::-1], run_in[:, bass.ds(r + R, 1)],
                                           ALU.mult, ALU.add))
                ch2(vec.tensor_tensor(fwd, fwd, bwd, ALU.add))
                ch2(vec.tensor_tensor(fwd, fwd, val, ALU.subtract))
                ch2(vec.scalar_tensor_tensor(out=fwd, in0=rtype, scalar=rel_col[0:P, bass.ds(r, 1)], in1=fwd,
                                             op0=ALU.is_equal, op1=ALU.mult))
                ch2(vec.tensor_tensor(best, best, fwd, ALU.add))
            ch.start()
            ch(vec.reciprocal(best, best))
            ch(vec.tensor_tensor(val, score, best, ALU.mult))
            ch(vec.tensor_tensor(link_row[:, 0, 0:P - 1], run_row[:, 1:P, 2 * R], run_row[:, 0:P - 1, 2 * R + 1],
                                 ALU.is_lt))
            ch(vec.tensor_single_scalar(link_row[:, 1, 0:P], run_row[:, :, 2 * R], 0.0, op=ALU.is_lt))
            ch.add(vec.tensor_reduce(out=falls[:, 0:1], in_=link_row[:, 0, 0:P - 1], op=ALU.max, axis=AX.X))
            ch(vec.tensor_reduce(out=falls[:, 1:2], in_=link_row[:, 1, 0:P], op=ALU.max, axis=AX.X))
            ch(vec.tensor_tensor(falls[:, 0:1], falls[:, 0:1], falls[:, 1:2], ALU.max))
            ch(vec.tensor_scalar_add(falls[:, 0:1], falls[:, 0:1], 1.0))
            ch(vec.tensor_copy(falls_i[:, :], falls[:, 0:1]))
            ch(vec.memset(ones_col[:, :], 1.0))
            dve.sem_inc(s_alpha, 1)

            def any_order(k):
                with dve.Fori(0, G) as g:
                    first, cnt, cum = group_windows(dve, 1, g)
                    for h in range(2):
                        ch.start()
                        wait_reg(dve, s_any_in, g * 2 + (k * 2 * G + h + 1))
                        ch(vec.tensor_copy(any_type, any_type_i))
                        ch(vec.tensor_tensor(any_score, any_trip[:, :, 0], any_trip[:, :, 1], ALU.add))
                        ch(vec.scalar_tensor_tensor(out=any_score, in0=any_score, scalar=0.2, in1=any_score,
                                                    op0=ALU.mult, op1=ALU.max))
                        ch(vec.memset(any_alpha, 0.0))
                        wide = lambda row: bc(row.unsqueeze(1), 128, R, HE)
                        with dve.Fori(0, cnt) as i:
                            w = dve.snap(within(first + i, NW - 1))
                            node = lambda table: table[:, bass.ds(w, 1), :]
                            column = lambda table: bc(node(table).rearrange("p a r -> p (a r)").unsqueeze(2), 128, R, HE)
                            ch2 = Chain(dve, s_vch)
                            ch2.start()
                            ch2(vec.tensor_scalar(any_off, any_dst, node_col[:, bass.ds(w, 1)], None, ALU.not_equal))
                            ch2(vec.tensor_tensor(any_mask, wide(any_type), bc(rel_col[:, :].unsqueeze(2), 128, R, HE),
                                                  ALU.not_equal))
                            ch2(vec.tensor_tensor(any_mask, any_mask, wide(any_off), ALU.max))
                            ch2(vec.tensor_scalar(any_mask, any_mask, -BIG, None, ALU.mult))
                            if k == 0:
                                for row, table in ((any_score, any_max), (any_trip[:, :, 2], any_self)):
                                    ch2(vec.tensor_tensor(any_val, any_mask, wide(row), ALU.add))
                                    ch2(vec.tensor_reduce(out=any_col[:, 0, :], in_=any_val, op=ALU.max, axis=AX.X))
                                    ch2(vec.tensor_tensor(node(table), node(table), any_col, ALU.max))
                            else:
                                ch2(vec.tensor_tensor(any_val, any_mask, wide(any_score), ALU.add))
                                ch2(vec.tensor_tensor(any_val, any_val, column(any_max), ALU.subtract))
                                dve.sem_inc(s_any_gap[k - 1], 1)
                                wait_reg(dve, s_any_exp[k - 1], cum * 2 + cnt * h + i + 1)
                            if k == 1:
                                ch2(vec.tensor_reduce(out=any_col[:, 0, :], in_=any_val, op=ALU.add, axis=AX.X))
                                ch2(vec.tensor_tensor(node(any_den), node(any_den), any_col, ALU.add))
                            if k == 2:
                                ch2(vec.tensor_tensor(any_val, any_val, column(any_den), ALU.mult))
                                ch2(vec.tensor_reduce(out=any_off, in_=any_val.rearrange("p r e -> p e r"),
                                                      op=ALU.add, axis=AX.X))
                                ch2(vec.tensor_tensor(any_alpha, any_alpha, any_off, ALU.add))
                        if k == 2:
                            ch.start()
                            dve.sem_inc(s_any_acc, 1)
                            wait_reg(dve, s_any_sum, g * 2 + (h + 1))
                            ch(vec.tensor_copy(any_row, p_a[0:1, 0, 0:HE]))
                        dve.sem_inc(s_any_used, 1)

            with dve.If(out_of_order(dve)):
                ch.start()
                ch(vec.memset(dtab[:, :, :], NO_EDGE))
                any_order(0)
                ch.start()
                ch(vec.tensor_tensor(any_max, any_max, any_self, ALU.max))
                ch(vec.tensor_tensor(any_self, any_self, any_max, ALU.subtract))
                dve.sem_inc(s_ein, 1)
                dve.wait_ge(s_eout, 3)
                any_order(1)
                ch.start()
                ch(vec.reciprocal(any_den, any_den))
                any_order(2)
            ch.start()
            dve.wait_ge(s_alphal, 16)

            piped_pass(HROW)

            def scale_self(it, u, b, behind=None):
                ch.start()
                wait_reg(dve, s_mid[5], b + 1)
                own, nb = bank(p_a, u, D), bank(p_b, u, HROW)
                ch.add(vec.tensor_scalar(self_w[:, :, :], nb[:, :, D:HROW], -1.0, 1.0, ALU.mult, ALU.add))
                wait_reg(dve, s_xs[u], it * 16 + 16 * (1 + NI * 5))
                ch(vec.tensor_tensor(self_y[u], xs[:, u, :, :], own, ALU.add))
                ch(vec.tensor_tensor(self_y[u], self_y[u], nb[:, :, 0:D], ALU.add))
                dve.sem_inc(s_xfree[5], 1)
                for t in range(BT):
                    k, m = (BT * u + t) % 2, (BT * u + t) // 2
                    wait_reg(dve, s_h[1][k], it * BT + (m + 1))
                    vec.tensor_tensor(self_h[u][:, t, :, :], p_sum[:, k, :].rearrange("p (r d) -> p r d", r=R),
                                      bc(self_w[:, t, :].unsqueeze(2), 128, R, D), ALU.mult)\
                        .then_inc(s_hc[1][k], 1)
                    if behind is not None:
                        finish5(t, 1 - u, behind)
                for k in range(2):
                    m = (BT * u + BT - 1 - (BT * u + BT - 1 + k) % 2) // 2
                    wait_reg(dve, s_hc[1][k], it * BT + (m + 2))
                dve.sem_inc(s_self, 1)

            def finish5(step, u, b):
                rows5 = lambda r: bc(r[:, :].unsqueeze(2), 128, BT, D)
                if step == 0:
                    wait_reg(dve, s_selfsum, b + 1)
                    ch(vec.tensor_tensor(ya[:, :, :], self_y[u], self_h[u][:, :, 0, :], ALU.add))
                elif step == 1:
                    ch(vec.tensor_reduce(out=r2[:, :], in_=ya[:, :, :], op=ALU.add, axis=AX.X))
                elif step == 2:
                    ch(vec.scalar_tensor_tensor(out=ya[:, :, :], in0=rows5(r2), scalar=-1.0 / D, in1=ya[:, :, :],
                                                op0=ALU.mult, op1=ALU.add))
                elif step == 3:
                    ch(vec.tensor_tensor(yb[:, :, :], ya[:, :, :], ya[:, :, :], ALU.mult))
                elif step == 4:
                    ch(vec.tensor_reduce(out=r2[:, :], in_=yb[:, :, :], op=ALU.add, axis=AX.X))
                    dve.sem_inc(s_sqrt_in[5], 1)
                elif step == BT - 1:
                    wait_reg(dve, s_sqrt[5], b + 1)
                    ch(vec.reciprocal(r2[:, :], r2[:, :]))
                    wait_reg(dve, s_yfree[5], b + 1)
                    vec.tensor_tensor(yo[:, u, :, :], ya[:, :, :], rows5(r2), ALU.mult).then_inc(s_y[5], 1)
                    wait_reg(dve, s_y[5], b + 1)

            scale_self(0, 0, 0)
            with dve.Fori(0, NI - 1) as it:
                b = dve.snap(it * 2)
                scale_self(it, 1, dve.snap(b + 1), b)
                scale_self(dve.snap(it + 1), 0, dve.snap(b + 2), dve.snap(b + 1))
            scale_self(NI - 1, 1, NB - 1, NB - 2)
            for step in range(BT):
                finish5(step, 1, NB - 1)


def kernel(**inputs):
    import numpy as np
    import concourse.bacc as bacc
    from concourse.bass_utils import run_bass_kernel_spmd

    nc = bacc.Bacc("TRN2", target_bir_lowering=False, num_devices=1)
    arrays = {}

    def given(name, a):
        a = np.ascontiguousarray(a)
        arrays[f"in_{name}"] = a
        return nc.dram_tensor(f"in_{name}", a.shape, mybir.dt.from_np(a.dtype), kind="ExternalInput").ap()

    i = {k: np.asarray(v) for k, v in inputs.items()}
    grouped = lambda a: a.reshape(G, P, S).transpose(1, 0, 2)
    w2 = i["L2_gnn_W"].T
    laid = {
        "ws65": np.concatenate([i["L0_gnn_W_self"].T, i["L0_gnn_bias"][None]]), "wn": i["L0_gnn_W_neigh"].T,
        "w1": i["L1_gnn_W1"], "b1": i["L1_gnn_b1"][:, None],
        "w2b": np.concatenate([i["L1_gnn_W2"], i["L1_gnn_b2"][None]]),
        "wi": w2[:D], "wj": w2[D:], "b2": i["L2_gnn_b"][None],
        "gamma": i["L2_gnn_gamma"][:, None], "beta": i["L2_gnn_beta"][:, None],
        "wself": i["L3_gnn_W_self"], "bself": i["L3_gnn_b_self"][None],
        "wcat": i["L3_gnn_W"].transpose(1, 0, 2).reshape(D, R * D),
        "wrt": i["L3_gnn_W"].transpose(2, 0, 1).reshape(D, R * D),
        "att": np.stack([i["L3_gnn_att_src"], i["L3_gnn_att_dst"]], -1).transpose(1, 0, 2).reshape(D, 2 * R),
        "rbias": i["L3_gnn_bias"].reshape(1, R * D),
    }
    args = [given("x", i["x"]), given("src_p", grouped(i["src"])), given("dst_p", grouped(i["dst"])),
            given("type_p", grouped(i["edge_type_8"])), given("weight_p", grouped(i["edge_weight"])),
            given("dst_f", i["dst"]), given("type_f", i["edge_type_8"]), given("edge_attr", i["edge_attr_64"]),
            {name: given(name, laid[name]) for name, _ in WEIGHTS}]
    out = nc.dram_tensor("out", (N, D), mybir.dt.float32, kind="ExternalOutput").ap()
    program(nc, *args, out)
    return run_bass_kernel_spmd(nc, [arrays], core_ids=[0]).results[0]["out"]
```
